# Optimizing a Trainium2 kernel written in Bass

```python
import numpy as np
import jax
import jax.numpy as jnp

def _softmax(x, axis=-1):
    return jax.nn.softmax(x, axis=axis)

def _gelu(x):
    return jax.nn.gelu(x, approximate=True)

def _silu(x):
    return jax.nn.silu(x)

def _sigmoid(x):
    return jax.nn.sigmoid(x)

def _layernorm(x, axis=-1, eps=1e-05):
    m = jnp.mean(x, axis=axis, keepdims=True)
    v = jnp.var(x, axis=axis, keepdims=True)
    return (x - m) / jnp.sqrt(v + eps)

def _scatter_add(tgt, idx, src, axis=0):
    return tgt.at[idx].add(src)

def _segment_sum(src, seg, n):
    return jax.ops.segment_sum(src, seg, n)
kernel_name = 'mk_flamingo_gated_d4_seqx_r8_e28421'

def setup_inputs(seed: int=0):
    np.random.seed(seed)
    _w = jnp.asarray

    def _rec_inputs():
        import jax
        import jax.numpy as jnp
        _rk = jax.random.key(seed)
        x = -0.0003929 + 0.9999 * jax.random.normal(jax.random.fold_in(_rk, 1), (8, 128, 256), jnp.float32)
        _lenS = 128 - jax.random.randint(jax.random.fold_in(_rk, 7), (8,), 0, max(1, 128 // 4) + 1, jnp.int32)
        _lenS2 = 128 - jax.random.randint(jax.random.fold_in(_rk, 8), (8,), 0, max(1, 128 // 4) + 1, jnp.int32)
        _ctx_2048P = jax.random.normal(jax.random.fold_in(_rk, 11), (8, 16, 256), jnp.float32)
        _ctx_2048c = jax.random.dirichlet(jax.random.fold_in(_rk, 511), 0.3 * jnp.ones((16,), jnp.float32), (8, 128))
        _ctx_2048t = jnp.einsum('bsk,bkd->bsd', _ctx_2048c, _ctx_2048P)
        _ctx_2048t = _ctx_2048t * jax.lax.rsqrt(jnp.mean(jnp.square(_ctx_2048t)) + 1e-12) * 0.953939
        ctx_2048 = -0.000514642 + 1.00011 * (_ctx_2048t + 0.3 * jax.random.normal(jax.random.fold_in(_rk, 611), (8, 128, 256), jnp.float32))
        _validS = jnp.arange(128)[None, :] < _lenS[:, None]
        _validS2 = jnp.arange(128)[None, :] < _lenS2[:, None]
        _causal = jnp.tril(jnp.ones((128, 128), dtype=bool))
        mask_BxS2_bk0 = jnp.logical_not(jnp.broadcast_to(_validS2[:, :], (8, 128)))
        _g = jax.random.normal(jax.random.fold_in(_rk, 9001), (2, 4), jnp.float32)
        _g = jnp.sign(_g) * jnp.maximum(jnp.abs(_g), 1.0) + (_g == 0) * 1.0
        g_xattn = _g[0]
        g_ffn = _g[1]
        return (x, ctx_2048, mask_BxS2_bk0, g_xattn, g_ffn)
    x, ctx_2048, mask_BxS2_bk0, g_xattn, g_ffn = _rec_inputs()

    def _L0_xattn_setup():
        import jax, jax.numpy as jnp
        import numpy as np
        DIM = 256
        NHEADS = 32
        HEAD_DIM = DIM // NHEADS
        EPS = 1e-06

        def _rmsnorm(t):
            return t * jax.lax.rsqrt(jnp.mean(t * t, axis=-1, keepdims=True) + EPS)
        key = jax.random.key(seed)
        kx, kc, kq, kk, kv = jax.random.split(key, 5)
        x = jax.random.normal(kx, (2, 512, DIM), dtype=jnp.float32)
        context = jax.random.normal(kc, (2, 64, DIM), dtype=jnp.float32)
        std = 0.02
        Wq = jax.random.normal(kq, (DIM, DIM), dtype=jnp.float32) * std
        Wk = jax.random.normal(kk, (DIM, DIM), dtype=jnp.float32) * std
        Wv = jax.random.normal(kv, (DIM, DIM), dtype=jnp.float32) * std
        return {'x': x, 'context': context, 'Wq': Wq, 'Wk': Wk, 'Wv': Wv}
    _L0_xattn_all = _L0_xattn_setup()
    _L0_xattn_in = {k: v for k, v in _L0_xattn_all.items() if k in ('Wq', 'Wk', 'Wv')}
    del _L0_xattn_all

    def _L0_ffn_setup():
        import jax, jax.numpy as jnp
        import numpy as np
        EPS = 1e-05

        def fwht(x):
            orig_shape = x.shape
            n = orig_shape[-1]
            x = x.reshape(-1, n)
            h = 1
            while h < n:
                x = x.reshape(-1, n // (2 * h), 2, h)
                a, b = (x[:, :, 0, :], x[:, :, 1, :])
                x = jnp.stack([a + b, a - b], axis=2).reshape(-1, n)
                h *= 2
            return (x * (1.0 / np.sqrt(n))).reshape(orig_shape)

        def act_quant(x):
            scale = 127.0 / jnp.clip(jnp.max(jnp.abs(x), axis=-1, keepdims=True), EPS)
            q = jnp.clip(jnp.round(x * scale), -128.0, 127.0) / scale
            return x + jax.lax.stop_gradient(q - x)

        def weight_quant(w):
            scale = jnp.clip(jnp.mean(jnp.abs(w)), EPS)
            q = jnp.clip(jnp.round(w / scale), -1.0, 1.0) * scale
            return w + jax.lax.stop_gradient(q - w)

        def h_bitlinear(x, w):
            xq = act_quant(fwht(x))
            wq = weight_quant(w)
            return jnp.einsum('bsh,oh->bso', xq, wq)
        key = jax.random.key(seed)
        k1, k2, k3, k4 = jax.random.split(key, 4)
        H, I = (256, 1024)
        B, S = (2, 256)
        hidden_states = jax.random.normal(k1, (B, S, H), dtype=jnp.float32)
        w_gate = jax.random.normal(k2, (I, H), dtype=jnp.float32) * 0.02
        w_up = jax.random.normal(k3, (I, H), dtype=jnp.float32) * 0.02
        w_down = jax.random.normal(k4, (H, I), dtype=jnp.float32) * 0.02
        return {'hidden_states': hidden_states, 'w_gate': w_gate, 'w_up': w_up, 'w_down': w_down}
    _L0_ffn_all = _L0_ffn_setup()
    _L0_ffn_in = {k: v for k, v in _L0_ffn_all.items() if k in ('w_gate', 'w_up', 'w_down')}
    del _L0_ffn_all

    def _L1_xattn_setup():
        import jax, jax.numpy as jnp
        import numpy as np
        FP8_MAX = 448.0
        EPS = 1e-05

        def _fp8_roundtrip(x):
            return x.astype(jnp.float8_e4m3fn).astype(jnp.float32)

        def _div_clamp_fp8(x, scale):
            y = jnp.clip(x.astype(jnp.float32) / scale, -FP8_MAX, FP8_MAX)
            y = y.astype(jnp.bfloat16).astype(jnp.float32)
            return _fp8_roundtrip(y)

        def _ln(x, w, b):
            mu = jnp.mean(x, axis=-1, keepdims=True)
            var = jnp.mean(jnp.square(x - mu), axis=-1, keepdims=True)
            return (x - mu) * jax.lax.rsqrt(var + EPS) * w + b

        def _fp8_linear_pertensor(x, wq, w_scale, in_scale):
            xq = _div_clamp_fp8(x, in_scale)
            return jnp.einsum('bsi,oi->bso', xq * in_scale, wq) * w_scale

        def _gqa(q, k, v):
            scale = 1.0 / np.sqrt(q.shape[-1])
            scores = jnp.einsum('bsghd,btgd->bghst', q, k) * scale
            p = jax.nn.softmax(scores, axis=-1)
            return jnp.einsum('bghst,btgd->bsghd', p, v)
        key = jax.random.key(seed)
        ks = jax.random.split(key, 8)
        B, S, SC, H, NH, G, D = (2, 256, 64, 256, 16, 8, 128)

        def qw(k, out_f, in_f):
            w = jax.random.normal(k, (out_f, in_f), jnp.float32) * 0.02
            sc = jnp.max(jnp.abs(w)) / FP8_MAX
            return (_fp8_roundtrip(w / sc), sc.astype(jnp.float32))
        wq, wq_s = qw(ks[0], NH * D, H)
        wqx, wqx_s = qw(ks[1], NH * D, H)
        wk, wk_s = qw(ks[2], G * D, H)
        wv, wv_s = qw(ks[3], G * D, H)
        wproj, wp_s = qw(ks[4], H, 2 * NH * D)
        return {'hidden_states': jax.random.normal(ks[5], (B, S, H), jnp.float32), 'cond': jax.random.normal(ks[6], (B, SC, H), jnp.float32), 'ln_w': jnp.ones((H,), jnp.float32), 'ln_b': jnp.zeros((H,), jnp.float32), 'wq': wq, 'wq_scale': wq_s, 'q_in_scale': jnp.full((H,), 0.05, jnp.float32), 'wqx': wqx, 'wqx_scale': wqx_s, 'qx_in_scale': jnp.full((H,), 0.05, jnp.float32), 'wk': wk, 'wk_scale': wk_s, 'k_in_scale': jnp.full((H,), 0.05, jnp.float32), 'wv': wv, 'wv_scale': wv_s, 'v_in_scale': jnp.full((H,), 0.05, jnp.float32), 'w_kv_x': jax.random.normal(ks[7], (2 * G * D, H), jnp.float32) * 0.02, 'qln_w': jnp.ones((D,), jnp.float32), 'qln_b': jnp.zeros((D,), jnp.float32), 'kln_w': jnp.ones((D,), jnp.float32), 'kln_b': jnp.zeros((D,), jnp.float32), 'qxln_w': jnp.ones((D,), jnp.float32), 'qxln_b': jnp.zeros((D,), jnp.float32), 'kxln_w': jnp.ones((D,), jnp.float32), 'kxln_b': jnp.zeros((D,), jnp.float32), 'wproj': wproj, 'proj_w_scale': wp_s, 'proj_in_scale': jnp.asarray(0.05, jnp.float32), 'proj_smooth': jnp.full((2 * NH * D,), 0.05, jnp.float32)}
    _L1_xattn_all = _L1_xattn_setup()
    _L1_xattn_in = {k: v for k, v in _L1_xattn_all.items() if k in ('ln_w', 'ln_b', 'wq', 'wq_scale', 'q_in_scale', 'wqx', 'wqx_scale', 'qx_in_scale', 'wk', 'wk_scale', 'k_in_scale', 'wv', 'wv_scale', 'v_in_scale', 'w_kv_x', 'qln_w', 'qln_b', 'kln_w', 'kln_b', 'qxln_w', 'qxln_b', 'kxln_w', 'kxln_b', 'wproj', 'proj_w_scale', 'proj_in_scale', 'proj_smooth')}
    del _L1_xattn_all

    def _L1_ffn_setup():
        import jax, jax.numpy as jnp
        import numpy as np
        B_, S, D = (2, 256, 256)
        F_ = 1024
        R = 16
        H = 16
        HD = D // H
        MOD_SCALE = 0.1
        EPS = 1e-06

        def _rmsnorm(x, w):
            v = jnp.mean(x * x, axis=-1, keepdims=True)
            return x * jax.lax.rsqrt(v + EPS) * w

        def _attention(x, Wq, Wk, Wv, Wo):
            b, s, d = x.shape
            q = (x @ Wq.T).reshape(b, s, H, HD)
            k = (x @ Wk.T).reshape(b, s, H, HD)
            v = (x @ Wv.T).reshape(b, s, H, HD)
            scores = jnp.einsum('bqhd,bkhd->bhqk', q, k) / np.sqrt(HD).astype(np.float32)
            causal = jnp.tril(jnp.ones((s, s), bool))
            scores = jnp.where(causal, scores, jnp.finfo(scores.dtype).min)
            probs = jax.nn.softmax(scores, axis=-1)
            out = jnp.einsum('bhqk,bkhd->bqhd', probs, v).reshape(b, s, d)
            return out @ Wo.T
        key = jax.random.key(seed)
        ks = jax.random.split(key, 12)
        sd = 0.02
        return {'hidden_states': jax.random.normal(ks[0], (B_, S, D), jnp.float32), 'ln1_w': jnp.ones((D,), jnp.float32), 'ln2_w': jnp.ones((D,), jnp.float32), 'Wq': jax.random.normal(ks[1], (D, D), jnp.float32) * sd, 'Wk': jax.random.normal(ks[2], (D, D), jnp.float32) * sd, 'Wv': jax.random.normal(ks[3], (D, D), jnp.float32) * sd, 'Wo': jax.random.normal(ks[4], (D, D), jnp.float32) * sd, 'A': jax.random.normal(ks[5], (D, R), jnp.float32) * (0.01 / np.sqrt(D)), 'B': jax.random.normal(ks[6], (R, F_), jnp.float32) * (0.01 / np.sqrt(R)), 'W_in_base': jax.random.normal(ks[7], (F_, D), jnp.float32) * sd, 'W_up_base': jax.random.normal(ks[8], (F_, D), jnp.float32) * sd, 'W_down': jax.random.normal(ks[9], (D, F_), jnp.float32) * sd}
    _L1_ffn_all = _L1_ffn_setup()
    _L1_ffn_in = {k: v for k, v in _L1_ffn_all.items() if k in ('ln1_w', 'ln2_w', 'Wq', 'Wk', 'Wv', 'Wo', 'A', 'B', 'W_in_base', 'W_up_base', 'W_down')}
    del _L1_ffn_all

    def _L2_xattn_setup():
        import jax, jax.numpy as jnp
        import numpy as np
        D_MODEL = 256
        NUM_HEADS = 16
        HEAD_DIM = D_MODEL // NUM_HEADS

        def _fq_sym(x, axis):
            s = jnp.max(jnp.abs(x), axis=axis, keepdims=True) / 127.0
            s = jnp.maximum(s, 1e-08)
            q = jnp.clip(jnp.round(x / s), -127.0, 127.0) * s
            return x + jax.lax.stop_gradient(q - x)

        def _fq_unsigned(x, axis):
            s = jnp.max(x, axis=axis, keepdims=True) / 255.0
            s = jnp.maximum(s, 1e-08)
            q = jnp.clip(jnp.round(x / s), 0.0, 255.0) * s
            return x + jax.lax.stop_gradient(q - x)
        key = jax.random.key(seed)
        ks = jax.random.split(key, 8)
        B, N, M, C = (2, 256, 64, D_MODEL)
        return {'x': jax.random.normal(ks[0], (B, N, C), jnp.float32), 'cond': jax.random.normal(ks[1], (B, M, C), jnp.float32), 'Wq': jax.random.normal(ks[2], (C, C), jnp.float32) * 0.02, 'bq': jnp.zeros((C,), jnp.float32), 'Wkv': jax.random.normal(ks[3], (C, 2 * C), jnp.float32) * 0.02, 'bkv': jnp.zeros((2 * C,), jnp.float32), 'Wp': jax.random.normal(ks[4], (C, C), jnp.float32) * 0.02, 'bp': jnp.zeros((C,), jnp.float32)}
    _L2_xattn_all = _L2_xattn_setup()
    _L2_xattn_in = {k: v for k, v in _L2_xattn_all.items() if k in ('Wq', 'bq', 'Wkv', 'bkv', 'Wp', 'bp')}
    del _L2_xattn_all

    def _L2_ffn_setup():
        import jax, jax.numpy as jnp
        import numpy as np
        K = 2

        def gelu(v):
            return jax.nn.gelu(v, approximate=False)
        key = jax.random.key(seed)
        ks = jax.random.split(key, 10)
        B, S, D, H, E = (4, 256, 256, 128, 8)
        SH = 2 * H
        u = lambda k_, shape, b: jax.random.uniform(k_, shape, jnp.float32, -b, b)
        return {'x': jax.random.normal(ks[0], (B, S, D), jnp.float32), 'gate_w': u(ks[1], (D, E), 1.0 / D), 'w1': u(ks[2], (E, D, H), 1.0 / D), 'b1': u(ks[3], (E, H), 1.0 / np.sqrt(D)), 'w2': u(ks[4], (E, H, D), 1.0 / H), 'b2': u(ks[5], (E, D), 1.0 / np.sqrt(H)), 'shared_w1': u(ks[6], (D, SH), 1.0 / D), 'shared_b1': u(ks[7], (SH,), 1.0 / np.sqrt(D)), 'shared_w2': u(ks[8], (SH, D), 1.0 / SH), 'shared_b2': u(ks[9], (D,), 1.0 / np.sqrt(SH))}
    _L2_ffn_all = _L2_ffn_setup()
    _L2_ffn_in = {k: v for k, v in _L2_ffn_all.items() if k in ('gate_w', 'w1', 'b1', 'w2', 'b2', 'shared_w1', 'shared_b1', 'shared_w2', 'shared_b2')}
    del _L2_ffn_all

    def _L3_xattn_setup():
        import jax, jax.numpy as jnp
        import numpy as np
        key = jax.random.key(seed)
        k1, k2, k3 = jax.random.split(key, 3)
        B, S, D, M = (8, 256, 256, 128)
        hidden_states = jax.random.normal(k1, (B, S, D), dtype=jnp.float32)
        memory_tokens = jax.random.normal(k2, (B, M, D), dtype=jnp.float32)
        memory_mask = jax.random.randint(k3, (B, M), 0, 2).astype(jnp.bool_)
        return {'hidden_states': hidden_states, 'memory_tokens': memory_tokens, 'memory_mask': memory_mask}
    _L3_xattn_all = _L3_xattn_setup()
    _L3_xattn_in = {k: v for k, v in _L3_xattn_all.items() if k in ()}
    del _L3_xattn_all

    def _L3_ffn_setup():
        import jax, jax.numpy as jnp
        import numpy as np
        HIDDEN = 256
        INTER = 1024
        SCALE = 64.0

        def fwht(x):
            orig_shape = x.shape
            n = orig_shape[-1]
            x = x.reshape(-1, n)
            h = 1
            while h < n:
                x = x.reshape(-1, n // (2 * h), 2, h)
                a, b = (x[:, :, 0, :], x[:, :, 1, :])
                x = jnp.stack([a + b, a - b], axis=2).reshape(-1, n)
                h *= 2
            return (x / jnp.sqrt(jnp.asarray(n, x.dtype))).reshape(orig_shape)
        key = jax.random.key(seed)
        ks = jax.random.split(key, 8)
        inp = jax.random.normal(ks[0], (4, 256, HIDDEN), dtype=jnp.float32)
        SU_ug = jnp.where(jax.random.bernoulli(ks[1], 0.5, (HIDDEN,)), 1.0, -1.0).astype(jnp.float32)
        SU_dp = jnp.where(jax.random.bernoulli(ks[2], 0.5, (INTER,)), 1.0, -1.0).astype(jnp.float32)
        Wscale_ug = jax.random.uniform(ks[3], (2 * INTER,), jnp.float32, 0.5, 1.5)
        Wscale_dp = jax.random.uniform(ks[4], (HIDDEN,), jnp.float32, 0.5, 1.5)
        W_up = jax.random.normal(ks[5], (INTER, HIDDEN), dtype=jnp.float32) * 0.02
        W_gate = jax.random.normal(ks[6], (INTER, HIDDEN), dtype=jnp.float32) * 0.02
        W_down = jax.random.normal(ks[7], (HIDDEN, INTER), dtype=jnp.float32) * 0.02
        return {'input': inp, 'SU_ug': SU_ug, 'SU_dp': SU_dp, 'Wscale_ug': Wscale_ug, 'Wscale_dp': Wscale_dp, 'W_up': W_up, 'W_gate': W_gate, 'W_down': W_down}
    _L3_ffn_all = _L3_ffn_setup()
    _L3_ffn_in = {k: v for k, v in _L3_ffn_all.items() if k in ('SU_ug', 'SU_dp', 'Wscale_ug', 'Wscale_dp', 'W_up', 'W_gate', 'W_down')}
    del _L3_ffn_all
    return {'x': x, 'ctx_2048': ctx_2048, 'mask_BxS2_bk0': mask_BxS2_bk0, 'g_xattn': g_xattn, 'g_ffn': g_ffn, 'L0_xattn_Wq': _L0_xattn_in['Wq'], 'L0_xattn_Wk': _L0_xattn_in['Wk'], 'L0_xattn_Wv': _L0_xattn_in['Wv'], 'L0_ffn_w_gate': _L0_ffn_in['w_gate'], 'L0_ffn_w_up': _L0_ffn_in['w_up'], 'L0_ffn_w_down': _L0_ffn_in['w_down'], 'L1_xattn_ln_w': _L1_xattn_in['ln_w'], 'L1_xattn_ln_b': _L1_xattn_in['ln_b'], 'L1_xattn_wq': _L1_xattn_in['wq'], 'L1_xattn_wq_scale': _L1_xattn_in['wq_scale'], 'L1_xattn_q_in_scale': _L1_xattn_in['q_in_scale'], 'L1_xattn_wqx': _L1_xattn_in['wqx'], 'L1_xattn_wqx_scale': _L1_xattn_in['wqx_scale'], 'L1_xattn_qx_in_scale': _L1_xattn_in['qx_in_scale'], 'L1_xattn_wk': _L1_xattn_in['wk'], 'L1_xattn_wk_scale': _L1_xattn_in['wk_scale'], 'L1_xattn_k_in_scale': _L1_xattn_in['k_in_scale'], 'L1_xattn_wv': _L1_xattn_in['wv'], 'L1_xattn_wv_scale': _L1_xattn_in['wv_scale'], 'L1_xattn_v_in_scale': _L1_xattn_in['v_in_scale'], 'L1_xattn_w_kv_x': _L1_xattn_in['w_kv_x'], 'L1_xattn_qln_w': _L1_xattn_in['qln_w'], 'L1_xattn_qln_b': _L1_xattn_in['qln_b'], 'L1_xattn_kln_w': _L1_xattn_in['kln_w'], 'L1_xattn_kln_b': _L1_xattn_in['kln_b'], 'L1_xattn_qxln_w': _L1_xattn_in['qxln_w'], 'L1_xattn_qxln_b': _L1_xattn_in['qxln_b'], 'L1_xattn_kxln_w': _L1_xattn_in['kxln_w'], 'L1_xattn_kxln_b': _L1_xattn_in['kxln_b'], 'L1_xattn_wproj': _L1_xattn_in['wproj'], 'L1_xattn_proj_w_scale': _L1_xattn_in['proj_w_scale'], 'L1_xattn_proj_in_scale': _L1_xattn_in['proj_in_scale'], 'L1_xattn_proj_smooth': _L1_xattn_in['proj_smooth'], 'L1_ffn_ln1_w': _L1_ffn_in['ln1_w'], 'L1_ffn_ln2_w': _L1_ffn_in['ln2_w'], 'L1_ffn_Wq': _L1_ffn_in['Wq'], 'L1_ffn_Wk': _L1_ffn_in['Wk'], 'L1_ffn_Wv': _L1_ffn_in['Wv'], 'L1_ffn_Wo': _L1_ffn_in['Wo'], 'L1_ffn_A': _L1_ffn_in['A'], 'L1_ffn_B': _L1_ffn_in['B'], 'L1_ffn_W_in_base': _L1_ffn_in['W_in_base'], 'L1_ffn_W_up_base': _L1_ffn_in['W_up_base'], 'L1_ffn_W_down': _L1_ffn_in['W_down'], 'L2_xattn_Wq': _L2_xattn_in['Wq'], 'L2_xattn_bq': _L2_xattn_in['bq'], 'L2_xattn_Wkv': _L2_xattn_in['Wkv'], 'L2_xattn_bkv': _L2_xattn_in['bkv'], 'L2_xattn_Wp': _L2_xattn_in['Wp'], 'L2_xattn_bp': _L2_xattn_in['bp'], 'L2_ffn_gate_w': _L2_ffn_in['gate_w'], 'L2_ffn_w1': _L2_ffn_in['w1'], 'L2_ffn_b1': _L2_ffn_in['b1'], 'L2_ffn_w2': _L2_ffn_in['w2'], 'L2_ffn_b2': _L2_ffn_in['b2'], 'L2_ffn_shared_w1': _L2_ffn_in['shared_w1'], 'L2_ffn_shared_b1': _L2_ffn_in['shared_b1'], 'L2_ffn_shared_w2': _L2_ffn_in['shared_w2'], 'L2_ffn_shared_b2': _L2_ffn_in['shared_b2'], 'L3_ffn_SU_ug': _L3_ffn_in['SU_ug'], 'L3_ffn_SU_dp': _L3_ffn_in['SU_dp'], 'L3_ffn_Wscale_ug': _L3_ffn_in['Wscale_ug'], 'L3_ffn_Wscale_dp': _L3_ffn_in['Wscale_dp'], 'L3_ffn_W_up': _L3_ffn_in['W_up'], 'L3_ffn_W_gate': _L3_ffn_in['W_gate'], 'L3_ffn_W_down': _L3_ffn_in['W_down']}

def reference(x, ctx_2048, mask_BxS2_bk0, g_xattn, g_ffn, L0_xattn_Wq, L0_xattn_Wk, L0_xattn_Wv, L0_ffn_w_gate, L0_ffn_w_up, L0_ffn_w_down, L1_xattn_ln_w, L1_xattn_ln_b, L1_xattn_wq, L1_xattn_wq_scale, L1_xattn_q_in_scale, L1_xattn_wqx, L1_xattn_wqx_scale, L1_xattn_qx_in_scale, L1_xattn_wk, L1_xattn_wk_scale, L1_xattn_k_in_scale, L1_xattn_wv, L1_xattn_wv_scale, L1_xattn_v_in_scale, L1_xattn_w_kv_x, L1_xattn_qln_w, L1_xattn_qln_b, L1_xattn_kln_w, L1_xattn_kln_b, L1_xattn_qxln_w, L1_xattn_qxln_b, L1_xattn_kxln_w, L1_xattn_kxln_b, L1_xattn_wproj, L1_xattn_proj_w_scale, L1_xattn_proj_in_scale, L1_xattn_proj_smooth, L1_ffn_ln1_w, L1_ffn_ln2_w, L1_ffn_Wq, L1_ffn_Wk, L1_ffn_Wv, L1_ffn_Wo, L1_ffn_A, L1_ffn_B, L1_ffn_W_in_base, L1_ffn_W_up_base, L1_ffn_W_down, L2_xattn_Wq, L2_xattn_bq, L2_xattn_Wkv, L2_xattn_bkv, L2_xattn_Wp, L2_xattn_bp, L2_ffn_gate_w, L2_ffn_w1, L2_ffn_b1, L2_ffn_w2, L2_ffn_b2, L2_ffn_shared_w1, L2_ffn_shared_b1, L2_ffn_shared_w2, L2_ffn_shared_b2, L3_ffn_SU_ug, L3_ffn_SU_dp, L3_ffn_Wscale_ug, L3_ffn_Wscale_dp, L3_ffn_W_up, L3_ffn_W_gate, L3_ffn_W_down):
    import jax
    import jax.numpy as jnp

    def _L0_xattn_ref(x, context, Wq, Wk, Wv):
        import jax, jax.numpy as jnp
        import numpy as np
        DIM = 256
        NHEADS = 32
        HEAD_DIM = DIM // NHEADS
        EPS = 1e-06

        def _rmsnorm(t):
            return t * jax.lax.rsqrt(jnp.mean(t * t, axis=-1, keepdims=True) + EPS)
        b, n, _ = x.shape
        m = context.shape[1]
        q = x @ Wq.T
        k_raw = context @ Wk.T
        v_raw = context @ Wv.T
        q = q.reshape(b, n, NHEADS, HEAD_DIM).transpose(0, 2, 1, 3)
        kv = jnp.concatenate([k_raw, v_raw], axis=-1)
        kv = kv.reshape(b, m, NHEADS, HEAD_DIM, 2)
        k = kv[..., 0].transpose(0, 2, 1, 3)
        v = kv[..., 1].transpose(0, 2, 1, 3)
        q = _rmsnorm(q)
        k = _rmsnorm(k)
        scale = HEAD_DIM ** (-0.5)
        scores = jnp.einsum('bhnd,bhmd->bhnm', q, k) * scale
        attn = jax.nn.softmax(scores, axis=-1)
        out = jnp.einsum('bhnm,bhmd->bhnd', attn, v)
        return out.transpose(0, 2, 1, 3).reshape(b, n, NHEADS * HEAD_DIM)

    def _L0_ffn_ref(hidden_states, w_gate, w_up, w_down):
        import jax, jax.numpy as jnp
        import numpy as np
        EPS = 1e-05

        def fwht(x):
            orig_shape = x.shape
            n = orig_shape[-1]
            x = x.reshape(-1, n)
            h = 1
            while h < n:
                x = x.reshape(-1, n // (2 * h), 2, h)
                a, b = (x[:, :, 0, :], x[:, :, 1, :])
                x = jnp.stack([a + b, a - b], axis=2).reshape(-1, n)
                h *= 2
            return (x * (1.0 / np.sqrt(n))).reshape(orig_shape)

        def act_quant(x):
            scale = 127.0 / jnp.clip(jnp.max(jnp.abs(x), axis=-1, keepdims=True), EPS)
            q = jnp.clip(jnp.round(x * scale), -128.0, 127.0) / scale
            return x + jax.lax.stop_gradient(q - x)

        def weight_quant(w):
            scale = jnp.clip(jnp.mean(jnp.abs(w)), EPS)
            q = jnp.clip(jnp.round(w / scale), -1.0, 1.0) * scale
            return w + jax.lax.stop_gradient(q - w)

        def h_bitlinear(x, w):
            xq = act_quant(fwht(x))
            wq = weight_quant(w)
            return jnp.einsum('bsh,oh->bso', xq, wq)
        gate = h_bitlinear(hidden_states, w_gate)
        up = h_bitlinear(hidden_states, w_up)
        return h_bitlinear(jax.nn.silu(gate) * up, w_down)

    def _L1_xattn_ref(hidden_states, cond, ln_w, ln_b, wq, wq_scale, q_in_scale, wqx, wqx_scale, qx_in_scale, wk, wk_scale, k_in_scale, wv, wv_scale, v_in_scale, w_kv_x, qln_w, qln_b, kln_w, kln_b, qxln_w, qxln_b, kxln_w, kxln_b, wproj, proj_w_scale, proj_in_scale, proj_smooth):
        import jax, jax.numpy as jnp
        import numpy as np
        FP8_MAX = 448.0
        EPS = 1e-05

        def _fp8_roundtrip(x):
            return x.astype(jnp.float8_e4m3fn).astype(jnp.float32)

        def _div_clamp_fp8(x, scale):
            y = jnp.clip(x.astype(jnp.float32) / scale, -FP8_MAX, FP8_MAX)
            y = y.astype(jnp.bfloat16).astype(jnp.float32)
            return _fp8_roundtrip(y)

        def _ln(x, w, b):
            mu = jnp.mean(x, axis=-1, keepdims=True)
            var = jnp.mean(jnp.square(x - mu), axis=-1, keepdims=True)
            return (x - mu) * jax.lax.rsqrt(var + EPS) * w + b

        def _fp8_linear_pertensor(x, wq, w_scale, in_scale):
            xq = _div_clamp_fp8(x, in_scale)
            return jnp.einsum('bsi,oi->bso', xq * in_scale, wq) * w_scale

        def _gqa(q, k, v):
            scale = 1.0 / np.sqrt(q.shape[-1])
            scores = jnp.einsum('bsghd,btgd->bghst', q, k) * scale
            p = jax.nn.softmax(scores, axis=-1)
            return jnp.einsum('bghst,btgd->bsghd', p, v)
        b, s, _ = hidden_states.shape
        sc = cond.shape[1]
        d = qln_w.shape[0]
        nh = wq.shape[0] // d
        g = wk.shape[0] // d
        hpg = nh // g
        ln_out = _ln(hidden_states, ln_w, ln_b)
        q = _fp8_linear_pertensor(ln_out, wq, wq_scale, q_in_scale).reshape(b, s, g, hpg, d)
        q = _ln(q, qln_w, qln_b)
        k = _fp8_linear_pertensor(ln_out, wk, wk_scale, k_in_scale).reshape(b, s, g, d)
        k = _ln(k, kln_w, kln_b)
        v = _fp8_linear_pertensor(ln_out, wv, wv_scale, v_in_scale).reshape(b, s, g, d)
        core = _gqa(q, k, v).reshape(b, s, nh * d)
        qx = _fp8_linear_pertensor(ln_out, wqx, wqx_scale, qx_in_scale).reshape(b, s, g, hpg, d)
        qx = _ln(qx, qxln_w, qxln_b)
        kvx = jnp.einsum('bsi,oi->bso', cond, w_kv_x)
        kx, vx = jnp.split(kvx, 2, axis=-1)
        kx = _ln(kx.reshape(b, sc, g, d), kxln_w, kxln_b)
        vx = vx.reshape(b, sc, g, d)
        xout = _gqa(qx, kx, vx).reshape(b, s, nh * d)
        cat = jnp.concatenate([core, xout], axis=-1)
        catq = _div_clamp_fp8(cat, proj_smooth)
        return jnp.einsum('bsi,oi->bso', catq, wproj) * (proj_in_scale * proj_w_scale)

    def _L1_ffn_ref(hidden_states, ln1_w, ln2_w, Wq, Wk, Wv, Wo, A, B, W_in_base, W_up_base, W_down):
        import jax, jax.numpy as jnp
        import numpy as np
        B_, S, D = (2, 256, 256)
        F_ = 1024
        R = 16
        H = 16
        HD = D // H
        MOD_SCALE = 0.1
        EPS = 1e-06

        def _rmsnorm(x, w):
            v = jnp.mean(x * x, axis=-1, keepdims=True)
            return x * jax.lax.rsqrt(v + EPS) * w

        def _attention(x, Wq, Wk, Wv, Wo):
            b, s, d = x.shape
            q = (x @ Wq.T).reshape(b, s, H, HD)
            k = (x @ Wk.T).reshape(b, s, H, HD)
            v = (x @ Wv.T).reshape(b, s, H, HD)
            scores = jnp.einsum('bqhd,bkhd->bhqk', q, k) / np.sqrt(HD).astype(np.float32)
            causal = jnp.tril(jnp.ones((s, s), bool))
            scores = jnp.where(causal, scores, jnp.finfo(scores.dtype).min)
            probs = jax.nn.softmax(scores, axis=-1)
            out = jnp.einsum('bhqk,bkhd->bqhd', probs, v).reshape(b, s, d)
            return out @ Wo.T
        residual = hidden_states
        x = _rmsnorm(hidden_states, ln1_w)
        attn = _attention(x, Wq, Wk, Wv, Wo)
        mod = MOD_SCALE * jnp.tanh(attn @ A)
        h = _rmsnorm(residual, ln2_w)
        gate_pre = h @ W_in_base.T + mod * (h @ A) @ B
        gate = jax.nn.silu(gate_pre)
        up = h @ W_up_base.T
        mlp_out = gate * up @ W_down.T
        return residual + mlp_out

    def _L2_xattn_ref(x, cond, Wq, bq, Wkv, bkv, Wp, bp):
        import jax, jax.numpy as jnp
        import numpy as np
        D_MODEL = 256
        NUM_HEADS = 16
        HEAD_DIM = D_MODEL // NUM_HEADS

        def _fq_sym(x, axis):
            s = jnp.max(jnp.abs(x), axis=axis, keepdims=True) / 127.0
            s = jnp.maximum(s, 1e-08)
            q = jnp.clip(jnp.round(x / s), -127.0, 127.0) * s
            return x + jax.lax.stop_gradient(q - x)

        def _fq_unsigned(x, axis):
            s = jnp.max(x, axis=axis, keepdims=True) / 255.0
            s = jnp.maximum(s, 1e-08)
            q = jnp.clip(jnp.round(x / s), 0.0, 255.0) * s
            return x + jax.lax.stop_gradient(q - x)
        B, N, C = x.shape
        H, hd = (NUM_HEADS, HEAD_DIM)
        q = (x @ Wq + bq).reshape(1, B * N, H, hd)
        kv = (cond @ Wkv + bkv).reshape(1, -1, 2, H, hd)
        k, v = (kv[:, :, 0], kv[:, :, 1])
        scale = 1.0 / np.sqrt(hd).astype(np.float32)
        q = jnp.transpose(q * scale, (0, 2, 1, 3))
        k = jnp.transpose(k, (0, 2, 1, 3))
        v = jnp.transpose(v, (0, 2, 1, 3))
        q = _fq_sym(q, axis=-1)
        k = _fq_sym(k, axis=-1)
        v = _fq_sym(v, axis=2)
        attn = jnp.einsum('bhqd,bhkd->bhqk', q, k)
        attn = jax.nn.softmax(attn.astype(jnp.float32), axis=-1)
        attn = _fq_unsigned(attn, axis=-1)
        out = jnp.einsum('bhqk,bhkd->bhqd', attn, v)
        out = jnp.transpose(out, (0, 2, 1, 3)).reshape(B, N, C)
        return out @ Wp + bp

    def _L2_ffn_ref(x, gate_w, w1, b1, w2, b2, shared_w1, shared_b1, shared_w2, shared_b2):
        import jax, jax.numpy as jnp
        import numpy as np
        K = 2

        def gelu(v):
            return jax.nn.gelu(v, approximate=False)
        B, S, D = x.shape
        E = gate_w.shape[1]
        xf = x.reshape(-1, D)
        logits = xf @ gate_w
        top_logits, top_idx = jax.lax.top_k(logits, K)
        top_gates = jax.nn.softmax(top_logits, axis=-1)
        gates = jnp.sum(jax.nn.one_hot(top_idx, E, dtype=xf.dtype) * top_gates[..., None], axis=1)
        h = gelu(jnp.einsum('nd,edh->neh', xf, w1) + b1)
        out_e = jnp.einsum('neh,ehd->ned', h, w2) + b2
        routed = jnp.einsum('ne,ned->nd', gates, out_e)
        shared = gelu(xf @ shared_w1 + shared_b1) @ shared_w2 + shared_b2
        return (routed + shared).reshape(B, S, D)

    def _L3_xattn_ref(hidden_states, memory_tokens, memory_mask):
        import jax, jax.numpy as jnp
        import numpy as np
        B, S, D = hidden_states.shape
        scale = 1.0 / jnp.sqrt(jnp.asarray(D, hidden_states.dtype))
        scores = jnp.einsum('bsd,bmd->bsm', hidden_states, memory_tokens) * scale
        neg_inf = jnp.asarray(-1e+30, scores.dtype)
        scores = jnp.where(memory_mask[:, None, :], scores, neg_inf)
        attn = jax.nn.softmax(scores, axis=-1)
        readout = jnp.einsum('bsm,bmd->bsd', attn, memory_tokens)
        valid_b = jnp.any(memory_mask, axis=-1)
        out = jnp.where(valid_b[:, None, None], readout, jnp.zeros_like(readout))
        return out

    def _L3_ffn_ref(input, SU_ug, SU_dp, Wscale_ug, Wscale_dp, W_up, W_gate, W_down):
        import jax, jax.numpy as jnp
        import numpy as np
        HIDDEN = 256
        INTER = 1024
        SCALE = 64.0

        def fwht(x):
            orig_shape = x.shape
            n = orig_shape[-1]
            x = x.reshape(-1, n)
            h = 1
            while h < n:
                x = x.reshape(-1, n // (2 * h), 2, h)
                a, b = (x[:, :, 0, :], x[:, :, 1, :])
                x = jnp.stack([a + b, a - b], axis=2).reshape(-1, n)
                h *= 2
            return (x / jnp.sqrt(jnp.asarray(n, x.dtype))).reshape(orig_shape)
        n = SU_ug.shape[0]
        x = input.reshape(-1, n)
        x = fwht(x * SU_ug) / SCALE
        x_up = x @ W_up.T * (Wscale_ug[:INTER] * SCALE)
        x_gate = x @ W_gate.T * (Wscale_ug[INTER:] * SCALE)
        x = jax.nn.silu(x_gate) * x_up
        x = fwht(x * SU_dp) / SCALE
        x = x @ W_down.T * (Wscale_dp * SCALE)
        return x.reshape(input.shape)
    x = x + jnp.tanh(g_xattn[0]) * _L0_xattn_ref(_layernorm(x, axis=-1), ctx_2048, L0_xattn_Wq, L0_xattn_Wk, L0_xattn_Wv)
    x = x + jnp.tanh(g_ffn[0]) * _L0_ffn_ref(_layernorm(x, axis=-1), L0_ffn_w_gate, L0_ffn_w_up, L0_ffn_w_down)
    x = x + jnp.tanh(g_xattn[1]) * _L1_xattn_ref(_layernorm(x, axis=-1), ctx_2048, L1_xattn_ln_w, L1_xattn_ln_b, L1_xattn_wq, L1_xattn_wq_scale, L1_xattn_q_in_scale, L1_xattn_wqx, L1_xattn_wqx_scale, L1_xattn_qx_in_scale, L1_xattn_wk, L1_xattn_wk_scale, L1_xattn_k_in_scale, L1_xattn_wv, L1_xattn_wv_scale, L1_xattn_v_in_scale, L1_xattn_w_kv_x, L1_xattn_qln_w, L1_xattn_qln_b, L1_xattn_kln_w, L1_xattn_kln_b, L1_xattn_qxln_w, L1_xattn_qxln_b, L1_xattn_kxln_w, L1_xattn_kxln_b, L1_xattn_wproj, L1_xattn_proj_w_scale, L1_xattn_proj_in_scale, L1_xattn_proj_smooth)
    x = x + jnp.tanh(g_ffn[1]) * _L1_ffn_ref(_layernorm(x, axis=-1), L1_ffn_ln1_w, L1_ffn_ln2_w, L1_ffn_Wq, L1_ffn_Wk, L1_ffn_Wv, L1_ffn_Wo, L1_ffn_A, L1_ffn_B, L1_ffn_W_in_base, L1_ffn_W_up_base, L1_ffn_W_down)
    x = x + jnp.tanh(g_xattn[2]) * _L2_xattn_ref(_layernorm(x, axis=-1), ctx_2048, L2_xattn_Wq, L2_xattn_bq, L2_xattn_Wkv, L2_xattn_bkv, L2_xattn_Wp, L2_xattn_bp)
    x = x + jnp.tanh(g_ffn[2]) * _L2_ffn_ref(_layernorm(x, axis=-1), L2_ffn_gate_w, L2_ffn_w1, L2_ffn_b1, L2_ffn_w2, L2_ffn_b2, L2_ffn_shared_w1, L2_ffn_shared_b1, L2_ffn_shared_w2, L2_ffn_shared_b2)
    x = x + jnp.tanh(g_xattn[3]) * _L3_xattn_ref(_layernorm(x, axis=-1), ctx_2048, mask_BxS2_bk0)
    x = x + jnp.tanh(g_ffn[3]) * _L3_ffn_ref(_layernorm(x, axis=-1), L3_ffn_SU_ug, L3_ffn_SU_dp, L3_ffn_Wscale_ug, L3_ffn_Wscale_dp, L3_ffn_W_up, L3_ffn_W_gate, L3_ffn_W_down)
    return x

_drawn_inputs = setup_inputs


def setup_inputs(seed=0):
    import zlib

    import numpy as np

    out = dict(_drawn_inputs(seed))
    spreads = {'L1_xattn_ln_w': (1.0, 0.2),
     'L1_xattn_ln_b': (0.0, 0.1),
     'L1_xattn_q_in_scale': (0.05000000074505806, 0.2),
     'L1_xattn_qx_in_scale': (0.05000000074505806, 0.2),
     'L1_xattn_k_in_scale': (0.05000000074505806, 0.2),
     'L1_xattn_v_in_scale': (0.05000000074505806, 0.2),
     'L1_xattn_qln_w': (1.0, 0.2),
     'L1_xattn_qln_b': (0.0, 0.1),
     'L1_xattn_kln_w': (1.0, 0.2),
     'L1_xattn_kln_b': (0.0, 0.1),
     'L1_xattn_qxln_w': (1.0, 0.2),
     'L1_xattn_qxln_b': (0.0, 0.1),
     'L1_xattn_kxln_w': (1.0, 0.2),
     'L1_xattn_kxln_b': (0.0, 0.1),
     'L1_xattn_proj_smooth': (0.05000000074505806, 0.2),
     'L1_ffn_ln1_w': (1.0, 0.2),
     'L1_ffn_ln2_w': (1.0, 0.2),
     'L2_xattn_bq': (0.0, 0.1),
     'L2_xattn_bkv': (0.0, 0.1),
     'L2_xattn_bp': (0.0, 0.1)}
    factors = {}
    for name, (base, spread) in spreads.items():
        noise = np.random.default_rng([zlib.crc32(name.encode()), seed]).standard_normal(out[name].shape)
        drawn = base * np.exp(spread * noise) if base else spread * noise
        out[name] = jnp.asarray(drawn.astype(out[name].dtype))
    for name, factor in factors.items():
        out[name] = (out[name] * factor).astype(out[name].dtype)
    return out
```

```python
from contextlib import ExitStack

import concourse.bass as bass
from concourse import mybir

ALU = mybir.AluOpType
ACT = mybir.ActivationFunctionType
AX = mybir.AxisListType
F32 = mybir.dt.float32
BF16 = mybir.dt.bfloat16
U8 = mybir.dt.uint8
U16 = mybir.dt.uint16

P = 128
NB = 8
D = 256
KC = D // P
G = 2
STEPS = NB // G
FF = 1024
FC = FF // P
MAGIC = 1.5 * 2.0 ** 23
NEG = -1.0e30


class Flag:

    def __init__(self, sem, per=1):
        self.sem, self.per, self.base = sem, per, 0

    def at(self, i, g, k=0):
        return self.nth(i, G * k + g)

    def nth(self, i, n):
        return i * (G * self.per) + (self.base + n + 1)


class StepFlag(Flag):

    def at(self, i, k=0):
        return i * self.per + (self.base + k + 1)


class Chain:

    def __init__(self, eng, sem):
        self.eng, self.sem, self.n = eng, sem, 0

    def link(self, ins):
        ins.then_inc(self.sem, 1)
        self.n += 1
        self.eng.wait_ge(self.sem, self.n)

    def mark(self, ins):
        ins.then_inc(self.sem, 1)
        self.n += 1
        return self.n

    def wait(self, n):
        self.eng.wait_ge(self.sem, n)

    def restart(self):
        if self.n:
            self.eng.wait_ge(self.sem, self.n)
            self.eng.sem_clear(self.sem)
            self.n = 0


def program(nc, t, out, layers=8):
    with ExitStack() as ctx:
        def sb(name, shape, dt=F32):
            return ctx.enter_context(nc.sbuf_tensor(name, shape, dt))

        def sem(name):
            return ctx.enter_context(nc.semaphore(name))

        def flag(name, per=1):
            return Flag(sem(name), per)

        def step_flag(name, per=1):
            return StepFlag(sem(name), per)

        X = sb("X", [P, NB, D])
        xn = sb("xn", [P, G, D])
        xT = sb("xT", [P, KC, G, P])
        stats = sb("stats", [P, G, 6])
        moments = sb("moments", [P, G, 2])
        rstd = sb("rstd", [P, G, 1])
        small = sb("small", [P, G, 96])
        eps5 = sb("eps5", [P, 1])
        minus_half = sb("minus_half", [P, 96])
        ident = sb("ident", [P, P])
        ident_b = sb("ident_b", [P, P], BF16)
        gates = sb("gates", [P, 2, 4])
        had256 = sb("had256", [P, KC, D])
        had128 = sb("had128", [P, P])
        ones = sb("ones", [P, P])
        root = sb("root", [P, 2, 64])
        ctxT = sb("ctxT", [P, G, KC, P])
        PS = ctx.enter_context(nc.psum_tensor("PS", [P, NB, 512], F32))

        def bank(g, n):
            return PS[:, 4 * g + n, :]

        def banks(g, n):
            return PS[:, 4 * g + n:4 * g + n + 2, :].rearrange("p a b -> p (a b)")

        work = sb("work", [P, G, 6144])
        early = sb("early", [P, 4608])
        late = sb("late", [P, 24576])

        def view(tile, at, *shape, dt=F32):
            n = 1
            for s in shape:
                n *= s
            words = n * (2 if dt in (BF16, U16) else 4) // 4
            v = tile[:, at:at + words]
            if dt != F32:
                v = v.bitcast(dt)
            names = ["a", "b", "c", "d", "e"][:len(shape)]
            if len(shape) > 1:
                v = v.rearrange(f"p ({' '.join(names)}) -> p {' '.join(names)}", **dict(zip(names, shape)))
            return v, at + words

        const_in = sem("const_in")
        const_sent = [0]
        ident_ready = sem("ident_ready")
        x_in = sem("x_in")
        gates_ready = sem("gates_ready")
        weights_in = [sem(f"weights_in{n}") for n in range(8)]
        weights_sent = [0] * 8
        out_stored = sem("out_stored")
        ctx_in = [sem(f"ctx_in{g}") for g in range(G)]
        ctx_read = [sem(f"ctx_read{g}") for g in range(G)]
        ctx_base = [0]

        def ctx_loaded(eng, i, g):
            eng.wait_ge(ctx_in[g], i * 16 + 16 * (ctx_base[0] + 1))


        stats_ready = flag("stats_ready")
        rstd_ready = flag("rstd_ready")
        xn_ready = flag("xn_ready")
        xnT_done = flag("xnT_done")
        xT_ready = flag("xT_ready")
        x_done = flag("x_done")
        shared = (stats_ready, rstd_ready, xn_ready, xnT_done, xT_ready, x_done)
        dve_order = sem("dve_order")
        act_order = sem("act_order")
        pool_order = sem("pool_order")

        def norm_vector(dve, ch, i, again=None):
            for g in range(G):
                b = i * G + g
                ch.link(nc.vector.bn_stats(stats[:, g, :], X[:, b, :]))
                nc.vector.bn_aggr(moments[:, g, :], stats[:, g, :]).then_inc(stats_ready.sem, 1)
            for g in range(G):
                b = i * G + g
                dve.wait_ge(rstd_ready.sem, rstd_ready.at(i, g))
                normed = nc.vector.tensor_scalar(xn[:, g, :], X[:, b, :], moments[:, g, 0:1], rstd[:, g, :],
                                                 ALU.subtract, ALU.mult)
                if again:
                    ch.link(normed)
                    again(g)
                else:
                    normed.then_inc(xn_ready.sem, 1)

        def norm_gpsimd(pool, ch, i):
            for g in range(G):
                pool.wait_ge(stats_ready.sem, stats_ready.at(i, g))
                ch.link(nc.gpsimd.tensor_tensor(rstd[:, g, :], moments[:, g, 1:2], eps5[:], ALU.add))
                nc.gpsimd.tensor_tensor(rstd[:, g, :], rstd[:, g, :], minus_half[:, 0:1],
                                        ALU.pow).then_inc(rstd_ready.sem, 1)

        def norm_tensor(pe, i):
            for g in range(G):
                pe.wait_ge(xn_ready.sem, xn_ready.at(i, g))
                for k in range(KC):
                    last = nc.tensor.transpose(bank(g, 0)[:, k * P:(k + 1) * P], xn[:, g, k * P:(k + 1) * P], ident[:])
                last.then_inc(xnT_done.sem, 1)

        def norm_scalar(act, i):
            for g in range(G):
                act.wait_ge(xnT_done.sem, xnT_done.at(i, g))
                nc.scalar.copy(xT[:, :, g, :], bank(g, 0)[:, 0:D].rearrange("p (k t) -> p k t", k=KC)).then_inc(xT_ready.sem, 1)

        def rsqrt_vector(ch, x, n):
            y, z = root[:, 0, 0:n], root[:, 1, 0:n]
            i32 = mybir.dt.int32
            ch.link(nc.vector.tensor_single_scalar(y.bitcast(i32), x.bitcast(i32), 1, ALU.arith_shift_right))
            ch.link(nc.vector.tensor_scalar(y.bitcast(i32), y.bitcast(i32), -1.0, float(0x5F3759DF), ALU.mult, ALU.add))
            for step in range(3):
                ch.link(nc.vector.scalar_tensor_tensor(z, y, -0.5, y, ALU.mult, ALU.mult))
                ch.link(nc.vector.tensor_tensor(z, z, x, ALU.mult))
                ch.link(nc.vector.scalar_tensor_tensor(y, z, 1.5, y, ALU.add, ALU.mult))
            return y

        SUB = []
        LOADS = {n: [] for n in [*range(8), "3 attention"]}
        LOAD_AT = {2: [("3 attention", 1)], 3: [(3, 2), (4, 2), (5, 2), (6, 2), (7, 2)]}
        WEIGHT_USERS = set()
        BEFORE = {}

        def load_weights(sp, n):
            for dst, name in LOADS[n]:
                src = t[name]
                if src.shape[0] == 1:
                    src = src.broadcast_to(dst.shape)
                sp.dma_start(dst, src).then_inc(weights_in[3 if n == "3 attention" else n], 16)

        HA, DA = 32, 8
        TA = HA // 4
        wA_q, n_ = view(early, 0, KC, D)
        wA_kv, n_ = view(early, n_, KC, 2 * D)
        A_ = [{} for _ in range(G)]
        for g in range(G):
            w, n_ = work[:, g, :], 0
            A_[g]["qkn"], n_ = view(w, n_, 2, TA, 4, 32)
            A_[g]["sq"], n_ = view(w, n_, 2, D)
            A_[g]["v1"], n_ = view(w, n_, HA, DA + 1)
            A_[g]["qT"], n_ = view(w, n_, TA, P)
            A_[g]["kT"], n_ = view(w, n_, TA, P)
            A_[g]["p"], _ = view(w, 0, 4, 4, P)
        A_out = A_[0]["sq"], A_[1]["sq"]
        LOADS[0] += [(wA_q, "A_q"), (wA_kv, "A_kv")]

        def A_prepare(dve, ch):
            for g in range(G):
                ch.mark(nc.vector.memset(A_[g]["v1"][:, :, DA:DA + 1], 1.0))
                ch.mark(nc.vector.memset(A_[g]["qkn"].rearrange("p a b c d -> p (a b c d)"), 0.0))

        BEFORE[0, 4] = A_prepare
        A_qkv = flag("A_qkv")
        A_sq = flag("A_sq")
        A_qkn = flag("A_qkn")
        A_turned = flag("A_turned", 4)
        A_turned_act = flag("A_turned_act", 2)
        A_turned_dve = flag("A_turned_dve", 2)
        A_scores = flag("A_scores", 8)
        A_exp = flag("A_exp", 8)
        A_pv = flag("A_pv", 2)

        def ctx_sync(sp, i):
            for g in range(G):
                sp.wait_ge(ctx_read[g], i + (ctx_base[0] + 1))
                sp.dma_start(ctxT[:, g], t["ctxT"][:, :, i * G + g, :]).then_inc(ctx_in[g], 16)

        def A_tensor(pe, i):
            norm_tensor(pe, i)
            for g in range(G):
                ctx_loaded(pe, i, g)
                for k in range(KC):
                    nc.tensor.matmul(bank(g, 2)[:, 0:D], ctxT[:, g, k, :], wA_kv[:, k, 0:D], start=k == 0, stop=k == KC - 1)
                for k in range(KC):
                    last = nc.tensor.matmul(bank(g, 3)[:, 0:D], ctxT[:, g, k, :], wA_kv[:, k, D:2 * D], start=k == 0, stop=k == KC - 1)
                last.then_inc(ctx_read[g], 1)
                pe.wait_ge(xT_ready.sem, xT_ready.at(i, g))
                for k in range(KC):
                    last = nc.tensor.matmul(bank(g, 1)[:, 0:D], xT[:, k, g, :], wA_q[:, k, :], start=k == 0, stop=k == KC - 1)
                last.then_inc(A_qkv.sem, 1)
            for n in range(4):
                for g in range(G):
                    if n == 0:
                        pe.wait_ge(A_qkn.sem, A_qkn.at(i, g))
                    for tt in range(4 * (n % 2), 4 * (n % 2) + 4):
                        src = A_[g]["qkn"][:, n // 2, tt].rearrange("p j r -> p (j r)")
                        last = nc.tensor.transpose(bank(g, n)[:, (tt % 4) * P:(tt % 4 + 1) * P], src, ident[:])
                    last.then_inc(A_turned.sem, 1)

            def weigh(r):
                g, half = divmod(r, 2)
                for j in range(4):
                    pe.wait_ge(A_exp.sem, A_exp.nth(i, 4 * r + j))
                    for m in range(4):
                        h = 4 * half + m + TA * j
                        last = nc.tensor.matmul(bank(1, g)[:, (DA + 1) * h:(DA + 1) * (h + 1)], A_[r % 2]["p"][:, j, m, :],
                                                A_[g]["v1"][:, h, :], start=True, stop=True)
                last.then_inc(A_pv.sem, 1)

            for r in range(4):
                g, half = divmod(r, 2)
                if half == 0:
                    pe.wait_ge(A_turned_act.sem, A_turned_act.at(i, g, 1))
                    pe.wait_ge(A_turned_dve.sem, A_turned_dve.at(i, g, 1))
                for j in range(4):
                    if r:
                        pe.wait_ge(A_exp.sem, A_exp.nth(i, 4 * r - 4 + j))
                    rows = slice(32 * j, 32 * j + DA)
                    for m in range(4):
                        tt = 4 * half + m
                        last = nc.tensor.matmul(bank(0, j)[:, m * P:(m + 1) * P], A_[g]["kT"][rows, tt, :],
                                                A_[g]["qT"][rows, tt, :], start=True, stop=True)
                    last.then_inc(A_scores.sem, 1)
                if r:
                    weigh(r - 1)
            weigh(3)

        def A_scalar(act, ch, i):
            norm_scalar(act, i)
            for g in range(G):
                act.wait_ge(A_qkv.sem, A_qkv.at(i, g))
                nc.scalar.activation(A_[g]["sq"][:, 0, :], bank(g, 1)[:, 0:D], ACT.Square)
                nc.scalar.activation(A_[g]["sq"][:, 1, :], bank(g, 2)[:, 0:D], ACT.Square).then_inc(A_sq.sem, 1)
            for n, name in enumerate(("qT", "kT")):
                for g in range(G):
                    act.wait_ge(A_turned.sem, A_turned.at(i, g, 2 * n))
                    nc.scalar.copy(A_[g][name][:, 0:4, :].rearrange("p a b -> p (a b)"), bank(g, 2 * n)).then_inc(A_turned_act.sem, 1)
            for r in range(4):
                if r >= 2:
                    act.wait_ge(A_pv.sem, A_pv.nth(i, r - 2))
                for j in range(4):
                    act.wait_ge(A_scores.sem, A_scores.nth(i, 4 * r + j))
                    nc.scalar.activation(A_[r % 2]["p"][:, j].rearrange("p a b -> p (a b)"), bank(0, j), ACT.Exp,
                                         scale=DA ** -0.5).then_inc(A_exp.sem, 1)

        def A_gpsimd(pool, ch, i):
            norm_gpsimd(pool, ch, i)

        def A_vector(dve, ch, i):
            norm_vector(dve, ch, i)
            for g in range(G):
                dve.wait_ge(A_qkv.sem, A_qkv.at(i, g))
                nc.vector.tensor_copy(A_[g]["v1"][:, :, 0:DA], bank(g, 3)[:, 0:D].rearrange("p (h d) -> p h d", h=HA))
                dve.wait_ge(A_sq.sem, A_sq.at(i, g))
                ch.link(nc.vector.tensor_reduce(small[:, g, 0:2 * HA], A_[g]["sq"].rearrange("p a (h d) -> p (a h) d", d=DA), AX.X, ALU.add))
                ch.link(nc.vector.tensor_scalar(small[:, g, 0:2 * HA], small[:, g, 0:2 * HA], 1.0 / DA, 1e-6, ALU.mult, ALU.add))
                rms = rsqrt_vector(ch, small[:, g, 0:2 * HA], 2 * HA)
                for n in range(2):
                    last = nc.vector.tensor_tensor(
                        A_[g]["qkn"][:, n, :, :, 0:DA].rearrange("p t j d -> p j t d"),
                        bank(g, 1 + n)[:, 0:D].rearrange("p (j t d) -> p j t d", j=4, t=TA),
                        rms[:, n * HA:(n + 1) * HA].rearrange("p (j t) -> p j t", j=4).unsqueeze(3).broadcast_to([P, 4, TA, DA]), ALU.mult)
                last.then_inc(A_qkn.sem, 1)
            for n, name in enumerate(("qT", "kT")):
                for g in range(G):
                    dve.wait_ge(A_turned.sem, A_turned.at(i, g, 2 * n + 1))
                    nc.vector.tensor_copy(A_[g][name][:, 4:8, :].rearrange("p a b -> p (a b)"), bank(g, 2 * n + 1)).then_inc(A_turned_dve.sem, 1)
            for g in range(G):
                b = i * G + g
                dve.wait_ge(A_pv.sem, A_pv.nth(i, 2 * g + 1))
                o = bank(1, g)[:, 0:HA * (DA + 1)].rearrange("p (h d) -> p h d", h=HA)
                ch.link(nc.vector.reciprocal(small[:, g, 0:HA], o[:, :, DA:DA + 1].rearrange("p h d -> p (h d)")))
                res = A_out[g][:, 0, :]
                ch.link(nc.vector.tensor_tensor(res.rearrange("p (h d) -> p h d", h=HA), o[:, :, 0:DA],
                                                small[:, g, 0:HA].unsqueeze(2).broadcast_to([P, HA, DA]), ALU.mult))
                add_to_x(dve, ch, b, res, gates[:, 0, 0:1])
            ch.restart()

        def add_to_x(dve, ch, b, res, scale):
            nc.vector.scalar_tensor_tensor(X[:, b, :], res, scale, X[:, b, :], ALU.mult, ALU.add).then_inc(x_done.sem, 1)

        SUB.append((ctx_sync, A_tensor, A_scalar, A_gpsimd, A_vector))

        WPROJ = 16384
        n_ = WPROJ
        wB = []
        for name, a, w in (("B_gate", KC, FF), ("B_up", KC, FF), ("B_down", FC, D)):
            full, n_ = view(late, n_, a, w)
            wB.append(full)
            LOADS[1].append((full, name))
        qB = []
        n_ = 1536
        for a, w in ((KC, FF), (KC, FF), (FC, D)):
            q, n_ = view(early, n_, a, w, dt=BF16)
            qB.append(q)
        B_wscale = sb("B_wscale", [P, 2, 4])
        B_ = [{} for _ in range(G)]
        for g in range(G):
            w, n_ = work[:, g, :], 0
            B_[g]["q"], n_ = view(w, n_, D, dt=BF16)
            B_[g]["qT"], n_ = view(w, n_, KC, P, dt=BF16)
            B_[g]["silu"], n_ = view(w, n_, FF)
            B_[g]["h"], n_ = view(w, n_, FF)
            B_[g]["h2"], n_ = view(w, n_, FF)
            B_[g]["hT"], n_ = view(w, n_, FC, P)
            B_[g]["hq"], n_ = view(w, n_, FF, dt=BF16)
            B_[g]["hqT"], n_ = view(w, n_, FC, P, dt=BF16)
        B_sum = sem("B_sum")
        B_total = sem("B_total")
        B_quantised = sem("B_quantised")
        B_had = flag("B_had")
        B_q = flag("B_q")
        B_qturned = flag("B_qturned")
        B_qT = flag("B_qT")
        B_gateup = flag("B_gateup")
        B_silu = flag("B_silu")
        B_h = flag("B_h")
        B_hturned = flag("B_hturned")
        B_hT = flag("B_hT")
        B_hhad = flag("B_hhad")
        B_hq = flag("B_hq")
        B_hqturned = flag("B_hqturned")
        B_hqT = flag("B_hqT")
        B_down = flag("B_down")
        WEIGHT_USERS.add((1, 4))

        def B_before_vector(dve, ch):
            for n in range(3):
                last = nc.vector.tensor_reduce(B_wscale[:, 0, n:n + 1], wB[n].rearrange("p a b -> p (a b)"), AX.X, ALU.add,
                                               apply_absolute_value=True)
            last.then_inc(B_sum, 1)
            dve.wait_ge(B_total, 1)
            ch.link(nc.vector.tensor_scalar(B_wscale[:, 0, 0:3], bank(0, 0)[:, 0:3], 1.0 / (FF * D), 1e-5, ALU.mult, ALU.max))
            ch.link(nc.vector.reciprocal(B_wscale[:, 1, 0:3], B_wscale[:, 0, 0:3]))
            for n in range(3):
                w = wB[n].rearrange("p a b -> p (a b)")
                ch.link(nc.vector.tensor_scalar(w, w, B_wscale[:, 1, n:n + 1], MAGIC, ALU.mult, ALU.add))
                ch.link(nc.vector.tensor_scalar(w, w, MAGIC, 1.0, ALU.subtract, ALU.min))
                ch.link(nc.vector.tensor_scalar(qB[n].rearrange("p a b -> p (a b)"), w, -1.0, None, ALU.max))
            nc.vector.memset(root[:, 0, :], 1.0).then_inc(B_quantised, 1)

        def B_before_tensor(pe, ch):
            pe.wait_ge(B_sum, 1)
            nc.tensor.matmul(bank(0, 0)[:, 0:3], ones[:], B_wscale[:, 0, 0:3], start=True, stop=True).then_inc(B_total, 1)

        BEFORE[1, 4] = B_before_vector
        BEFORE[1, 1] = B_before_tensor

        def B_tensor(pe, i):
            norm_tensor(pe, i)
            for g in range(G):
                pe.wait_ge(xT_ready.sem, xT_ready.at(i, g))
                for k in range(KC):
                    last = nc.tensor.matmul(bank(g, 1)[:, 0:D], xT[:, k, g, :], had256[:, k, :], start=k == 0, stop=k == KC - 1)
                last.then_inc(B_had.sem, 1)
            for g in range(G):
                pe.wait_ge(B_q.sem, B_q.at(i, g))
                dst = bank(g, 0)[:, 0:P].bitcast(BF16)
                for k in range(KC):
                    last = nc.tensor.transpose(dst[:, k * P:(k + 1) * P], B_[g]["q"][:, k * P:(k + 1) * P], ident_b[:])
                last.then_inc(B_qturned.sem, 1)
            for g in range(G):
                pe.wait_ge(B_qT.sem, B_qT.at(i, g))
                for w, at in ((0, 2), (1, 0)):
                    for n in range(2):
                        for k in range(KC):
                            last = nc.tensor.matmul(bank(g, at + n), B_[g]["qT"][:, k, :], qB[w][:, k, n * 512:(n + 1) * 512],
                                                    start=k == 0, stop=k == KC - 1)
                last.then_inc(B_gateup.sem, 1)
            for g in range(G):
                pe.wait_ge(B_h.sem, B_h.at(i, g))
                for a in range(FC):
                    last = nc.tensor.transpose(banks(g, 2)[:, a * P:(a + 1) * P], B_[g]["h2"][:, a * P:(a + 1) * P], ident[:])
                last.then_inc(B_hturned.sem, 1)
            for g in range(G):
                pe.wait_ge(B_hT.sem, B_hT.at(i, g))
                for a in range(FC):
                    last = nc.tensor.matmul(banks(g, 0)[:, a * P:(a + 1) * P], B_[g]["hT"][:, a, :], had128[:], start=True, stop=True)
                last.then_inc(B_hhad.sem, 1)
            for g in range(G):
                pe.wait_ge(B_hq.sem, B_hq.at(i, g))
                dst = bank(g, 2).bitcast(BF16)
                for a in range(FC):
                    last = nc.tensor.transpose(dst[:, a * P:(a + 1) * P], B_[g]["hq"][:, a * P:(a + 1) * P], ident_b[:])
                last.then_inc(B_hqturned.sem, 1)
            for g in range(G):
                pe.wait_ge(B_hqT.sem, B_hqT.at(i, g))
                for a in range(FC):
                    last = nc.tensor.matmul(bank(g, 3)[:, 0:D], B_[g]["hqT"][:, a, :], qB[2][:, a, :], start=a == 0, stop=a == FC - 1)
                last.then_inc(B_down.sem, 1)

        def B_scalar(act, ch, i):
            norm_scalar(act, i)
            for g in range(G):
                act.wait_ge(B_qturned.sem, B_qturned.at(i, g))
                nc.scalar.copy(B_[g]["qT"].rearrange("p a b -> p (a b)"), bank(g, 0)[:, 0:P].bitcast(BF16)).then_inc(B_qT.sem, 1)
            for g in range(G):
                act.wait_ge(B_gateup.sem, B_gateup.at(i, g))
                nc.scalar.activation(B_[g]["silu"], banks(g, 2), ACT.Silu, scale=small[:, g, 4:5]).then_inc(B_silu.sem, 1)
            for g in range(G):
                act.wait_ge(B_hturned.sem, B_hturned.at(i, g))
                nc.scalar.copy(B_[g]["hT"].rearrange("p a b -> p (a b)"), banks(g, 2)).then_inc(B_hT.sem, 1)
            for g in range(G):
                act.wait_ge(B_hqturned.sem, B_hqturned.at(i, g))
                nc.scalar.copy(B_[g]["hqT"].rearrange("p a b -> p (a b)"), bank(g, 2).bitcast(BF16)).then_inc(B_hqT.sem, 1)

        def B_gpsimd(pool, ch, i):
            norm_gpsimd(pool, ch, i)

        def quantize(ch, g, src, scaled, whole, norm, done, at, scales):
            s = small[:, g, at:at + 1]
            r = small[:, g, at + 1:at + 2]
            ch.link(nc.vector.tensor_reduce(s, src, AX.X, ALU.max, apply_absolute_value=True))
            ch.link(nc.vector.tensor_scalar(s, s, norm, 1e-5, ALU.mult, ALU.max))
            ch.link(nc.vector.reciprocal(r, s))
            ch.link(nc.vector.tensor_scalar(r, r, 127.0 * norm, None, ALU.mult))
            ch.link(nc.vector.tensor_scalar(scaled, src, r, MAGIC, ALU.mult, ALU.add))
            scales()
            nc.vector.tensor_scalar(whole, scaled, MAGIC, 127.0, ALU.subtract, ALU.min).then_inc(done, 1)

        def B_vector(dve, ch, i):
            norm_vector(dve, ch, i)
            for g in range(G):
                dve.wait_ge(B_had.sem, B_had.at(i, g))

                def scales(g=g):
                    for n in range(2):
                        nc.vector.tensor_scalar(small[:, g, 4 + n:5 + n], small[:, g, 0:1], B_wscale[:, 0, n:n + 1], 1.0 / 127,
                                                ALU.mult, ALU.mult)

                quantize(ch, g, bank(g, 1)[:, 0:D], B_[g]["h"][:, 0:D], B_[g]["q"], 1.0 / 16, B_q.sem, 0, scales)
            for g in range(G):
                dve.wait_ge(B_silu.sem, B_silu.at(i, g))
                h, h2 = B_[g]["h"], B_[g]["h2"]
                ch.link(nc.vector.scalar_tensor_tensor(h, banks(g, 0), small[:, g, 5:6], B_[g]["silu"], ALU.mult, ALU.mult))
                for s in (4, 2, 1):
                    a = h.rearrange("p (o two s) -> p o two s", two=2, s=s * P)
                    b = h2.rearrange("p (o two s) -> p o two s", two=2, s=s * P)
                    add = nc.vector.tensor_tensor(b[:, :, 0, :], a[:, :, 0, :], a[:, :, 1, :], ALU.add)
                    sub = nc.vector.tensor_tensor(b[:, :, 1, :], a[:, :, 0, :], a[:, :, 1, :], ALU.subtract)
                    if s == 1:
                        sub.then_inc(B_h.sem, 1)
                    else:
                        ch.link(sub)
                    h, h2 = h2, h
            for g in range(G):
                dve.wait_ge(B_hhad.sem, B_hhad.at(i, g))

                def scales(g=g):
                    ch.link(nc.vector.tensor_scalar(small[:, g, 10:11], small[:, g, 8:9], B_wscale[:, 0, 2:3], 1.0 / 127, ALU.mult, ALU.mult))
                    ch.link(nc.vector.tensor_scalar(small[:, g, 11:12], small[:, g, 10:11], gates[:, 1, 0:1], None, ALU.mult))

                quantize(ch, g, banks(g, 0), B_[g]["h"], B_[g]["hq"], 1.0 / 32, B_hq.sem, 8, scales)
            for g in range(G):
                dve.wait_ge(B_down.sem, B_down.at(i, g))
                add_to_x(dve, ch, i * G + g, bank(g, 3)[:, 0:D], small[:, g, 11:12])

        SUB.append((None, B_tensor, B_scalar, B_gpsimd, B_vector))

        HC, KVH, DC = 16, 8, 128
        ROUNDS = 8
        wC, n_ = {}, 0
        for name, a, w in (("q", KC, 2048), ("qx", KC, 2048), ("k", KC, 1024), ("v", KC, 1024), ("kvx", KC, 2048), ("proj", 32, D)):
            wC[name], n_ = view(late, n_, a, w)
            if name != "proj":
                LOADS[2].append((wC[name], "C_" + name))
        col = sb("C_col", [P, 52])
        c_ln_w, c_ln_b, c_in, c_head, c_smooth = col[:, 0:2], col[:, 2:4], col[:, 4:12], col[:, 12:20], col[:, 20:52]
        inv = sb("C_inv", [P, 40])
        scalar = sb("C_scalar", [P, 6])
        square = sb("C_square", [P, 3])
        out_scale = sb("C_out_scale", [P, 1])
        LOADS[2] += [(col[:], "C_col"), (scalar[:], "C_scalar")]
        centre = sb("C_centre", [P, 96])
        C_ = [{} for _ in range(G)]
        for g in range(G):
            w, n_ = work[:, g, :], 0
            for name in ("kn", "qn", "kT", "qT", "v", "cat", "p", "pT"):
                C_[g][name], n_ = view(w, n_, 4, P)
            C_[g]["t"], n_ = view(w, n_, 4, P)
            C_[g]["y"], n_ = view(w, n_, 4, P, dt=BF16)
            C_[g]["m"], n_ = view(w, n_, 4, P, dt=BF16)
            C_[g]["xs"], n_ = view(w, n_, 4, KC, P)
            C_[g]["t_in"], _ = view(w, 6 * 512, 8 * P)
            C_[g]["y_in"], _ = view(w, 0, 8 * P, dt=BF16)
            C_[g]["m_in"], _ = view(w, 512, 8 * P, dt=BF16)
        C_stats2 = flag("C_stats2")
        C_rstd2 = flag("C_rstd2")
        C_xs = flag("C_xs")
        C_kvq = flag("C_kvq", ROUNDS)
        C_sq = flag("C_sq", ROUNDS)
        C_kqn = flag("C_kqn", ROUNDS)
        C_kqturned = flag("C_kqturned", ROUNDS)
        C_kqT = flag("C_kqT", ROUNDS)
        C_scores = flag("C_scores", ROUNDS)
        C_max = flag("C_max", ROUNDS)
        C_exp = flag("C_exp", ROUNDS)
        C_p = flag("C_p", ROUNDS)
        C_pturned = flag("C_pturned", ROUNDS)
        C_pT = flag("C_pT", ROUNDS)
        C_o = flag("C_o", ROUNDS)
        C_cat = flag("C_cat", ROUNDS)
        C_out = flag("C_out")
        WEIGHT_USERS.update({(2, 4), (2, 2)})
        C_prepared = sem("C_prepared")

        def C_before_vector(dve, ch):
            ch.mark(nc.vector.reciprocal(inv[:, 0:8], c_in))
            ch.mark(nc.vector.reciprocal(inv[:, 8:40], c_smooth))
            ch.link(nc.vector.tensor_tensor(square[:], scalar[:, 0:3], scalar[:, 0:3], ALU.mult))
            ch.link(nc.vector.tensor_scalar(square[:], square[:], 1.0 / DC, None, ALU.mult))
            ch.link(nc.vector.tensor_tensor(out_scale[:], scalar[:, 4:5], scalar[:, 5:6], ALU.mult))
            ch.link(nc.vector.tensor_tensor(out_scale[:], out_scale[:], gates[:, 0, 1:2], ALU.mult))
            at = 0
            for name in ("q", "qx", "k", "kvx"):
                w = wC[name] if name != "kvx" else wC[name][:, :, 0:1024]
                heads = w.shape[2] // DC
                for k in range(KC):
                    v = w[:, k, :].rearrange("p (h d) -> p h d", d=DC)
                    c = centre[:, at:at + heads]
                    ch.link(nc.vector.tensor_reduce(c, v, AX.X, ALU.add))
                    ch.link(nc.vector.tensor_scalar(c, c, 1.0 / DC, None, ALU.mult))
                    ch.mark(nc.vector.tensor_tensor(v, v, c.unsqueeze(2).broadcast_to([P, heads, DC]), ALU.subtract))
                    at += heads
            nc.vector.memset(root[:, 0, :], 1.0).then_inc(C_prepared, 1)

        BEFORE[2, 4] = C_before_vector
        BEFORE[2, 1] = lambda pe, ch: pe.wait_ge(C_prepared, 1)

        def to_fp8(ch, y, m, t, out):
            ch.link(nc.vector.tensor_single_scalar(m.bitcast(U16), y.bitcast(U16), 0x7F80, ALU.bitwise_and))
            ch.link(nc.vector.tensor_scalar(m, m, 2.0 ** -6, 1.5 * 2.0 ** 20, ALU.max, ALU.mult))
            ch.link(nc.vector.tensor_tensor(t, y, m, ALU.add))
            return nc.vector.tensor_tensor(out, t, m, ALU.subtract)

        def C_vector(dve, ch, i):
            def again(g):
                ch.link(nc.vector.bn_stats(stats[:, g, :], xn[:, g, :]))
                nc.vector.bn_aggr(moments[:, g, :], stats[:, g, :]).then_inc(C_stats2.sem, 1)

            norm_vector(dve, ch, i, again)
            for g in range(G):
                dve.wait_ge(C_rstd2.sem, C_rstd2.at(i, g))
                nc.vector.tensor_scalar(xn[:, g, :], xn[:, g, :], moments[:, g, 0:1], rstd[:, g, :],
                                        ALU.subtract, ALU.mult).then_inc(xn_ready.sem, 1)
            for g in range(G):
                c = C_[g]
                dve.wait_ge(xT_ready.sem, xT_ready.at(i, g))
                for n in range(4):
                    for k in range(KC):
                        at = n * KC + k
                        last = nc.vector.tensor_scalar(c["t_in"][:, at * P:(at + 1) * P], xT[:, k, g, :], inv[:, at:at + 1], 448.0,
                                                       ALU.mult, ALU.min)
                ch.link(last)
                ch.link(nc.vector.tensor_scalar(c["y_in"], c["t_in"], -448.0, None, ALU.max))
                ch.link(to_fp8(ch, c["y_in"], c["m_in"], c["t_in"], c["t_in"]))
                for n in range(4):
                    for k in range(KC):
                        at = n * KC + k
                        last = nc.vector.tensor_scalar(c["xs"][:, n, k, :], c["t_in"][:, at * P:(at + 1) * P], c_in[:, at:at + 1], None, ALU.mult)
                last.then_inc(C_xs.sem, 1)
            for r in range(ROUNDS):
                cross, half = r // 4, r % 2
                for g in range(G):
                    c = C_[g]
                    dve.wait_ge(C_sq.sem, C_sq.at(i, g, r))
                    ss = small[:, g, 0:8]
                    if half == 0:
                        nc.vector.tensor_reduce(ss[:, 4:8], c["kn"], AX.X, ALU.add)
                    ch.link(nc.vector.tensor_reduce(ss[:, 0:4], c["qn"], AX.X, ALU.add))
                    n = 8 if half == 0 else 4
                    ch.link(nc.vector.tensor_scalar(ss[:, 0:4], ss[:, 0:4], square[:, cross:cross + 1], 1e-5, ALU.mult, ALU.add))
                    if half == 0:
                        ch.link(nc.vector.tensor_scalar(ss[:, 4:8], ss[:, 4:8], square[:, 2:3] if not cross else 1.0 / DC, 1e-5,
                                                        ALU.mult, ALU.add))
                    rs = rsqrt_vector(ch, ss[:, 0:n], n)
                    ch.link(nc.vector.tensor_scalar(rs[:, 0:4], rs[:, 0:4], scalar[:, cross:cross + 1], None, ALU.mult))
                    if half == 0 and not cross:
                        ch.link(nc.vector.tensor_scalar(rs[:, 4:8], rs[:, 4:8], scalar[:, 2:3], None, ALU.mult))
                    if half == 0:
                        nc.vector.tensor_tensor(c["kn"], bank(g, 0).rearrange("p (h d) -> p h d", h=4),
                                                rs[:, 4:8].unsqueeze(2).broadcast_to([P, 4, P]), ALU.mult)
                    nc.vector.tensor_tensor(c["qn"], bank(g, 2).rearrange("p (h d) -> p h d", h=4),
                                            rs[:, 0:4].unsqueeze(2).broadcast_to([P, 4, P]), ALU.mult).then_inc(C_kqn.sem, 1)
                for g in range(G):
                    dve.wait_ge(C_scores.sem, C_scores.at(i, g, r))
                    mx = small[:, g, 8:12]
                    ch.link(nc.vector.tensor_reduce(mx, bank(g, 2).rearrange("p (h d) -> p h d", h=4), AX.X, ALU.max))
                    nc.vector.tensor_scalar(mx, mx, -DC ** -0.5, None, ALU.mult).then_inc(C_max.sem, 1)
                for g in range(G):
                    c = C_[g]
                    dve.wait_ge(C_exp.sem, C_exp.at(i, g, r))
                    ch.link(nc.vector.reciprocal(small[:, g, 16:20], small[:, g, 12:16]))
                    nc.vector.tensor_tensor(c["p"], c["p"], small[:, g, 16:20].unsqueeze(2).broadcast_to([P, 4, P]),
                                            ALU.mult).then_inc(C_p.sem, 1)
                for g in range(G):
                    c = C_[g]
                    dve.wait_ge(C_o.sem, C_o.at(i, g, r))
                    smooth = inv[:, 8 + 4 * r:12 + 4 * r].unsqueeze(2).broadcast_to([P, 4, P])
                    ch.link(nc.vector.tensor_tensor(c["t"], bank(g, 1).rearrange("p (h d) -> p h d", h=4), smooth, ALU.mult))
                    ch.link(nc.vector.tensor_scalar(c["y"], c["t"], 448.0, -448.0, ALU.min, ALU.max))
                    to_fp8(ch, c["y"], c["m"], c["t"], c["cat"]).then_inc(C_cat.sem, 1)
            for g in range(G):
                dve.wait_ge(C_out.sem, C_out.at(i, g))
                add_to_x(dve, ch, i * G + g, bank(g, 3)[:, 0:D], out_scale[:])

        def C_gpsimd(pool, ch, i):
            norm_gpsimd(pool, ch, i)
            for g in range(G):
                pool.wait_ge(C_stats2.sem, C_stats2.at(i, g))
                ch.link(nc.gpsimd.tensor_tensor(rstd[:, g, :], moments[:, g, 1:2], eps5[:], ALU.add))
                nc.gpsimd.tensor_tensor(rstd[:, g, :], rstd[:, g, :], minus_half[:, 0:1], ALU.pow).then_inc(C_rstd2.sem, 1)

        def C_scalar(act, ch, i):
            for g in range(G):
                act.wait_ge(xnT_done.sem, xnT_done.at(i, g))
                for k in range(KC):
                    last = nc.scalar.activation(xT[:, k, g, :], bank(g, 0)[:, k * P:(k + 1) * P], ACT.Identity,
                                                scale=c_ln_w[:, k:k + 1], bias=c_ln_b[:, k:k + 1])
                last.then_inc(xT_ready.sem, 1)
            for r in range(ROUNDS):
                cross, half = r // 4, r % 2
                flat = lambda v: v.rearrange("p a b -> p (a b)")
                for g in range(G):
                    c = C_[g]
                    act.wait_ge(C_kvq.sem, C_kvq.at(i, g, r))
                    if half == 0:
                        nc.scalar.activation(flat(c["kn"]), bank(g, 0), ACT.Square)
                        nc.scalar.activation(flat(c["v"]), bank(g, 1), ACT.Copy, scale=scalar[:, 3:4] if not cross else 1.0)
                    nc.scalar.activation(flat(c["qn"]), bank(g, 2), ACT.Square).then_inc(C_sq.sem, 1)
                for g in range(G):
                    c = C_[g]
                    act.wait_ge(C_kqturned.sem, C_kqturned.at(i, g, r))
                    h = 4 * cross
                    if half == 0:
                        nc.scalar.activation(flat(c["kT"]), bank(g, 0), ACT.Identity, scale=c_head[:, h + 2:h + 3], bias=c_head[:, h + 3:h + 4])
                    nc.scalar.activation(flat(c["qT"]), bank(g, 1), ACT.Identity, scale=c_head[:, h:h + 1],
                                         bias=c_head[:, h + 1:h + 2]).then_inc(C_kqT.sem, 1)
                for g in range(G):
                    c = C_[g]
                    act.wait_ge(C_max.sem, C_max.at(i, g, r))
                    for h in range(4):
                        last = nc.scalar.activation(c["p"][:, h, :], bank(g, 2)[:, h * P:(h + 1) * P], ACT.Exp, scale=DC ** -0.5,
                                                    bias=small[:, g, 8 + h:9 + h], accum_out=small[:, g, 12 + h:13 + h])
                    last.then_inc(C_exp.sem, 1)
                for g in range(G):
                    c = C_[g]
                    act.wait_ge(C_pturned.sem, C_pturned.at(i, g, r))
                    nc.scalar.copy(flat(c["pT"]), bank(g, 0)).then_inc(C_pT.sem, 1)

        def C_tensor(pe, i):
            norm_tensor(pe, i)

            def project(dst, src, w, c0):
                for k in range(KC):
                    last = nc.tensor.matmul(dst, src(k), w[:, k, c0:c0 + 512], start=k == 0, stop=k == KC - 1)
                return last

            for r in range(ROUNDS):
                cross, quad, half = r // 4, (r // 2) % 2, r % 2
                for g in range(G):
                    c = C_[g]
                    if r == 0:
                        pe.wait_ge(C_xs.sem, C_xs.at(i, g))
                    if r == 4:
                        ctx_loaded(pe, i, g)
                    x_of = lambda n: (lambda k: c["xs"][:, n, k, :])
                    ctx_of = lambda k: ctxT[:, g, k, :]
                    if half == 0:
                        if r:
                            pe.wait_ge(C_cat.sem, C_cat.at(i, g, r - 1))
                        if not cross:
                            project(bank(g, 0), x_of(2), wC["k"], 512 * quad)
                            project(bank(g, 1), x_of(3), wC["v"], 512 * quad)
                        else:
                            project(bank(g, 0), ctx_of, wC["kvx"], 512 * quad)
                            last = project(bank(g, 1), ctx_of, wC["kvx"], 1024 + 512 * quad)
                            if quad:
                                last.then_inc(ctx_read[g], 1)
                    project(bank(g, 2), x_of(cross), wC["qx" if cross else "q"], 1024 * quad + 512 * half).then_inc(C_kvq.sem, 1)
                for g in range(G):
                    c = C_[g]
                    pe.wait_ge(C_kqn.sem, C_kqn.at(i, g, r))
                    if half == 0:
                        for h in range(4):
                            nc.tensor.transpose(bank(g, 0)[:, h * P:(h + 1) * P], c["kn"][:, h, :], ident[:])
                    if half:
                        pe.wait_ge(C_cat.sem, C_cat.at(i, g, r - 1))
                    for h in range(4):
                        last = nc.tensor.transpose(bank(g, 1)[:, h * P:(h + 1) * P], c["qn"][:, h, :], ident[:])
                    last.then_inc(C_kqturned.sem, 1)
                for g in range(G):
                    c = C_[g]
                    pe.wait_ge(C_kqT.sem, C_kqT.at(i, g, r))
                    for h in range(4):
                        last = nc.tensor.matmul(bank(g, 2)[:, h * P:(h + 1) * P], c["qT"][:, h, :], c["kT"][:, 2 * half + h // 2, :],
                                                start=True, stop=True)
                    last.then_inc(C_scores.sem, 1)
                for g in range(G):
                    c = C_[g]
                    pe.wait_ge(C_p.sem, C_p.at(i, g, r))
                    for h in range(4):
                        last = nc.tensor.transpose(bank(g, 0)[:, h * P:(h + 1) * P], c["p"][:, h, :], ident[:])
                    last.then_inc(C_pturned.sem, 1)
                for g in range(G):
                    c = C_[g]
                    pe.wait_ge(C_pT.sem, C_pT.at(i, g, r))
                    for h in range(2):
                        last = nc.tensor.matmul(bank(g, 1)[:, h * D:(h + 1) * D], c["v"][:, 2 * half + h, :],
                                                c["pT"][:, 2 * h:2 * h + 2, :].rearrange("p a b -> p (a b)"), start=True, stop=True)
                    last.then_inc(C_o.sem, 1)
                for g in range(G):
                    c = C_[g]
                    pe.wait_ge(C_cat.sem, C_cat.at(i, g, r))
                    for h in range(4):
                        last = nc.tensor.matmul(bank(g, 3)[:, 0:D], c["cat"][:, h, :], wC["proj"][:, 4 * r + h, :],
                                                start=r == 0 and h == 0, stop=r == ROUNDS - 1 and h == 3)
                    if r == ROUNDS - 1:
                        last.then_inc(C_out.sem, 1)

        SUB.append((ctx_sync, C_tensor, C_scalar, C_gpsimd, C_vector))

        HD_, DD = 16, 16
        n_ = 0
        wD = {}
        for name, a, w in (("q", KC, 512), ("k", KC, 512), ("v", KC, D), ("o", KC, D), ("a", KC, 16)):
            wD[name], n_ = view(early, n_, a, w)
            LOADS["3 attention"].append((wD[name], "D_" + name))
        wD["b"], n_ = view(early, n_, FF)
        LOADS["3 attention"].append((wD["b"][0:16, :], "D_b"))
        n_ = 0
        for name, a, w in (("in", KC, FF), ("up", KC, FF), ("down", FC, D)):
            wD[name], n_ = view(late, n_, a, w)
            LOADS[3].append((wD[name], "D_" + name))
        LATE_4 = n_
        D_col = sb("D_col", [P, 4])
        D_mask = sb("D_mask", [P, P])
        D_mask4 = sb("D_mask4", [P, 4, P], BF16)
        LOADS["3 attention"] += [(D_col[:], "D_col"), (D_mask[:], "D_mask")]
        eps6 = sb("eps6", [P, 1])
        x2T = sb("x2T", [P, KC, G, P])
        D_ = [{} for _ in range(G)]
        for g in range(G):
            w, n_ = work[:, g, :], 0
            D_[g]["p"], n_ = view(w, n_, 16, P)
            D_[g]["pT"], n_ = view(w, n_, 16, P)
            D_[g]["xb"], n_ = view(w, n_, D)
            D_[g]["v"], n_ = view(w, n_, D)
            D_[g]["o"], n_ = view(w, n_, D)
            D_[g]["qk"], n_ = view(w, n_, 4, D)
        n_ = 5888
        D_oT = sb("D_oT", [P, KC, G, P])
        D_aoT, _ = view(work[:, 0, :], 0, KC, G * P)
        D_mod, _ = view(work[:, 0, :], 512, D)
        D_prod, _ = view(work[:, 0, :], 768, D)
        D_silu, _ = view(work[:, 1, :], 0, FC, D)
        D_m, _ = view(work[:, 1, :], 2048, FC, D)
        D_ms = flag("D_ms")
        D_rstd2 = flag("D_rstd2")
        D_qkv = flag("D_qkv")
        D_qkvs = flag("D_qkvs")
        D_scores = flag("D_scores")
        D_max = flag("D_max")
        D_exp = flag("D_exp")
        D_pturned = flag("D_pturned")
        D_pT = flag("D_pT")
        D_pv = flag("D_pv")
        D_o = flag("D_o")
        D_oturned = flag("D_oturned")
        D_oTs = flag("D_oTs")
        D_ao = step_flag("D_ao")
        D_aos = step_flag("D_aos")
        D_ranks = step_flag("D_ranks")
        D_tanh = step_flag("D_tanh")
        D_prods = step_flag("D_prods")
        D_gate = step_flag("D_gate")
        D_silus = step_flag("D_silus")
        D_up = step_flag("D_up")
        D_ms_ready = step_flag("D_ms_ready")
        D_down = flag("D_down")
        D_prepared = sem("D_prepared")
        WEIGHT_USERS.update({(3, 4), (3, 2)})

        def D_before_vector(dve, ch):
            for n in range(4):
                last = nc.vector.tensor_copy(D_mask4[:, n, :], D_mask[:])
            ch.mark(last)
            nc.vector.memset(eps6[:], 1e-6).then_inc(D_prepared, 1)

        BEFORE[3, 4] = D_before_vector
        BEFORE[3, 1] = lambda pe, ch: pe.wait_ge(D_prepared, 1)
        BEFORE[3, 3] = lambda pool, ch: pool.wait_ge(D_prepared, 1)

        def D_vector(dve, ch, i):
            def again(g):
                nc.vector.tensor_tensor_reduce(D_[g]["xb"], xn[:, g, :], xn[:, g, :], 1.0 / D, 0.0, ALU.mult, ALU.add,
                                               moments[:, g, 1:2]).then_inc(D_ms.sem, 1)

            norm_vector(dve, ch, i, again)
            for g in range(G):
                dve.wait_ge(D_rstd2.sem, D_rstd2.at(i, g))
                nc.vector.tensor_scalar(D_[g]["xb"], xn[:, g, :], rstd[:, g, :], None, ALU.mult).then_inc(xn_ready.sem, 1)
            for g in range(G):
                dve.wait_ge(D_scores.sem, D_scores.at(i, g))
                mx = small[:, g, 0:16]
                s = PS[:, 4 * g:4 * g + 4, :].rearrange("p j (t k) -> p (j t) k", t=4)
                ch.link(nc.vector.tensor_reduce(mx, s, AX.X, ALU.max))
                nc.vector.tensor_scalar(mx, mx, -DD ** -0.5, None, ALU.mult).then_inc(D_max.sem, 1)
            for g in range(G):
                dve.wait_ge(D_pturned.sem, D_pturned.at(i, g))
                s = PS[:, 4 * g:4 * g + 4, :].rearrange("p j x -> p (j x)")
                nc.vector.tensor_copy(D_[g]["pT"].rearrange("p a b -> p (a b)"), s).then_inc(D_pT.sem, 1)
            for g in range(G):
                dve.wait_ge(D_pv.sem, D_pv.at(i, g))
                ch.link(nc.vector.reciprocal(small[:, g, 32:48], small[:, g, 16:32]))
                nc.vector.tensor_tensor(
                    D_[g]["o"].rearrange("p (t j d) -> p j t d", t=4, j=4),
                    bank(g, 0)[:, 0:D].rearrange("p (t j d) -> p j t d", t=4, j=4),
                    small[:, g, 32:48].rearrange("p (j t) -> p j t", j=4).unsqueeze(3).broadcast_to([P, 4, 4, DD]),
                    ALU.mult).then_inc(D_o.sem, 1)
            dve.wait_ge(D_tanh.sem, D_tanh.at(i))
            nc.vector.scalar_tensor_tensor(D_prod[0:16, :], D_mod[0:16, :], 0.1, bank(1, 2)[0:16, 0:D], ALU.mult, ALU.mult).then_inc(D_prods.sem, 1)
            dve.wait_ge(D_silus.sem, D_silus.at(i))
            dve.wait_ge(D_up.sem, D_up.at(i))
            nc.vector.tensor_tensor(D_m.rearrange("p a b -> p (a b)"), D_silu.rearrange("p a b -> p (a b)"),
                                    PS[:, 4:8, :].rearrange("p j x -> p (j x)"), ALU.mult).then_inc(D_ms_ready.sem, 1)
            for g in range(G):
                dve.wait_ge(D_down.sem, D_down.at(i, g))
                ch.link(nc.vector.tensor_tensor(D_[g]["o"], xn[:, g, :], bank(g, 0)[:, 0:D], ALU.add))
                add_to_x(dve, ch, i * G + g, D_[g]["o"], gates[:, 1, 1:2])

        def D_gpsimd(pool, ch, i):
            norm_gpsimd(pool, ch, i)
            for g in range(G):
                pool.wait_ge(D_ms.sem, D_ms.at(i, g))
                ch.link(nc.gpsimd.tensor_tensor(rstd[:, g, :], moments[:, g, 1:2], eps6[:], ALU.add))
                nc.gpsimd.tensor_tensor(rstd[:, g, :], rstd[:, g, :], minus_half[:, 0:1], ALU.pow).then_inc(D_rstd2.sem, 1)

        def D_scalar(act, ch, i):
            for g in range(G):
                act.wait_ge(xnT_done.sem, xnT_done.at(i, g))
                for m, dst in enumerate((xT, x2T)):
                    for k in range(KC):
                        last = nc.scalar.activation(dst[:, k, g, :], bank(g, 0)[:, k * P:(k + 1) * P], ACT.Copy,
                                                    scale=D_col[:, 2 * m + k:2 * m + k + 1])
                last.then_inc(xT_ready.sem, 1)
            for g in range(G):
                act.wait_ge(D_qkv.sem, D_qkv.at(i, g))
                nc.scalar.copy(D_[g]["v"], bank(g, 3)[:, 0:D])
                nc.scalar.copy(D_[g]["qk"].rearrange("p a b -> p (a b)"), banks(g, 1)).then_inc(D_qkvs.sem, 1)
            for g in range(G):
                act.wait_ge(D_max.sem, D_max.at(i, g))
                for n in range(16):
                    last = nc.scalar.activation(D_[g]["p"][:, n, :], bank(g, n // 4)[:, (n % 4) * P:(n % 4 + 1) * P], ACT.Exp,
                                                scale=DD ** -0.5, bias=small[:, g, n:n + 1], accum_out=small[:, g, 16 + n:17 + n])
                last.then_inc(D_exp.sem, 1)
            for g in range(G):
                act.wait_ge(D_oturned.sem, D_oturned.at(i, g))
                nc.scalar.copy(D_oT[:, :, g, :], bank(g, 1)[:, 0:D].rearrange("p (k t) -> p k t", k=KC)).then_inc(D_oTs.sem, 1)
            act.wait_ge(D_ao.sem, D_ao.at(i))
            nc.scalar.copy(D_aoT.rearrange("p a b -> p (a b)"), bank(0, 2)).then_inc(D_aos.sem, 1)
            act.wait_ge(D_ranks.sem, D_ranks.at(i))
            nc.scalar.activation(D_mod[0:16, :], bank(0, 3)[0:16, 0:D], ACT.Tanh).then_inc(D_tanh.sem, 1)
            act.wait_ge(D_gate.sem, D_gate.at(i))
            nc.scalar.activation(D_silu.rearrange("p a b -> p (a b)"), PS[:, 0:4, :].rearrange("p j x -> p (j x)"), ACT.Silu).then_inc(D_silus.sem, 1)

        def D_tensor(pe, i):
            for g in range(G):
                pe.wait_ge(xn_ready.sem, xn_ready.at(i, g))
                for k in range(KC):
                    last = nc.tensor.transpose(bank(g, 0)[:, k * P:(k + 1) * P], D_[g]["xb"][:, k * P:(k + 1) * P], ident[:])
                last.then_inc(xnT_done.sem, 1)
            pair = lambda src, k: src[:, k].rearrange("p g t -> p (g t)")
            for g in range(G):
                pe.wait_ge(xT_ready.sem, xT_ready.at(i, 1))
                for tt in range(4):
                    for k in range(KC):
                        nc.tensor.matmul(banks(g, 1)[:, tt * D:(tt + 1) * D], wD["qk"[g]][:, k, tt * P:(tt + 1) * P], pair(xT, k),
                                         start=k == 0, stop=k == KC - 1)
                for k in range(KC):
                    last = nc.tensor.matmul(bank(g, 3)[:, 0:D], xT[:, k, g, :], wD["v"][:, k, :], start=k == 0, stop=k == KC - 1)
                last.then_inc(D_qkv.sem, 1)
            for g in range(G):
                pe.wait_ge(D_qkvs.sem, D_qkvs.at(i, 1))
                for j in range(4):
                    nc.tensor.matmul(bank(g, j), ident_b[:], D_mask4[:].rearrange("p a b -> p (a b)"), start=True, stop=False)
                    rows_ = slice(32 * j, 32 * j + DD)
                    for tt in range(4):
                        last = nc.tensor.matmul(bank(g, j)[:, tt * P:(tt + 1) * P], D_[0]["qk"][rows_, tt, g * P:(g + 1) * P],
                                                D_[1]["qk"][rows_, tt, g * P:(g + 1) * P], start=False, stop=tt == 3)
                last.then_inc(D_scores.sem, 1)
            for g in range(G):
                pe.wait_ge(D_exp.sem, D_exp.at(i, g))
                for n in range(16):
                    last = nc.tensor.transpose(bank(g, n // 4)[:, (n % 4) * P:(n % 4 + 1) * P], D_[g]["p"][:, n, :], ident[:])
                last.then_inc(D_pturned.sem, 1)
            for g in range(G):
                pe.wait_ge(D_pT.sem, D_pT.at(i, g))
                for n in range(16):
                    h = 4 * (n % 4) + n // 4
                    last = nc.tensor.matmul(bank(g, 0)[:, h * DD:(h + 1) * DD], D_[g]["pT"][:, n, :], D_[g]["v"][:, h * DD:(h + 1) * DD],
                                            start=True, stop=True)
                last.then_inc(D_pv.sem, 1)
            for g in range(G):
                pe.wait_ge(D_o.sem, D_o.at(i, g))
                for k in range(KC):
                    last = nc.tensor.transpose(bank(g, 1)[:, k * P:(k + 1) * P], D_[g]["o"][:, k * P:(k + 1) * P], ident[:])
                last.then_inc(D_oturned.sem, 1)
            pe.wait_ge(D_oTs.sem, D_oTs.at(i, 1))
            for m in range(KC):
                for k in range(KC):
                    last = nc.tensor.matmul(bank(0, 2)[:, m * D:(m + 1) * D], wD["o"][:, k, m * P:(m + 1) * P], pair(D_oT, k),
                                            start=k == 0, stop=k == KC - 1)
            last.then_inc(D_ao.sem, 1)
            for k in range(KC):
                nc.tensor.matmul(bank(1, 2)[0:16, 0:D], wD["a"][:, k, :], pair(x2T, k), start=k == 0, stop=k == KC - 1)
            pe.wait_ge(D_aos.sem, D_aos.at(i))
            for k in range(KC):
                last = nc.tensor.matmul(bank(0, 3)[0:16, 0:D], wD["a"][:, k, :], D_aoT[:, k, :], start=k == 0, stop=k == KC - 1)
            last.then_inc(D_ranks.sem, 1)
            pe.wait_ge(D_prods.sem, D_prods.at(i))
            for f in range(FC):
                dst = bank(0, f // 2)[:, (f % 2) * D:(f % 2 + 1) * D]
                for k in range(KC):
                    nc.tensor.matmul(dst, wD["in"][:, k, f * P:(f + 1) * P], pair(x2T, k), start=k == 0, stop=False)
                last = nc.tensor.matmul(dst, wD["b"][0:16, f * P:(f + 1) * P], D_prod[0:16, :], start=False, stop=True)
            last.then_inc(D_gate.sem, 1)
            for f in range(FC):
                dst = bank(1, f // 2)[:, (f % 2) * D:(f % 2 + 1) * D]
                for k in range(KC):
                    last = nc.tensor.matmul(dst, wD["up"][:, k, f * P:(f + 1) * P], pair(x2T, k), start=k == 0, stop=k == KC - 1)
            last.then_inc(D_up.sem, 1)
            pe.wait_ge(D_ms_ready.sem, D_ms_ready.at(i))
            for g in range(G):
                for f in range(FC):
                    last = nc.tensor.matmul(bank(g, 0)[:, 0:D], D_m[:, f, g * P:(g + 1) * P], wD["down"][:, f, :],
                                            start=f == 0, stop=f == FC - 1)
                last.then_inc(D_down.sem, 1)

        SUB.append((None, D_tensor, D_scalar, D_gpsimd, D_vector))

        HE, DE, TE = 16, 16, 8
        ROWS = 64
        n_ = LATE_4
        wE = {}
        for name, a, w in (("q", KC, D), ("kv", KC, 2 * D), ("p", KC, D)):
            wE[name], n_ = view(late, n_, a, w)
            LOADS[4].append((wE[name], "E_" + name))
        E_bias, n_ = view(late, n_, 4 * D)
        LOADS[4].append((E_bias, "E_bias"))
        LATE_5 = n_
        E_kT, _ = view(early, 0, TE, NB * P, dt=BF16)
        E_vs = sb("E_vs", [P, 2, D])
        E_v, _ = view(work[:, 0, :], 4096, NB, D)
        E_vq, _ = view(work[:, 1, :], 5120, NB, D, dt=BF16)
        E_ = [{} for _ in range(G)]
        for g in range(G):
            w, n_ = work[:, g, :], 0
            E_[g]["stack"], n_ = view(w, n_, HE, 4, DE, dt=BF16)
            E_[g]["qT"], n_ = view(w, n_, TE, P, dt=BF16)
            E_[g]["t"], n_ = view(w, n_, D)
            E_[g]["u"], n_ = view(w, n_, D)
            E_[g]["e"], n_ = view(w, n_, 1024)
            E_[g]["pb"], n_ = view(w, n_, 1024, dt=BF16)
            E_[g]["pT"], n_ = view(w, n_, NB, P, dt=BF16)
            E_[g]["oT"], n_ = view(w, n_, KC, P)
        assert n_ <= 4096
        E_kv = flag("E_kv")
        E_kstack = flag("E_kstack")
        E_kturned = flag("E_kturned")
        E_kTs = flag("E_kTs")
        E_vmax = sem("E_vmax")
        E_vall = sem("E_vall")
        E_prepared = sem("E_prepared")
        E_q = flag("E_q")
        E_qstack = flag("E_qstack")
        E_qturned = flag("E_qturned")
        E_qTs = flag("E_qTs")
        E_scores = flag("E_scores", HE)
        E_max = flag("E_max", HE)
        E_exp = flag("E_exp", HE)
        E_pb = flag("E_pb", HE)
        E_pturned = flag("E_pturned", HE)
        E_pT = flag("E_pT", HE)
        E_pv = flag("E_pv", HE)
        E_o = flag("E_o")
        E_oturned = flag("E_oturned")
        E_oTs = flag("E_oTs")
        E_out = flag("E_out")
        WEIGHT_USERS.add((4, 4))
        heads16 = lambda v: v.rearrange("p (h d) -> p h d", h=16)
        over_d = lambda v: v.unsqueeze(2).broadcast_to([P, HE, DE])

        def E_before_sync(sp):
            with sp.Fori(0, STEPS) as i:
                ctx_sync(sp, i)
            ctx_base[0] += STEPS

        def E_before_tensor(pe, ch):
            pe.wait_ge(x_done.sem, 4 * NB)
            with pe.Fori(0, STEPS) as i:
                for g in range(G):
                    ctx_loaded(pe, i, g)
                    for k in range(KC):
                        last = nc.tensor.matmul(bank(g, 0), ctxT[:, g, k, :], wE["kv"][:, k, :], start=k == 0, stop=k == KC - 1)
                    last.then_inc(E_kv.sem, 1)
                for g in range(G):
                    pe.wait_ge(E_kstack.sem, E_kstack.at(i, g))
                    for tt in range(TE):
                        last = nc.tensor.transpose(bank(g, 1).bitcast(BF16)[:, tt * P:(tt + 1) * P],
                                                   E_[g]["stack"][:, 2 * tt:2 * tt + 2].rearrange("p a b c -> p (a b c)"), ident_b[:])
                        if tt == 0:
                            last.then_inc(ctx_read[g], 1)
                    last.then_inc(E_kturned.sem, 1)
            pe.wait_ge(E_prepared, 1)

        def E_before_scalar(act, ch):
            with act.Fori(0, STEPS) as i:
                for g in range(G):
                    b = i * G + g
                    act.wait_ge(E_kturned.sem, E_kturned.at(i, g))
                    nc.scalar.copy(E_kT.rearrange("p t (b k) -> p t b k", b=NB)[:, :, b, :],
                                   bank(g, 1).bitcast(BF16).rearrange("p (t k) -> p t k", t=TE)).then_inc(E_kTs.sem, 1)

        def step_of(ch, x, s, r):
            ch.link(nc.vector.tensor_reduce(s, heads16(x), AX.X, ALU.max, apply_absolute_value=True))
            ch.link(nc.vector.tensor_scalar(s, s, 1.0 / 127, 1e-8, ALU.mult, ALU.max))
            ch.link(nc.vector.reciprocal(r, s))

        def E_before_vector(dve, ch):
            for g in range(G):
                ch.mark(nc.vector.memset(E_[g]["stack"].rearrange("p a b c -> p (a b c)"), 0.0))
            ch.restart()
            with dve.Fori(0, STEPS) as i:
                for g in range(G):
                    b = i * G + g
                    e = E_[g]
                    dve.wait_ge(E_kv.sem, E_kv.at(i, g))
                    nc.vector.tensor_tensor(E_v[:, b, :], bank(g, 0)[:, D:2 * D], E_bias[:, 2 * D:3 * D], ALU.add)
                    ch.link(nc.vector.tensor_tensor(e["t"], bank(g, 0)[:, 0:D], E_bias[:, D:2 * D], ALU.add))
                    s, r = small[:, g, 0:16], small[:, g, 16:32]
                    step_of(ch, e["t"], s, r)
                    ch.link(nc.vector.tensor_tensor(heads16(e["t"]), heads16(e["t"]), over_d(r), ALU.mult))
                    ch.link(nc.vector.tensor_scalar(e["t"], e["t"], MAGIC, MAGIC, ALU.add, ALU.subtract))
                    ch.link(nc.vector.tensor_tensor(heads16(e["t"]), heads16(e["t"]), over_d(s), ALU.mult))
                    ch.link(nc.vector.tensor_copy(e["stack"][:, :, 0, :], heads16(e["t"])))
                    ch.link(nc.vector.tensor_tensor(heads16(e["u"]), heads16(e["t"]), e["stack"][:, :, 0, :], ALU.subtract))
                    ch.link(nc.vector.tensor_copy(e["stack"][:, :, 1, :], heads16(e["u"])))
                    nc.vector.tensor_tensor(e["stack"][:, :, 2, :], heads16(e["u"]), e["stack"][:, :, 1, :], ALU.subtract).then_inc(E_kstack.sem, 1)
                for g in range(G):
                    dve.wait_ge(E_kTs.sem, E_kTs.at(i, g))
                    ch.link(nc.vector.memset(E_[g]["stack"][:, 0, 3, :], 0.0))
                ch.restart()
            vm = E_vs[:, 1, :]
            nc.vector.tensor_reduce(vm, E_v.rearrange("p b d -> p d b"), AX.X, ALU.max, apply_absolute_value=True).then_inc(E_vmax, 1)
            dve.wait_ge(E_vall, 1)
            ch.link(nc.vector.tensor_scalar(E_vs[:, 0, :], E_vs[:, 0, :], 1.0 / 127, 1e-8, ALU.mult, ALU.max))
            ch.link(nc.vector.reciprocal(E_vs[:, 1, :], E_vs[:, 0, :]))
            ch.link(nc.vector.tensor_tensor(E_v, E_v, E_vs[:, 1, :].unsqueeze(1).broadcast_to([P, NB, D]), ALU.mult))
            nc.vector.tensor_scalar(E_vq, E_v, MAGIC, MAGIC, ALU.add, ALU.subtract).then_inc(E_prepared, 1)

        def E_before_gpsimd(pool, ch):
            pool.wait_ge(E_vmax, 1)
            nc.gpsimd.partition_all_reduce(E_vs[:, 0, :], E_vs[:, 1, :], P, bass.bass_isa.ReduceOp.max).then_inc(E_vall, 1)

        BEFORE.update({(4, 0): E_before_sync, (4, 1): E_before_tensor, (4, 2): E_before_scalar, (4, 3): E_before_gpsimd, (4, 4): E_before_vector})

        def E_tensor(pe, i):
            norm_tensor(pe, i)
            for g in range(G):
                pe.wait_ge(xT_ready.sem, xT_ready.at(i, g))
                for k in range(KC):
                    last = nc.tensor.matmul(bank(g, 1)[:, 0:D], xT[:, k, g, :], wE["q"][:, k, :], start=k == 0, stop=k == KC - 1)
                last.then_inc(E_q.sem, 1)
            for g in range(G):
                pe.wait_ge(E_qstack.sem, E_qstack.at(i, g))
                for tt in range(TE):
                    last = nc.tensor.transpose(bank(g, 0).bitcast(BF16)[:, tt * P:(tt + 1) * P],
                                               E_[g]["stack"][:, 2 * tt:2 * tt + 2].rearrange("p a b c -> p (a b c)"), ident_b[:])
                last.then_inc(E_qturned.sem, 1)

            def scores(u):
                h, g = divmod(u, G)
                if h == 0:
                    pe.wait_ge(E_qTs.sem, E_qTs.at(i, g))
                else:
                    pe.wait_ge(E_exp.sem, E_exp.nth(i, u - G))
                r = slice(ROWS * (h % 2), ROWS * (h % 2) + ROWS)
                for n in range(2):
                    last = nc.tensor.matmul(bank(g, 2 + n), E_[g]["qT"][r, h // 2, :], E_kT[r, h // 2, n * 512:(n + 1) * 512],
                                            start=True, stop=True)
                last.then_inc(E_scores.sem, 1)

            def turn(u):
                g = u % G
                pe.wait_ge(E_pb.sem, E_pb.nth(i, u))
                if u >= G:
                    pe.wait_ge(E_pT.sem, E_pT.nth(i, u - G))
                for b in range(NB):
                    last = nc.tensor.transpose(bank(g, 1).bitcast(BF16)[:, b * P:(b + 1) * P], E_[g]["pb"][:, b * P:(b + 1) * P], ident_b[:])
                last.then_inc(E_pturned.sem, 1)

            def weigh(u):
                h, g = divmod(u, G)
                pe.wait_ge(E_pT.sem, E_pT.nth(i, u))
                for b in range(NB):
                    last = nc.tensor.matmul(bank(g, 0)[:, h * DE:(h + 1) * DE], E_[g]["pT"][:, b, :], E_vq[:, b, h * DE:(h + 1) * DE],
                                            start=b == 0, stop=b == NB - 1)
                last.then_inc(E_pv.sem, 1)

            U = HE * G
            for u in range(G):
                scores(u)
            for u in range(U):
                if u + G < U:
                    scores(u + G)
                turn(u)
                if u >= 1:
                    weigh(u - 1)
            weigh(U - 1)
            for g in range(G):
                pe.wait_ge(E_o.sem, E_o.at(i, g))
                for k in range(KC):
                    last = nc.tensor.transpose(bank(g, 1)[:, k * P:(k + 1) * P], E_[g]["t"][:, k * P:(k + 1) * P], ident[:])
                last.then_inc(E_oturned.sem, 1)
            for g in range(G):
                pe.wait_ge(E_oTs.sem, E_oTs.at(i, g))
                for k in range(KC):
                    last = nc.tensor.matmul(bank(g, 2)[:, 0:D], E_[g]["oT"][:, k, :], wE["p"][:, k, :], start=k == 0, stop=k == KC - 1)
                last.then_inc(E_out.sem, 1)

        def E_scalar(act, ch, i):
            norm_scalar(act, i)
            for g in range(G):
                act.wait_ge(E_qturned.sem, E_qturned.at(i, g))
                nc.scalar.copy(E_[g]["qT"].rearrange("p a b -> p (a b)"), bank(g, 0).bitcast(BF16)).then_inc(E_qTs.sem, 1)

            def turn(u):
                g = u % G
                act.wait_ge(E_pturned.sem, E_pturned.nth(i, u))
                if u >= G:
                    act.wait_ge(E_pv.sem, E_pv.nth(i, u - G))
                nc.scalar.copy(E_[g]["pT"].rearrange("p a b -> p (a b)"), bank(g, 1).bitcast(BF16)).then_inc(E_pT.sem, 1)

            for u in range(HE * G):
                h, g = divmod(u, G)
                act.wait_ge(E_max.sem, E_max.nth(i, u))
                if u >= G:
                    act.wait_ge(E_pb.sem, E_pb.nth(i, u - G))
                nc.scalar.activation(E_[g]["e"], banks(g, 2), ACT.Exp, scale=small[:, g, h:h + 1],
                                     bias=small[:, g, 48 + h:49 + h], accum_out=small[:, g, 64 + h:65 + h]).then_inc(E_exp.sem, 1)
                if u >= 1:
                    turn(u - 1)
            turn(HE * G - 1)
            for g in range(G):
                act.wait_ge(E_oturned.sem, E_oturned.at(i, g))
                nc.scalar.copy(E_[g]["oT"].rearrange("p a b -> p (a b)"), bank(g, 1)[:, 0:D]).then_inc(E_oTs.sem, 1)

        def E_vector(dve, ch, i):
            norm_vector(dve, ch, i)
            for g in range(G):
                e = E_[g]
                dve.wait_ge(E_q.sem, E_q.at(i, g))
                ch.link(nc.vector.tensor_tensor(e["t"], bank(g, 1)[:, 0:D], E_bias[:, 0:D], ALU.add))
                ch.link(nc.vector.tensor_scalar(e["t"], e["t"], DE ** -0.5, None, ALU.mult))
                s, r = small[:, g, 0:16], small[:, g, 16:32]
                step_of(ch, e["t"], s, r)
                ch.link(nc.vector.tensor_scalar(small[:, g, 32:48], s, -1.0, None, ALU.mult))
                ch.link(nc.vector.tensor_tensor(heads16(e["u"]), heads16(e["t"]), over_d(r), ALU.mult))
                for part in range(3):
                    last = nc.vector.tensor_scalar(e["stack"][:, :, part, :], heads16(e["u"]), MAGIC, MAGIC, ALU.add, ALU.subtract)
                last.then_inc(E_qstack.sem, 1)

            def maximum(h, g):
                dve.wait_ge(E_scores.sem, E_scores.at(i, g, h))
                ch.link(nc.vector.tensor_reduce(small[:, g, 80:81], banks(g, 2), AX.X, ALU.max))
                nc.vector.tensor_scalar(small[:, g, 48 + h:49 + h], small[:, g, 80:81], small[:, g, 32 + h:33 + h],
                                        5.541263545158426, ALU.mult, ALU.add).then_inc(E_max.sem, 1)

            for u in range(G):
                maximum(0, u)
            for u in range(HE * G):
                h, g = divmod(u, G)
                dve.wait_ge(E_exp.sem, E_exp.nth(i, u))
                if u >= G:
                    dve.wait_ge(E_pturned.sem, E_pturned.nth(i, u - G))
                nc.vector.tensor_scalar(E_[g]["pb"], E_[g]["e"], MAGIC, MAGIC, ALU.add, ALU.subtract).then_inc(E_pb.sem, 1)
                if h + 1 < HE:
                    maximum(h + 1, g)
            for g in range(G):
                e = E_[g]
                dve.wait_ge(E_pv.sem, E_pv.at(i, g, HE - 1))
                ch.link(nc.vector.reciprocal(small[:, g, 16:32], small[:, g, 64:80]))
                ch.link(nc.vector.tensor_tensor(heads16(e["t"]), heads16(bank(g, 0)[:, 0:D]), over_d(small[:, g, 16:32]), ALU.mult))
                nc.vector.tensor_tensor(e["t"], e["t"], E_vs[:, 0, :], ALU.mult).then_inc(E_o.sem, 1)
            for g in range(G):
                dve.wait_ge(E_out.sem, E_out.at(i, g))
                ch.link(nc.vector.tensor_tensor(E_[g]["u"], bank(g, 2)[:, 0:D], E_bias[:, 3 * D:4 * D], ALU.add))
                add_to_x(dve, ch, i * G + g, E_[g]["u"], gates[:, 0, 2:3])

        SUB.append((None, E_tensor, E_scalar, B_gpsimd, E_vector))

        NE = 8
        n_ = LATE_5
        wF = {}
        for name, a, w in (("gate", KC, NE), ("w1", KC, NE * P), ("w2", NE, D), ("sw1", KC, D), ("sw2", KC, D)):
            wF[name], n_ = view(late, n_, a, w)
            LOADS[5].append((wF[name], "F_" + name))
        wF["b2"], n_ = view(late, n_, D)
        wF["sb2"], n_ = view(late, n_, D)
        LOADS[5] += [(wF["b2"][0:NE, :], "F_b2"), (wF["sb2"][0:1, :], "F_sb2")]
        LATE_6 = n_
        F_col = sb("F_col", [P, 10])
        LOADS[5].append((F_col[:], "F_col"))
        F_h, _ = view(work[:, 0, :], 0, 10, D)
        F_ = [{} for _ in range(G)]
        for g in range(G):
            w, n_ = work[:, g, :], 2560
            F_[g]["acc"], n_ = view(w, n_, D)
            F_[g]["gT"], n_ = view(w, n_, P)
        F_logits = flag("F_logits")
        F_diff = flag("F_diff")
        F_ratio = flag("F_ratio")
        F_gates = flag("F_gates")
        F_gturned = flag("F_gturned")
        F_gTs = flag("F_gTs")
        F_hidden = step_flag("F_hidden", 5)
        F_hs = step_flag("F_hs", 5)
        F_shared = flag("F_shared")
        F_expert = flag("F_expert", 4)
        F_added = flag("F_added", 4)
        BIG = 3.0e38
        WEIGHT_USERS.add((5, 2))

        def F_vector(dve, ch, i):
            norm_vector(dve, ch, i)
            lo = [small[:, g, 0:8] for g in range(G)]
            top = [small[:, g, 8:16] for g in range(G)]
            look = [small[:, g, 16:32] for g in range(G)]
            rest = [small[:, g, 32:48] for g in range(G)]
            one = [small[:, g, 48:56] for g in range(G)]
            for g in range(G):
                dve.wait_ge(F_logits.sem, F_logits.at(i, g))
                nc.vector.memset(look[g], -BIG)
                ch.link(nc.vector.tensor_copy(lo[g], bank(g, 1)[:, 0:NE]))
                ch.link(nc.vector.max(top[g], lo[g]))
                for n in range(2):
                    last = nc.vector.tensor_copy(look[g][:, 8 * n:8 * n + 1], top[g][:, n:n + 1])
                ch.link(last)
                last = nc.vector.tensor_tensor(small[:, g, 56:57], top[g][:, 1:2], top[g][:, 0:1], ALU.subtract)
                last.then_inc(F_diff.sem, 1)
                ch.link(nc.vector.match_replace(rest[g][:, 0:8], look[g][:, 0:8], lo[g], BIG))
                ch.link(nc.vector.match_replace(rest[g][:, 8:16], look[g][:, 8:16], rest[g][:, 0:8], BIG))
            for g in range(G):
                dve.wait_ge(F_ratio.sem, F_ratio.at(i, g))
                e, s = small[:, g, 57:58], small[:, g, 58:59]
                ch.link(nc.vector.tensor_scalar(s, e, 1.0, None, ALU.add))
                ch.link(nc.vector.reciprocal(s, s))
                ch.link(nc.vector.tensor_tensor(small[:, g, 59:60], e, s, ALU.mult))
                ch.link(nc.vector.tensor_single_scalar(one[g], rest[g][:, 0:8], BIG, ALU.is_equal))
                ch.link(nc.vector.tensor_single_scalar(lo[g], rest[g][:, 8:16], BIG, ALU.is_equal))
                ch.link(nc.vector.tensor_tensor(lo[g], lo[g], one[g], ALU.subtract))
                ch.link(nc.vector.tensor_scalar(lo[g], lo[g], small[:, g, 59:60], None, ALU.mult))
                nc.vector.scalar_tensor_tensor(lo[g], one[g], s, lo[g], ALU.mult, ALU.add).then_inc(F_gates.sem, 1)
            for g in range(G):
                dve.wait_ge(F_shared.sem, F_shared.at(i, g))
                ch.link(nc.vector.tensor_copy(F_[g]["acc"], bank(g, 0)[:, 0:D]))
            for n in range(4):
                for g in range(G):
                    acc = F_[g]["acc"]
                    dve.wait_ge(F_expert.sem, F_expert.at(i, g, n))
                    for m in range(2):
                        last = nc.vector.scalar_tensor_tensor(acc, bank(g, 2 + n % 2)[:, m * D:(m + 1) * D], lo[g][:, 2 * n + m:2 * n + m + 1],
                                                              acc, ALU.mult, ALU.add)
                        if m == 0:
                            ch.link(last)
                    last.then_inc(F_added.sem, 1)
                    dve.wait_ge(F_added.sem, F_added.at(i, g, n))
            for g in range(G):
                add_to_x(dve, ch, i * G + g, F_[g]["acc"], gates[:, 1, 2:3])

        def F_scalar(act, ch, i):
            norm_scalar(act, i)
            for g in range(G):
                act.wait_ge(F_diff.sem, F_diff.at(i, g))
                nc.scalar.activation(small[:, g, 57:58], small[:, g, 56:57], ACT.Exp).then_inc(F_ratio.sem, 1)
            for n in range(5):
                act.wait_ge(F_hidden.sem, F_hidden.at(i, n))
                for m in range(2):
                    last = nc.scalar.activation(F_h[:, 2 * n + m, :], HIDDEN[n % 4][:, m * D:(m + 1) * D], ACT.Gelu,
                                                bias=F_col[:, 2 * n + m:2 * n + m + 1])
                last.then_inc(F_hs.sem, 1)
            for g in range(G):
                act.wait_ge(F_gturned.sem, F_gturned.at(i, g))
                nc.scalar.copy(F_[g]["gT"][0:NE, :], bank(g, 1)[0:NE, 0:P]).then_inc(F_gTs.sem, 1)

        HIDDEN = [bank(0, 2), bank(0, 3), bank(1, 2), bank(1, 3)]

        def F_tensor(pe, i):
            norm_tensor(pe, i)
            for g in range(G):
                pe.wait_ge(xT_ready.sem, xT_ready.at(i, g))
                for k in range(KC):
                    last = nc.tensor.matmul(bank(g, 1)[:, 0:NE], xT[:, k, g, :], wF["gate"][:, k, :], start=k == 0, stop=k == KC - 1)
                last.then_inc(F_logits.sem, 1)
            for n in range(5):
                if n == 4:
                    pe.wait_ge(F_hs.sem, F_hs.at(i, 0))
                for m in range(2):
                    e = 2 * n + m
                    w = wF["w1"][:, :, e * P:(e + 1) * P] if n < 4 else wF["sw1"][:, :, m * P:(m + 1) * P]
                    for k in range(KC):
                        last = nc.tensor.matmul(HIDDEN[n % 4][:, m * D:(m + 1) * D], w[:, k, :], xT[:, k].rearrange("p g t -> p (g t)"),
                                                start=k == 0, stop=k == KC - 1)
                last.then_inc(F_hidden.sem, 1)
            for g in range(G):
                pe.wait_ge(F_gates.sem, F_gates.at(i, g))
                nc.tensor.transpose(bank(g, 1)[0:NE, 0:P], small[:, g, 0:8], ident[:]).then_inc(F_gturned.sem, 1)
            pe.wait_ge(F_hs.sem, F_hs.at(i, 4))
            for g in range(G):
                pe.wait_ge(F_gTs.sem, F_gTs.at(i, g))
                out_ = bank(g, 0)[:, 0:D]
                for m in range(2):
                    nc.tensor.matmul(out_, F_h[:, 8 + m, g * P:(g + 1) * P], wF["sw2"][:, m, :], start=m == 0, stop=False)
                nc.tensor.matmul(out_, ones[0:1, :], wF["sb2"][0:1, :], start=False, stop=False)
                nc.tensor.matmul(out_, F_[g]["gT"][0:NE, :], wF["b2"][0:NE, :], start=False, stop=True).then_inc(F_shared.sem, 1)
            for n in range(4):
                for g in range(G):
                    if n >= 2:
                        pe.wait_ge(F_added.sem, F_added.at(i, g, n - 2))
                    for m in range(2):
                        e = 2 * n + m
                        last = nc.tensor.matmul(bank(g, 2 + n % 2)[:, m * D:(m + 1) * D], F_h[:, e, g * P:(g + 1) * P], wF["w2"][:, e, :],
                                                start=True, stop=True)
                    last.then_inc(F_expert.sem, 1)

        SUB.append((None, F_tensor, F_scalar, B_gpsimd, F_vector))

        LATE_7 = LATE_6
        G_mask8 = sb("G_mask8", [P, NB * P], U8)
        G_on, n_ = view(work[:, 0, :], 4096, NB, P)
        G_off, n_ = view(work[:, 0, :], n_, NB, P)
        LOADS[6].append((G_mask8[:], "G_mask"))
        G_valid = sb("G_valid", [P, NB])
        G_ = [{} for _ in range(G)]
        for g in range(G):
            w, n_ = work[:, g, :], 0
            G_[g]["v"], n_ = view(w, n_, D)
            G_[g]["s"], n_ = view(w, n_, P)
            G_[g]["p"], n_ = view(w, n_, P)
            G_[g]["pT"], n_ = view(w, n_, P)
        v_in = [sem(f"v_in{g}") for g in range(G)]
        G_scores = flag("G_scores")
        G_max = flag("G_max")
        G_exp = flag("G_exp")
        G_pturned = flag("G_pturned")
        G_pT = flag("G_pT")
        G_o = flag("G_o")
        WEIGHT_USERS.add((6, 4))

        def G_before_vector(dve, ch):
            flat = lambda v: v.rearrange("p a b -> p (a b)")
            ch.link(nc.vector.tensor_copy(flat(G_on), G_mask8[:]))
            ch.mark(nc.vector.tensor_scalar(flat(G_off), flat(G_on), 1.0, -NEG, ALU.subtract, ALU.mult))
            ch.mark(nc.vector.tensor_reduce(G_valid[:], G_on, AX.X, ALU.max))

        BEFORE[6, 4] = G_before_vector

        def G_sync(sp, i):
            sp.wait_ge(x_done.sem, i * G + 6 * NB)
            for g in range(G):
                b = i * G + g
                sp.dma_start(ctxT[:, g], t["ctxT"][:, :, b, :]).then_inc(ctx_in[g], 16)
                sp.dma_start(G_[g]["v"], t["ctx"][:, b, :]).then_inc(v_in[g], 16)

        def G_vector(dve, ch, i):
            norm_vector(dve, ch, i)
            for g in range(G):
                b = i * G + g
                dve.wait_ge(G_scores.sem, G_scores.at(i, g))
                s, mx = G_[g]["s"], small[:, g, 0:1]
                ch.link(nc.vector.scalar_tensor_tensor(s, bank(g, 1)[:, 0:P], 1.0 / 16, G_on[:, b, :], ALU.mult, ALU.mult))
                ch.link(nc.vector.tensor_tensor(s, s, G_off[:, b, :], ALU.add))
                nc.vector.tensor_reduce(mx, s, AX.X, ALU.max, negate=True).then_inc(G_max.sem, 1)
            for g in range(G):
                b = i * G + g
                dve.wait_ge(G_exp.sem, G_exp.at(i, g))
                r = small[:, g, 2:3]
                ch.link(nc.vector.reciprocal(r, small[:, g, 1:2]))
                ch.link(nc.vector.tensor_scalar(r, r, gates[:, 0, 3:4], None, ALU.mult))
                ch.link(nc.vector.tensor_tensor(r, r, G_valid[:, bass.ds(b, 1)], ALU.mult))
            for g in range(G):
                dve.wait_ge(G_o.sem, G_o.at(i, g))
                add_to_x(dve, ch, i * G + g, bank(g, 2)[:, 0:D], small[:, g, 2:3])

        def G_scalar(act, ch, i):
            norm_scalar(act, i)
            for g in range(G):
                act.wait_ge(G_max.sem, G_max.at(i, g))
                nc.scalar.activation(G_[g]["p"], G_[g]["s"], ACT.Exp, bias=small[:, g, 0:1], accum_out=small[:, g, 1:2]).then_inc(G_exp.sem, 1)
            for g in range(G):
                act.wait_ge(G_pturned.sem, G_pturned.at(i, g))
                nc.scalar.copy(G_[g]["pT"], bank(g, 1)[:, 0:P]).then_inc(G_pT.sem, 1)

        def G_tensor(pe, i):
            norm_tensor(pe, i)
            for g in range(G):
                ctx_loaded(pe, i, g)
                pe.wait_ge(v_in[g], i * 16 + 16)
                pe.wait_ge(xT_ready.sem, xT_ready.at(i, g))
                for k in range(KC):
                    last = nc.tensor.matmul(bank(g, 1)[:, 0:P], xT[:, k, g, :], ctxT[:, g, k, :], start=k == 0, stop=k == KC - 1)
                last.then_inc(G_scores.sem, 1)
            for g in range(G):
                pe.wait_ge(G_exp.sem, G_exp.at(i, g))
                nc.tensor.transpose(bank(g, 1)[:, 0:P], G_[g]["p"], ident[:]).then_inc(G_pturned.sem, 1)
            for g in range(G):
                pe.wait_ge(G_pT.sem, G_pT.at(i, g))
                nc.tensor.matmul(bank(g, 2)[:, 0:D], G_[g]["pT"], G_[g]["v"], start=True, stop=True).then_inc(G_o.sem, 1)

        SUB.append((G_sync, G_tensor, G_scalar, B_gpsimd, G_vector))

        n_ = LATE_7
        wH = {}
        for name, a, w in (("up", KC, FF), ("gate", KC, FF), ("down", FC, D)):
            wH[name], n_ = view(late, n_, a, w)
            LOADS[7].append((wH[name], "H_" + name))
        H_row, n_ = view(late, n_, D)
        LOADS[7].append((H_row, "H_row"))
        assert n_ <= 24576
        H_col = sb("H_col", [P, 26])
        LOADS[7].append((H_col[:], "H_col"))
        H_up = sb("H_up", [P, FC])
        H_gate = sb("H_gate", [P, FC])
        H_rT, _ = view(work[:, 0, :], 0, KC, D)
        H_silu, _ = view(work[:, 0, :], 512, FC, D)
        H_h, _ = view(work[:, 0, :], 2560, FC, D)
        H_h2, _ = view(work[:, 1, :], 0, FC, D)
        H_yT, _ = view(work[:, 1, :], 2048, FC, D)
        H_t = [view(work[:, g, :], 4608, D)[0] for g in range(G)]
        H_rot = step_flag("H_rot")
        H_rTs = step_flag("H_rTs")
        H_gates = step_flag("H_gates")
        H_ups = step_flag("H_ups")
        H_silus = step_flag("H_silus")
        H_hs = step_flag("H_hs")
        H_turned = step_flag("H_turned")
        H_yTs = step_flag("H_yTs")
        H_down = flag("H_down")
        WEIGHT_USERS.update({(7, 4), (7, 2)})
        H_prepared = sem("H_prepared")

        def H_before_vector(dve, ch):
            ch.link(nc.vector.tensor_scalar(H_up[:], H_col[:, 10:18], 64.0, None, ALU.mult))
            ch.mark(nc.vector.tensor_tensor(H_up[:], H_up[:], H_col[:, 2:10], ALU.mult))
            ch.mark(nc.vector.tensor_scalar(H_gate[:], H_col[:, 18:26], 64.0, None, ALU.mult))
            nc.vector.tensor_scalar(H_row, H_row, 64.0, None, ALU.mult).then_inc(H_prepared, 1)

        BEFORE[7, 4] = H_before_vector
        BEFORE[7, 2] = lambda act, ch: act.wait_ge(H_prepared, 1)
        BEFORE[7, 1] = lambda pe, ch: pe.wait_ge(H_prepared, 1)
        all4 = lambda g: PS[:, 4 * g:4 * g + 4, :].rearrange("p j x -> p (j x)")

        def H_vector(dve, ch, i):
            norm_vector(dve, ch, i)
            dve.wait_ge(H_silus.sem, H_silus.at(i))
            dve.wait_ge(H_ups.sem, H_ups.at(i))
            for f in range(FC):
                last = nc.vector.scalar_tensor_tensor(H_h[:, f, :], all4(1)[:, f * D:(f + 1) * D], H_up[:, f:f + 1], H_silu[:, f, :],
                                                      ALU.mult, ALU.mult)
            ch.link(last)
            h, h2 = H_h, H_h2
            for s in (4, 2, 1):
                a = h.rearrange("p (o two s) d -> p o two (s d)", two=2, s=s)
                b = h2.rearrange("p (o two s) d -> p o two (s d)", two=2, s=s)
                nc.vector.tensor_tensor(b[:, :, 0, :], a[:, :, 0, :], a[:, :, 1, :], ALU.add)
                sub = nc.vector.tensor_tensor(b[:, :, 1, :], a[:, :, 0, :], a[:, :, 1, :], ALU.subtract)
                if s == 1:
                    sub.then_inc(H_hs.sem, 1)
                else:
                    ch.link(sub)
                h, h2 = h2, h
            for g in range(G):
                dve.wait_ge(H_down.sem, H_down.at(i, g))
                ch.link(nc.vector.tensor_tensor(H_t[g], bank(1, g)[:, 0:D], H_row, ALU.mult))
                add_to_x(dve, ch, i * G + g, H_t[g], gates[:, 1, 3:4])

        def H_scalar(act, ch, i):
            for g in range(G):
                act.wait_ge(xnT_done.sem, xnT_done.at(i, g))
                for k in range(KC):
                    last = nc.scalar.activation(xT[:, k, g, :], bank(g, 0)[:, k * P:(k + 1) * P], ACT.Copy, scale=H_col[:, k:k + 1])
                last.then_inc(xT_ready.sem, 1)
            act.wait_ge(H_rot.sem, H_rot.at(i))
            nc.scalar.activation(H_rT.rearrange("p a b -> p (a b)"), bank(0, 1), ACT.Copy, scale=1.0 / (16 * 64)).then_inc(H_rTs.sem, 1)
            act.wait_ge(H_gates.sem, H_gates.at(i))
            for f in range(FC):
                last = nc.scalar.activation(H_silu[:, f, :], all4(0)[:, f * D:(f + 1) * D], ACT.Silu, scale=H_gate[:, f:f + 1])
            last.then_inc(H_silus.sem, 1)
            act.wait_ge(H_turned.sem, H_turned.at(i))
            nc.scalar.activation(H_yT.rearrange("p a b -> p (a b)"), all4(0), ACT.Copy, scale=1.0 / (32 * 64)).then_inc(H_yTs.sem, 1)

        def H_tensor(pe, i):
            norm_tensor(pe, i)
            pe.wait_ge(xT_ready.sem, xT_ready.at(i, 1))
            for m in range(KC):
                for k in range(KC):
                    last = nc.tensor.matmul(bank(0, 1)[:, m * D:(m + 1) * D], had256[:, k, m * P:(m + 1) * P],
                                            xT[:, k].rearrange("p g t -> p (g t)"), start=k == 0, stop=k == KC - 1)
            last.then_inc(H_rot.sem, 1)
            pe.wait_ge(H_rTs.sem, H_rTs.at(i))
            for n, (name, done) in enumerate((("gate", H_gates), ("up", H_ups))):
                for f in range(FC):
                    for k in range(KC):
                        last = nc.tensor.matmul(all4(n)[:, f * D:(f + 1) * D], wH[name][:, k, f * P:(f + 1) * P], H_rT[:, k, :],
                                                start=k == 0, stop=k == KC - 1)
                last.then_inc(done.sem, 1)
            pe.wait_ge(H_hs.sem, H_hs.at(i))
            for n in range(4):
                last = nc.tensor.matmul(bank(0, n), had128[:], H_h2[:, 2 * n:2 * n + 2, :].rearrange("p a b -> p (a b)"), start=True, stop=True)
            last.then_inc(H_turned.sem, 1)
            pe.wait_ge(H_yTs.sem, H_yTs.at(i))
            for g in range(G):
                for f in range(FC):
                    last = nc.tensor.matmul(bank(1, g)[:, 0:D], H_yT[:, f, g * P:(g + 1) * P], wH["down"][:, f, :],
                                            start=f == 0, stop=f == FC - 1)
                last.then_inc(H_down.sem, 1)

        SUB.append((None, H_tensor, H_scalar, B_gpsimd, H_vector))

        for n in range(8):
            weights_sent[n] = 16 * len(LOADS[n])
        weights_sent[2] += 16
        weights_sent[3] += 16 * len(LOADS["3 attention"])
        block = ctx.enter_context(nc.Block())

        @block.sync
        def _(sp):
            def const(dst, src):
                sp.dma_start(dst, src).then_inc(const_in, 16)

            sp.dma_start(X[:], t["x"]).then_inc(x_in, 16)
            load_weights(sp, 0)
            const(gates[:], t["gates"].rearrange("(o a) b -> o a b", o=1).broadcast_to([P, 2, 4]))
            const(had256[:], t["had256"])
            const(had128[:], t["had128"])
            load_weights(sp, 1)
            load_weights(sp, 2)
            ctx_base[0] = 0
            for n, (f, *_) in enumerate(SUB[:layers]):
                if n == 2:
                    sp.wait_ge(B_quantised, 1)
                    sp.dma_start(wC["proj"], t["C_proj"]).then_inc(weights_in[2], 16)
                if n in LOAD_AT:
                    for m, prior in LOAD_AT[n]:
                        if (3 if m == "3 attention" else m) < layers:
                            sp.wait_ge(x_done.sem, NB * (prior + 1))
                            load_weights(sp, m)
                if (n, 0) in BEFORE:
                    BEFORE[n, 0](sp)
                if f is None:
                    continue
                with sp.Fori(0, STEPS) as i:
                    f(sp, i)
                ctx_base[0] += STEPS
            sp.wait_ge(x_done.sem, NB * layers)
            sp.dma_start(out, X[:]).then_inc(out_stored, 16)
            sp.wait_ge(out_stored, 16)

        def run(eng, chain_sem, which):
            for f in shared:
                f.base = 0
            ctx_base[0] = 0
            ch = Chain(eng, chain_sem) if chain_sem is not None else None
            for n, fs in enumerate(SUB[:layers]):
                if weights_sent[n] and which == 1 or (n, which) in WEIGHT_USERS:
                    eng.wait_ge(weights_in[n], weights_sent[n])
                if (n, which) in BEFORE:
                    BEFORE[n, which](eng, ch)
                    if ch:
                        ch.restart()
                if (n, 0) in BEFORE:
                    ctx_base[0] += STEPS
                with eng.Fori(0, STEPS) as i:
                    if ch:
                        fs[which](eng, ch, i)
                        ch.restart()
                    else:
                        fs[which](eng, i)
                for f in shared:
                    f.base += NB
                if fs[0] is not None:
                    ctx_base[0] += STEPS

        @block.gpsimd
        def _(pool):
            nc.gpsimd.memset(ident[:], 0.0).then_inc(pool_order, 1)
            nc.gpsimd.memset(minus_half[:], -0.5).then_inc(pool_order, 1)
            nc.gpsimd.memset(eps5[:], 1e-5).then_inc(pool_order, 1)
            nc.gpsimd.memset(ones[:], 1.0).then_inc(pool_order, 1)
            pool.wait_ge(pool_order, 4)
            nc.gpsimd.affine_select(out=ident[:], in_=ident[:], compare_op=ALU.not_equal, fill=1.0, base=0,
                                    pattern=[[-1, P]], channel_multiplier=1).then_inc(pool_order, 1)
            pool.wait_ge(pool_order, 5)
            nc.gpsimd.tensor_copy(ident_b[:], ident[:]).then_inc(ident_ready, 1)
            pool.sem_clear(pool_order)
            run(pool, pool_order, 3)

        @block.scalar
        def _(act):
            act.wait_ge(const_in, 48)
            nc.scalar.activation(gates[:], gates[:], ACT.Tanh).then_inc(gates_ready, 1)
            run(act, act_order, 2)

        @block.tensor
        def _(pe):
            for g in range(G):
                pe.sem_inc(ctx_read[g], 1)
            pe.wait_ge(ident_ready, 1)
            pe.wait_ge(const_in, 48)
            run(pe, None, 1)

        @block.vector
        def _(dve):
            dve.wait_ge(x_in, 16)
            dve.wait_ge(gates_ready, 1)
            run(dve, dve_order, 4)


def rows(w):
    k, n = w.shape
    return w.reshape(k // P, P, n).transpose(1, 0, 2)


def hadamard(n):
    import numpy as np
    h = np.ones((1, 1), np.float32)
    while h.shape[0] < n:
        h = np.block([[h, h], [h, -h]])
    return h.astype(np.float32)


def lay_out(i):
    import numpy as np
    a = {k: np.asarray(v) for k, v in i.items()}
    ctxs = a["ctx_2048"]
    r = {
        "x": a["x"].transpose(1, 0, 2),
        "ctxT": ctxs.transpose(2, 0, 1).reshape(KC, P, NB, P).transpose(1, 0, 2, 3),
        "gates": np.stack([a["g_xattn"], a["g_ffn"]]),
        "had256": rows(hadamard(D)),
        "had128": hadamard(P),
    }
    kv = np.concatenate([a["L0_xattn_Wk"], a["L0_xattn_Wv"]])
    r["A_q"] = rows(a["L0_xattn_Wq"].T)
    r["A_kv"] = rows(np.concatenate([kv[0::2], kv[1::2]]).T)
    r["B_gate"] = rows(a["L0_ffn_w_gate"].T)
    r["B_up"] = rows(a["L0_ffn_w_up"].T)
    r["B_down"] = rows(a["L0_ffn_w_down"].T)
    L = "L1_xattn_"
    for n, w in (("q", "wq"), ("qx", "wqx"), ("k", "wk"), ("v", "wv"), ("kvx", "w_kv_x"), ("proj", "wproj")):
        r["C_" + n] = rows(a[L + w].T)
    col = lambda v: v.reshape(-1, P).T
    r["C_col"] = np.concatenate([col(a[L + n]) for n in (
        "ln_w", "ln_b", "q_in_scale", "qx_in_scale", "k_in_scale", "v_in_scale",
        "qln_w", "qln_b", "kln_w", "kln_b", "qxln_w", "qxln_b", "kxln_w", "kxln_b", "proj_smooth")], axis=1)
    r["C_scalar"] = np.stack([a[L + n].reshape(()) for n in (
        "wq_scale", "wqx_scale", "wk_scale", "wv_scale", "proj_w_scale", "proj_in_scale")]).reshape(1, 6)
    L = "L1_ffn_"
    for n, w in (("q", "Wq"), ("k", "Wk")):
        padded = np.zeros((16, 32, D), a[L + w].dtype)
        padded[:, :16] = a[L + w].reshape(16, 16, D)
        r["D_" + n] = rows(padded.reshape(512, D).T)
    for n, w in (("v", "Wv"), ("o", "Wo"), ("in", "W_in_base"), ("up", "W_up_base"), ("down", "W_down")):
        r["D_" + n] = rows(a[L + w].T)
    r["D_a"] = rows(a[L + "A"])
    r["D_b"] = a[L + "B"]
    r["D_col"] = np.concatenate([col(a[L + "ln1_w"]), col(a[L + "ln2_w"])], axis=1)
    r["D_mask"] = np.where(np.tril(np.ones((P, P), bool)), np.float32(0), np.float32(NEG))
    L = "L2_xattn_"
    for n, w in (("q", "Wq"), ("kv", "Wkv"), ("p", "Wp")):
        r["E_" + n] = rows(a[L + w])
    r["E_bias"] = np.concatenate([a[L + "bq"], a[L + "bkv"], a[L + "bp"]]).reshape(1, -1)
    L = "L2_ffn_"
    r["F_gate"] = rows(a[L + "gate_w"])
    r["F_w1"] = rows(a[L + "w1"].transpose(1, 0, 2).reshape(D, 8 * P))
    r["F_w2"] = a[L + "w2"].transpose(1, 0, 2)
    r["F_sw1"] = rows(a[L + "shared_w1"])
    r["F_sw2"] = rows(a[L + "shared_w2"])
    r["F_b2"] = a[L + "b2"]
    r["F_sb2"] = a[L + "shared_b2"].reshape(1, D)
    r["F_col"] = np.concatenate([a[L + "b1"].T, col(a[L + "shared_b1"])], axis=1)
    r["ctx"] = ctxs.transpose(1, 0, 2)
    r["G_mask"] = a["mask_BxS2_bk0"].reshape(1, NB * P)
    L = "L3_ffn_"
    for n, w in (("up", "W_up"), ("gate", "W_gate"), ("down", "W_down")):
        r["H_" + n] = rows(a[L + w].T)
    r["H_col"] = np.concatenate([col(a[L + n]) for n in ("SU_ug", "SU_dp", "Wscale_ug")], axis=1)
    r["H_row"] = a[L + "Wscale_dp"].reshape(1, D)
    for f in LAYOUTS:
        r.update(f(a, np))
    return {k: np.ascontiguousarray(v) for k, v in r.items()}


LAYOUTS = []


def kernel(**inputs):
    import concourse.bacc as bacc
    from concourse.bass_utils import run_bass_kernel_spmd

    nc = bacc.Bacc("TRN2", target_bir_lowering=False, num_devices=1)
    arrays = lay_out(inputs)
    t = {k: nc.dram_tensor(f"in_{k}", v.shape, mybir.dt.from_np(v.dtype), kind="ExternalInput").ap() for k, v in arrays.items()}
    out = nc.dram_tensor("out", (P, NB, D), F32, kind="ExternalOutput").ap()
    program(nc, t, out)
    r = run_bass_kernel_spmd(nc, [{f"in_{k}": v for k, v in arrays.items()}], core_ids=[0])
    return r.results[0]["out"].transpose(1, 0, 2)
```

```python
from contextlib import ExitStack

import concourse.bass as bass
from concourse import mybir

ALU = mybir.AluOpType
ACT = mybir.ActivationFunctionType
AX = mybir.AxisListType
F32 = mybir.dt.float32
BF16 = mybir.dt.bfloat16
U8 = mybir.dt.uint8
U16 = mybir.dt.uint16

P = 128
NB = 8
D = 256
KC = D // P
G = 2
STEPS = NB // G
FF = 1024
FC = FF // P
MAGIC = 1.5 * 2.0 ** 23
NEG = -1.0e30


class Flag:

    def __init__(self, sem, per=1):
        self.sem, self.per, self.base = sem, per, 0

    def at(self, i, g, k=0):
        return self.nth(i, G * k + g)

    def nth(self, i, n):
        return i * (G * self.per) + (self.base + n + 1)


class StepFlag(Flag):

    def at(self, i, k=0):
        return i * self.per + (self.base + k + 1)


class Chain:

    def __init__(self, eng, sem):
        self.eng, self.sem, self.n = eng, sem, 0

    def link(self, ins):
        ins.then_inc(self.sem, 1)
        self.n += 1
        self.eng.wait_ge(self.sem, self.n)

    def mark(self, ins):
        ins.then_inc(self.sem, 1)
        self.n += 1
        return self.n

    def wait(self, n):
        self.eng.wait_ge(self.sem, n)

    def restart(self):
        if self.n:
            self.eng.wait_ge(self.sem, self.n)
            self.eng.sem_clear(self.sem)
            self.n = 0


def program(nc, t, out, layers=8):
    with ExitStack() as ctx:
        def sb(name, shape, dt=F32):
            return ctx.enter_context(nc.sbuf_tensor(name, shape, dt))

        def sem(name):
            return ctx.enter_context(nc.semaphore(name))

        def flag(name, per=1):
            return Flag(sem(name), per)

        def step_flag(name, per=1):
            return StepFlag(sem(name), per)

        X = sb("X", [P, NB, D])
        xn = sb("xn", [P, G, D])
        xT = sb("xT", [P, KC, G, P])
        stats = sb("stats", [P, G, 6])
        moments = sb("moments", [P, G, 2])
        rstd = sb("rstd", [P, G, 1])
        small = sb("small", [P, G, 96])
        eps5 = sb("eps5", [P, 1])
        minus_half = sb("minus_half", [P, 96])
        ident = sb("ident", [P, P])
        ident_b = sb("ident_b", [P, P], BF16)
        gates = sb("gates", [P, 2, 4])
        had256 = sb("had256", [P, KC, D])
        had128 = sb("had128", [P, P])
        ones = sb("ones", [P, P])
        root = sb("root", [P, 2, 64])
        ctxT = sb("ctxT", [P, G, KC, P])
        PS = ctx.enter_context(nc.psum_tensor("PS", [P, NB, 512], F32))

        def bank(g, n):
            return PS[:, 4 * g + n, :]

        def banks(g, n):
            return PS[:, 4 * g + n:4 * g + n + 2, :].rearrange("p a b -> p (a b)")

        work = sb("work", [P, G, 6144])
        spare = sb("spare", [P, 2048])
        early = sb("early", [P, 4608])
        late = sb("late", [P, 24576])

        def view(tile, at, *shape, dt=F32):
            n = 1
            for s in shape:
                n *= s
            words = n * (2 if dt in (BF16, U16) else 4) // 4
            v = tile[:, at:at + words]
            if dt != F32:
                v = v.bitcast(dt)
            names = ["a", "b", "c", "d", "e"][:len(shape)]
            if len(shape) > 1:
                v = v.rearrange(f"p ({' '.join(names)}) -> p {' '.join(names)}", **dict(zip(names, shape)))
            return v, at + words

        const_in = sem("const_in")
        const_sent = [0]
        ident_ready = sem("ident_ready")
        x_in = sem("x_in")
        gates_ready = sem("gates_ready")
        weights_in = [sem(f"weights_in{n}") for n in range(8)]
        weights_sent = [0] * 8
        out_stored = sem("out_stored")
        ctx_in = [sem(f"ctx_in{g}") for g in range(G)]
        ctx_read = [sem(f"ctx_read{g}") for g in range(G)]
        ctx_base = [0]

        def ctx_loaded(eng, i, g):
            eng.wait_ge(ctx_in[g], i * 16 + 16 * (ctx_base[0] + 1))


        stats_ready = flag("stats_ready")
        rstd_ready = flag("rstd_ready")
        xn_ready = flag("xn_ready")
        xnT_done = flag("xnT_done")
        xT_ready = flag("xT_ready")
        x_done = flag("x_done")
        shared = (stats_ready, rstd_ready, xn_ready, xnT_done, xT_ready, x_done)
        dve_order = sem("dve_order")
        act_order = sem("act_order")
        pool_order = sem("pool_order")

        def norm_stats(ch, i, units=range(G)):
            for u in units:
                ch.link(nc.vector.bn_stats(stats[:, u % G, :], X[:, i * G + u, :]))
                nc.vector.bn_aggr(moments[:, u % G, :], stats[:, u % G, :]).then_inc(stats_ready.sem, 1)

        def norm_vector(dve, ch, i, again=None):
            norm_stats(ch, i)
            for g in range(G):
                b = i * G + g
                dve.wait_ge(rstd_ready.sem, rstd_ready.at(i, g))
                normed = nc.vector.tensor_scalar(xn[:, g, :], X[:, b, :], moments[:, g, 0:1], rstd[:, g, :],
                                                 ALU.subtract, ALU.mult)
                if again:
                    ch.link(normed)
                    again(g)
                else:
                    normed.then_inc(xn_ready.sem, 1)

        def norm_gpsimd(pool, ch, i, units=range(G)):
            for u in units:
                g = u % G
                pool.wait_ge(stats_ready.sem, stats_ready.nth(i, u))
                ch.link(nc.gpsimd.tensor_tensor(rstd[:, g, :], moments[:, g, 1:2], eps5[:], ALU.add))
                nc.gpsimd.tensor_tensor(rstd[:, g, :], rstd[:, g, :], minus_half[:, 0:1],
                                        ALU.pow).then_inc(rstd_ready.sem, 1)

        def norm_tensor(pe, i):
            for g in range(G):
                pe.wait_ge(xn_ready.sem, xn_ready.at(i, g))
                for k in range(KC):
                    last = nc.tensor.transpose(bank(g, 0)[:, k * P:(k + 1) * P], xn[:, g, k * P:(k + 1) * P], ident[:])
                last.then_inc(xnT_done.sem, 1)

        def norm_scalar(act, i):
            for g in range(G):
                act.wait_ge(xnT_done.sem, xnT_done.at(i, g))
                nc.scalar.copy(xT[:, :, g, :], bank(g, 0)[:, 0:D].rearrange("p (k t) -> p k t", k=KC)).then_inc(xT_ready.sem, 1)

        def rsqrt_vector(ch, x, n):
            y, z = root[:, 0, 0:n], root[:, 1, 0:n]
            i32 = mybir.dt.int32
            ch.link(nc.vector.tensor_single_scalar(y.bitcast(i32), x.bitcast(i32), 1, ALU.arith_shift_right))
            ch.link(nc.vector.tensor_scalar(y.bitcast(i32), y.bitcast(i32), -1.0, float(0x5F3759DF), ALU.mult, ALU.add))
            for step in range(3):
                ch.link(nc.vector.scalar_tensor_tensor(z, y, -0.5, y, ALU.mult, ALU.mult))
                ch.link(nc.vector.tensor_tensor(z, z, x, ALU.mult))
                ch.link(nc.vector.scalar_tensor_tensor(y, z, 1.5, y, ALU.add, ALU.mult))
            return y

        SUB = []
        LOADS = {n: [] for n in [*range(8), "3 attention"]}
        LOAD_AT = {2: [("3 attention", 1)], 3: [(3, 2), (4, 2), (5, 2), (6, 2), (7, 2)]}
        WEIGHT_USERS = set()
        LOOPS = {}
        BEFORE = {}

        def load_weights(sp, n):
            for dst, name in LOADS[n]:
                src = t[name]
                if src.shape[0] == 1:
                    src = src.broadcast_to(dst.shape)
                sp.dma_start(dst, src).then_inc(weights_in[3 if n == "3 attention" else n], 16)

        HA, DA = 32, 8
        TA = HA // 4
        wA_q, n_ = view(early, 0, KC, D)
        wA_kv, n_ = view(early, n_, KC, 2 * D)
        A_ = [{} for _ in range(G)]
        A_qkn = []
        for g in range(G):
            w, n_ = work[:, g, :], 0
            A_[g]["sq"], n_ = view(w, n_, 2, D)
            A_[g]["v1"], _ = view(spare, 1024 * g, HA, 32)
            A_[g]["oT"], n_ = view(w, n_, 4, P)
            A_[g]["qT"], n_ = view(w, n_, TA, P)
            A_[g]["kT"], n_ = view(w, n_, TA, P)
            A_[g]["p"], n_ = view(w, n_, 4, 4, P)
            qkn, n_ = view(w, n_, TA, 4, 32)
            A_qkn.append(qkn)
        A_res = sb("A_res", [P, D])
        LOADS[0] += [(wA_q, "A_q"), (wA_kv, "A_kv")]

        def A_prepare(dve, ch):
            for g in range(G):
                ch.link(nc.vector.memset(A_[g]["v1"].rearrange("p h d -> p (h d)"), 0.0))
                ch.mark(nc.vector.memset(A_[g]["v1"][:, :, DA:DA + 1], 1.0))
                ch.mark(nc.vector.memset(A_qkn[g].rearrange("p t j r -> p (t j r)"), 0.0))

        BEFORE[0, 4] = A_prepare
        A_qkv = flag("A_qkv")
        A_sq = flag("A_sq")
        A_vs = flag("A_vs")
        A_normed = flag("A_normed")
        A_turned = flag("A_turned", 4)
        A_turned_act = flag("A_turned_act", 2)
        A_turned_dve = flag("A_turned_dve", 2)
        A_scores = flag("A_scores", 8)
        A_exp = flag("A_exp", 8)
        A_pv = flag("A_pv", 2)
        A_oTs = flag("A_oTs", 2)
        A_o = flag("A_o", 2)
        A_read = flag("A_read")
        A_read.base = 1
        PREP = (6, 7)

        def ctx_sync(sp, i):
            for g in range(G):
                sp.wait_ge(ctx_read[g], i + (ctx_base[0] + 1))
                sp.dma_start(ctxT[:, g], t["ctxT"][:, :, i * G + g, :]).then_inc(ctx_in[g], 16)

        def A_pipeline(eng, ch, first, slot):
            first(ch)
            if ch:
                ch.restart()
            with eng.Fori(0, STEPS - 1) as i:
                for u in range(G):
                    slot(ch, i, u, 2)
                if ch:
                    ch.restart()
            slot(ch, STEPS - 1, 0, 1)
            slot(ch, STEPS - 1, 1, 0)

        def A_tensor(pe):
            def turn_x(i, u):
                pe.wait_ge(xn_ready.sem, xn_ready.nth(i, u))
                for k in range(KC):
                    last = nc.tensor.transpose(PS[:, PREP[0], k * P:(k + 1) * P], xn[:, u % G, k * P:(k + 1) * P], ident[:])
                last.then_inc(xnT_done.sem, 1)

            def projections(i, u):
                g = u % G
                ctx_loaded(pe, i + u // G, g)
                for c in range(2):
                    for k in range(KC):
                        last = nc.tensor.matmul(PS[:, PREP[1], c * D:(c + 1) * D], ctxT[:, g, k, :], wA_kv[:, k, c * D:(c + 1) * D],
                                                start=k == 0, stop=k == KC - 1)
                last.then_inc(ctx_read[g], 1)
                pe.wait_ge(xT_ready.sem, xT_ready.nth(i, u))
                for k in range(KC):
                    last = nc.tensor.matmul(PS[:, PREP[0], 0:D], xT[:, k, g, :], wA_q[:, k, :], start=k == 0, stop=k == KC - 1)
                last.then_inc(A_qkv.sem, 1)

            def turn(i, u, n):
                if n == 0:
                    pe.wait_ge(A_normed.sem, A_normed.nth(i, u))
                else:
                    pe.wait_ge(A_turned_act.sem, A_turned_act.nth(i, 2 * u))
                    pe.wait_ge(A_turned_dve.sem, A_turned_dve.nth(i, 2 * u))
                for c in range(2):
                    for tt in range(4):
                        last = nc.tensor.transpose(PS[:, PREP[c], tt * P:(tt + 1) * P],
                                                   A_qkn[n][:, 4 * c + tt].rearrange("p j r -> p (j r)"), ident[:])
                    last.then_inc(A_turned.sem, 1)

            def scores(i, u, half):
                g, r = u % G, 2 * u + half
                if half == 0:
                    pe.wait_ge(A_turned_act.sem, A_turned_act.nth(i, 2 * u + 1))
                    pe.wait_ge(A_turned_dve.sem, A_turned_dve.nth(i, 2 * u + 1))
                for j in range(4):
                    if r:
                        pe.wait_ge(A_exp.sem, A_exp.nth(i, 4 * r - 4 + j))
                    rows = slice(32 * j, 32 * j + DA)
                    for m in range(4):
                        last = nc.tensor.matmul(PS[:, j, m * P:(m + 1) * P], A_[g]["kT"][rows, 4 * half + m, :],
                                                A_[g]["qT"][rows, 4 * half + m, :], start=True, stop=True)
                    last.then_inc(A_scores.sem, 1)

            def weigh(i, u, half):
                g, r = u % G, 2 * u + half
                if half == 0:
                    pe.wait_ge(A_read.sem, A_read.nth(i, u - 1))
                for j in range(4):
                    pe.wait_ge(A_exp.sem, A_exp.nth(i, 4 * r + j))
                    for m in range(4):
                        last = nc.tensor.matmul(PS[32 * j:32 * j + 32, 4 + half, m * P:(m + 1) * P],
                                                A_[g]["v1"][:, 4 * half + m + TA * j, :], A_[half]["p"][:, j, m, :], start=True, stop=True)
                last.then_inc(A_pv.sem, 1)

            def turn_back(i, u, half):
                pe.wait_ge(A_oTs.sem, A_oTs.nth(i, 2 * u + half))
                for m in range(4):
                    last = nc.tensor.transpose(PS[:, 4 + half, m * P:(m + 1) * P], A_[half]["oT"][:, m, :], ident[:])
                last.then_inc(A_o.sem, 1)

            def first(ch):
                turn_x(0, 0)
                projections(0, 0)
                turn(0, 0, 0)
                turn(0, 0, 1)

            def slot(ch, i, u, ahead):
                if ahead:
                    pe.wait_ge(A_turned_act.sem, A_turned_act.nth(i, 2 * u + 1))
                    pe.wait_ge(A_turned_dve.sem, A_turned_dve.nth(i, 2 * u + 1))
                    turn_x(i, u + 1)
                scores(i, u, 0)
                if ahead:
                    projections(i, u + 1)
                scores(i, u, 1)
                weigh(i, u, 0)
                if ahead:
                    turn(i, u + 1, 0)
                weigh(i, u, 1)
                if ahead:
                    turn(i, u + 1, 1)
                turn_back(i, u, 0)
                turn_back(i, u, 1)

            A_pipeline(pe, None, first, slot)

        def A_scalar(act, ch):
            def feature_major(i, u):
                act.wait_ge(xnT_done.sem, xnT_done.nth(i, u))
                nc.scalar.copy(xT[:, :, u % G, :], PS[:, PREP[0], 0:D].rearrange("p (k t) -> p k t", k=KC)).then_inc(xT_ready.sem, 1)

            def squares(i, u):
                g = u % G
                act.wait_ge(A_qkv.sem, A_qkv.nth(i, u))
                nc.scalar.activation(A_[g]["sq"][:, 0, :], PS[:, PREP[0], 0:D], ACT.Square)
                nc.scalar.activation(A_[g]["sq"][:, 1, :], PS[:, PREP[1], 0:D], ACT.Square).then_inc(A_sq.sem, 1)
                nc.scalar.copy(A_[g]["v1"][:, :, 0:DA], PS[:, PREP[1], D:2 * D].rearrange("p (h d) -> p h d", h=HA)).then_inc(A_vs.sem, 1)

            def turned(i, u):
                for n, name in enumerate(("qT", "kT")):
                    act.wait_ge(A_turned.sem, A_turned.nth(i, 4 * u + 2 * n))
                    nc.scalar.copy(A_[u % G][name][:, 0:4, :].rearrange("p a b -> p (a b)"), PS[:, PREP[0], :]).then_inc(A_turned_act.sem, 1)

            def exps(i, u, half):
                r = 2 * u + half
                for j in range(4):
                    if j == 0 and r >= 2:
                        act.wait_ge(A_pv.sem, A_pv.nth(i, r - 2))
                    act.wait_ge(A_scores.sem, A_scores.nth(i, 4 * r + j))
                    nc.scalar.activation(A_[half]["p"][:, j].rearrange("p a b -> p (a b)"), PS[:, j, :], ACT.Exp,
                                         scale=DA ** -0.5).then_inc(A_exp.sem, 1)

            def first(ch):
                feature_major(0, 0)
                squares(0, 0)
                turned(0, 0)

            def slot(ch, i, u, ahead):
                if ahead:
                    feature_major(i, u + 1)
                exps(i, u, 0)
                if ahead:
                    squares(i, u + 1)
                exps(i, u, 1)
                if ahead:
                    turned(i, u + 1)

            A_pipeline(act, ch, first, slot)

        def A_gpsimd(pool, ch):
            def slot(ch, i, u, ahead):
                if ahead == 2:
                    norm_gpsimd(pool, ch, i, [u + 2])

            A_pipeline(pool, ch, lambda ch: norm_gpsimd(pool, ch, 0), slot)

        def A_vector(dve, ch):
            def normed_x(i, u):
                dve.wait_ge(rstd_ready.sem, rstd_ready.nth(i, u))
                nc.vector.tensor_scalar(xn[:, u % G, :], X[:, i * G + u, :], moments[:, u % G, 0:1], rstd[:, u % G, :],
                                        ALU.subtract, ALU.mult).then_inc(xn_ready.sem, 1)

            def normed(ch, i, u):
                g = u % G
                dve.wait_ge(A_sq.sem, A_sq.nth(i, u))
                ch.link(nc.vector.tensor_reduce(small[:, g, 0:2 * HA], A_[g]["sq"].rearrange("p a (h d) -> p (a h) d", d=DA), AX.X, ALU.add))
                ch.link(nc.vector.tensor_scalar(small[:, g, 0:2 * HA], small[:, g, 0:2 * HA], 1.0 / DA, 1e-6, ALU.mult, ALU.add))
                rms = rsqrt_vector(ch, small[:, g, 0:2 * HA], 2 * HA)
                dve.wait_ge(A_vs.sem, A_vs.nth(i, u))
                for n in range(2):
                    last = nc.vector.tensor_tensor(
                        A_qkn[n][:, :, :, 0:DA].rearrange("p t j d -> p j t d"),
                        PS[:, PREP[n], 0:D].rearrange("p (j t d) -> p j t d", j=4, t=TA),
                        rms[:, n * HA:(n + 1) * HA].rearrange("p (j t) -> p j t", j=4).unsqueeze(3).broadcast_to([P, 4, TA, DA]), ALU.mult)
                last.then_inc(A_normed.sem, 1)

            def turned(i, u, n):
                dve.wait_ge(A_turned.sem, A_turned.nth(i, 4 * u + 2 * n + 1))
                nc.vector.tensor_copy(A_[u % G][("qT", "kT")[n]][:, 4:8, :].rearrange("p a b -> p (a b)"),
                                      PS[:, PREP[1], :]).then_inc(A_turned_dve.sem, 1)

            def out(ch, i, u):
                dve.wait_ge(A_o.sem, A_o.nth(i, 2 * u + 1))
                o = PS[:, 4:6, :].rearrange("p half (m j d) -> p j (half m) d", m=4, j=4)
                sums = small[:, u % G, 64:96].rearrange("p (j t) -> p j t", j=4)
                res = A_res[:].rearrange("p (j t d) -> p j t d", j=4, t=TA)
                ch.link(nc.vector.reciprocal(sums, o[:, :, :, DA]))
                last = nc.vector.tensor_tensor(res, o[:, :, :, 0:DA], sums.unsqueeze(3).broadcast_to([P, 4, TA, DA]), ALU.mult)
                last.then_inc(A_read.sem, 1)
                dve.wait_ge(A_read.sem, A_read.nth(i, u))
                add_to_x(dve, ch, i * G + u, A_res[:], gates[:, 0, 0:1])

            def out_T(i, u, half):
                dve.wait_ge(A_pv.sem, A_pv.nth(i, 2 * u + half))
                nc.vector.tensor_copy(A_[half]["oT"].rearrange("p a b -> p (a b)"), PS[:, 4 + half, :]).then_inc(A_oTs.sem, 1)

            def first(ch):
                dve.sem_inc(A_read.sem, 1)
                norm_stats(ch, 0)
                for u in range(G):
                    normed_x(0, u)
                normed(ch, 0, 0)
                turned(0, 0, 0)
                turned(0, 0, 1)

            def slot(ch, i, u, ahead):
                if ahead == 2:
                    norm_stats(ch, i, [u + 2])
                if ahead:
                    normed(ch, i, u + 1)
                out_T(i, u, 0)
                if ahead:
                    turned(i, u + 1, 0)
                if ahead == 2:
                    normed_x(i, u + 2)
                out_T(i, u, 1)
                if ahead:
                    turned(i, u + 1, 1)
                out(ch, i, u)

            A_pipeline(dve, ch, first, slot)

        def add_to_x(dve, ch, b, res, scale):
            nc.vector.scalar_tensor_tensor(X[:, b, :], res, scale, X[:, b, :], ALU.mult, ALU.add).then_inc(x_done.sem, 1)

        LOOPS[0] = (None, A_tensor, A_scalar, A_gpsimd, A_vector)
        SUB.append((ctx_sync, None, None, None, None))

        WPROJ = 16384
        n_ = WPROJ
        wB = []
        for name, a, w in (("B_gate", KC, FF), ("B_up", KC, FF), ("B_down", FC, D)):
            full, n_ = view(late, n_, a, w)
            wB.append(full)
            LOADS[1].append((full, name))
        qB = []
        n_ = 1536
        for a, w in ((KC, FF), (KC, FF), (FC, D)):
            q, n_ = view(early, n_, a, w, dt=BF16)
            qB.append(q)
        B_wscale = sb("B_wscale", [P, 2, 4])
        B_ = [{} for _ in range(G)]
        for g in range(G):
            w, n_ = work[:, g, :], 0
            B_[g]["q"], n_ = view(w, n_, D, dt=BF16)
            B_[g]["qT"], n_ = view(w, n_, KC, P, dt=BF16)
            B_[g]["silu"], n_ = view(w, n_, FF)
            B_[g]["h"], n_ = view(w, n_, FF)
            B_[g]["h2"], n_ = view(w, n_, FF)
            B_[g]["hT"], n_ = view(w, n_, FC, P)
            B_[g]["hq"], n_ = view(w, n_, FF, dt=BF16)
            B_[g]["hqT"], n_ = view(w, n_, FC, P, dt=BF16)
        B_sum = sem("B_sum")
        B_total = sem("B_total")
        B_quantised = sem("B_quantised")
        B_had = flag("B_had")
        B_q = flag("B_q")
        B_qturned = flag("B_qturned")
        B_qT = flag("B_qT")
        B_gateup = flag("B_gateup")
        B_silu = flag("B_silu")
        B_h = flag("B_h")
        B_hturned = flag("B_hturned")
        B_hT = flag("B_hT")
        B_hhad = flag("B_hhad")
        B_hq = flag("B_hq")
        B_hqturned = flag("B_hqturned")
        B_hqT = flag("B_hqT")
        B_down = flag("B_down")
        WEIGHT_USERS.add((1, 4))

        def B_before_vector(dve, ch):
            for n in range(3):
                last = nc.vector.tensor_reduce(B_wscale[:, 0, n:n + 1], wB[n].rearrange("p a b -> p (a b)"), AX.X, ALU.add,
                                               apply_absolute_value=True)
            last.then_inc(B_sum, 1)
            dve.wait_ge(B_total, 1)
            ch.link(nc.vector.tensor_scalar(B_wscale[:, 0, 0:3], bank(0, 0)[:, 0:3], 1.0 / (FF * D), 1e-5, ALU.mult, ALU.max))
            ch.link(nc.vector.reciprocal(B_wscale[:, 1, 0:3], B_wscale[:, 0, 0:3]))
            for n in range(3):
                w = wB[n].rearrange("p a b -> p (a b)")
                ch.link(nc.vector.tensor_scalar(w, w, B_wscale[:, 1, n:n + 1], MAGIC, ALU.mult, ALU.add))
                ch.link(nc.vector.tensor_scalar(w, w, MAGIC, 1.0, ALU.subtract, ALU.min))
                ch.link(nc.vector.tensor_scalar(qB[n].rearrange("p a b -> p (a b)"), w, -1.0, None, ALU.max))
            dve.wait_ge(weights_in[2], 16 * len(LOADS[2]))
            nc.vector.memset(root[:, 0, :], 1.0).then_inc(B_quantised, 1)

        def B_before_tensor(pe, ch):
            pe.wait_ge(B_sum, 1)
            nc.tensor.matmul(bank(0, 0)[:, 0:3], ones[:], B_wscale[:, 0, 0:3], start=True, stop=True).then_inc(B_total, 1)

        BEFORE[1, 4] = B_before_vector
        BEFORE[1, 1] = B_before_tensor

        def B_tensor(pe, i):
            norm_tensor(pe, i)
            for g in range(G):
                pe.wait_ge(xT_ready.sem, xT_ready.at(i, g))
                for k in range(KC):
                    last = nc.tensor.matmul(bank(g, 1)[:, 0:D], xT[:, k, g, :], had256[:, k, :], start=k == 0, stop=k == KC - 1)
                last.then_inc(B_had.sem, 1)
            for g in range(G):
                pe.wait_ge(B_q.sem, B_q.at(i, g))
                dst = bank(g, 0)[:, 0:P].bitcast(BF16)
                for k in range(KC):
                    last = nc.tensor.transpose(dst[:, k * P:(k + 1) * P], B_[g]["q"][:, k * P:(k + 1) * P], ident_b[:])
                last.then_inc(B_qturned.sem, 1)
            for g in range(G):
                pe.wait_ge(B_qT.sem, B_qT.at(i, g))
                for w, at in ((0, 2), (1, 0)):
                    for n in range(2):
                        for k in range(KC):
                            last = nc.tensor.matmul(bank(g, at + n), B_[g]["qT"][:, k, :], qB[w][:, k, n * 512:(n + 1) * 512],
                                                    start=k == 0, stop=k == KC - 1)
                last.then_inc(B_gateup.sem, 1)
            for g in range(G):
                pe.wait_ge(B_h.sem, B_h.at(i, g))
                for a in range(FC):
                    last = nc.tensor.transpose(banks(g, 2)[:, a * P:(a + 1) * P], B_[g]["h2"][:, a * P:(a + 1) * P], ident[:])
                last.then_inc(B_hturned.sem, 1)
            for g in range(G):
                pe.wait_ge(B_hT.sem, B_hT.at(i, g))
                for a in range(FC):
                    last = nc.tensor.matmul(banks(g, 0)[:, a * P:(a + 1) * P], B_[g]["hT"][:, a, :], had128[:], start=True, stop=True)
                last.then_inc(B_hhad.sem, 1)
            for g in range(G):
                pe.wait_ge(B_hq.sem, B_hq.at(i, g))
                dst = bank(g, 2).bitcast(BF16)
                for a in range(FC):
                    last = nc.tensor.transpose(dst[:, a * P:(a + 1) * P], B_[g]["hq"][:, a * P:(a + 1) * P], ident_b[:])
                last.then_inc(B_hqturned.sem, 1)
            for g in range(G):
                pe.wait_ge(B_hqT.sem, B_hqT.at(i, g))
                for a in range(FC):
                    last = nc.tensor.matmul(bank(g, 3)[:, 0:D], B_[g]["hqT"][:, a, :], qB[2][:, a, :], start=a == 0, stop=a == FC - 1)
                last.then_inc(B_down.sem, 1)

        def B_scalar(act, ch, i):
            norm_scalar(act, i)
            for g in range(G):
                act.wait_ge(B_qturned.sem, B_qturned.at(i, g))
                nc.scalar.copy(B_[g]["qT"].rearrange("p a b -> p (a b)"), bank(g, 0)[:, 0:P].bitcast(BF16)).then_inc(B_qT.sem, 1)
            for g in range(G):
                act.wait_ge(B_gateup.sem, B_gateup.at(i, g))
                nc.scalar.activation(B_[g]["silu"], banks(g, 2), ACT.Silu, scale=small[:, g, 4:5]).then_inc(B_silu.sem, 1)
            for g in range(G):
                act.wait_ge(B_hturned.sem, B_hturned.at(i, g))
                nc.scalar.copy(B_[g]["hT"].rearrange("p a b -> p (a b)"), banks(g, 2)).then_inc(B_hT.sem, 1)
            for g in range(G):
                act.wait_ge(B_hqturned.sem, B_hqturned.at(i, g))
                nc.scalar.copy(B_[g]["hqT"].rearrange("p a b -> p (a b)"), bank(g, 2).bitcast(BF16)).then_inc(B_hqT.sem, 1)

        def B_gpsimd(pool, ch, i):
            norm_gpsimd(pool, ch, i)

        def quantize(ch, g, src, scaled, whole, norm, done, at, scales):
            s = small[:, g, at:at + 1]
            r = small[:, g, at + 1:at + 2]
            ch.link(nc.vector.tensor_reduce(s, src, AX.X, ALU.max, apply_absolute_value=True))
            ch.link(nc.vector.tensor_scalar(s, s, norm, 1e-5, ALU.mult, ALU.max))
            ch.link(nc.vector.reciprocal(r, s))
            ch.link(nc.vector.tensor_scalar(r, r, 127.0 * norm, None, ALU.mult))
            ch.link(nc.vector.tensor_scalar(scaled, src, r, MAGIC, ALU.mult, ALU.add))
            scales()
            nc.vector.tensor_scalar(whole, scaled, MAGIC, 127.0, ALU.subtract, ALU.min).then_inc(done, 1)

        def B_vector(dve, ch, i):
            norm_vector(dve, ch, i)
            for g in range(G):
                dve.wait_ge(B_had.sem, B_had.at(i, g))

                def scales(g=g):
                    for n in range(2):
                        nc.vector.tensor_scalar(small[:, g, 4 + n:5 + n], small[:, g, 0:1], B_wscale[:, 0, n:n + 1], 1.0 / 127,
                                                ALU.mult, ALU.mult)

                quantize(ch, g, bank(g, 1)[:, 0:D], B_[g]["h"][:, 0:D], B_[g]["q"], 1.0 / 16, B_q.sem, 0, scales)
            C_centre(ch, i)
            for g in range(G):
                dve.wait_ge(B_silu.sem, B_silu.at(i, g))
                h, h2 = B_[g]["h"], B_[g]["h2"]
                ch.link(nc.vector.scalar_tensor_tensor(h, banks(g, 0), small[:, g, 5:6], B_[g]["silu"], ALU.mult, ALU.mult))
                for s in (4, 2, 1):
                    a = h.rearrange("p (o two s) -> p o two s", two=2, s=s * P)
                    b = h2.rearrange("p (o two s) -> p o two s", two=2, s=s * P)
                    add = nc.vector.tensor_tensor(b[:, :, 0, :], a[:, :, 0, :], a[:, :, 1, :], ALU.add)
                    sub = nc.vector.tensor_tensor(b[:, :, 1, :], a[:, :, 0, :], a[:, :, 1, :], ALU.subtract)
                    if s == 1:
                        sub.then_inc(B_h.sem, 1)
                    else:
                        ch.link(sub)
                    h, h2 = h2, h
            for g in range(G):
                dve.wait_ge(B_hhad.sem, B_hhad.at(i, g))

                def scales(g=g):
                    ch.link(nc.vector.tensor_scalar(small[:, g, 10:11], small[:, g, 8:9], B_wscale[:, 0, 2:3], 1.0 / 127, ALU.mult, ALU.mult))
                    ch.link(nc.vector.tensor_scalar(small[:, g, 11:12], small[:, g, 10:11], gates[:, 1, 0:1], None, ALU.mult))

                quantize(ch, g, banks(g, 0), B_[g]["h"], B_[g]["hq"], 1.0 / 32, B_hq.sem, 8, scales)
            for g in range(G):
                dve.wait_ge(B_down.sem, B_down.at(i, g))
                add_to_x(dve, ch, i * G + g, bank(g, 3)[:, 0:D], small[:, g, 11:12])

        SUB.append((None, B_tensor, B_scalar, B_gpsimd, B_vector))

        HC, KVH, DC = 16, 8, 128
        ROUNDS = 8
        UNITS, DEPTH = G * ROUNDS, 6
        wC, n_ = {}, 0
        for name, a, w in (("q", KC, 2048), ("qx", KC, 2048), ("k", KC, 1024), ("kx", KC, 1024), ("v", KC, 1024), ("vx", KC, 1024),
                           ("proj", 32, D)):
            wC[name], n_ = view(late, n_, a, w)
            if name != "proj":
                LOADS[2].append((wC[name], "C_" + name))
        col = sb("C_col", [P, 52])
        c_ln_w, c_ln_b, c_in, c_head, c_smooth = col[:, 0:2], col[:, 2:4], col[:, 4:12], col[:, 12:20], col[:, 20:52]
        inv = sb("C_inv", [P, 40])
        scalar = sb("C_scalar", [P, 6])
        square = sb("C_square", [P, 2, 8])
        out_scale = sb("C_out_scale", [P, 1])
        LOADS[2] += [(col[:], "C_col"), (scalar[:], "C_scalar")]
        centre = sb("C_centre", [P, 24])
        C_ = [{} for _ in range(G)]
        for g in range(G):
            w, n_ = work[:, g, :], 0
            for name in ("kn", "qn", "kT", "qT", "cat", "p", "pT", "t"):
                C_[g][name], n_ = view(w, n_, 4, P)
            C_[g]["y"], n_ = view(w, n_, 4, P, dt=BF16)
            C_[g]["m"], n_ = view(w, n_, 4, P, dt=BF16)
            C_[g]["v"], n_ = view(w, n_, 2, 4, P)
            C_[g]["t_in"], n_ = view(w, n_, KC * P)
            C_[g]["y_in"], n_ = view(w, n_, KC * P, dt=BF16)
            C_[g]["m_in"], n_ = view(w, n_, KC * P, dt=BF16)
            C_[g]["xs"], _ = view(spare, 1024 * g, 4, KC, P)
        C_stats2 = flag("C_stats2")
        C_rstd2 = flag("C_rstd2")
        C_xs = flag("C_xs", 4)
        C_k = flag("C_k", ROUNDS // 2)
        C_vq = flag("C_vq", ROUNDS)
        C_ksq = flag("C_ksq", ROUNDS // 2)
        C_qsq = flag("C_qsq", ROUNDS)
        C_v = flag("C_v", ROUNDS // 2)
        C_ksd = flag("C_ksd", ROUNDS // 2)
        C_qsd = flag("C_qsd", ROUNDS)
        C_kn = flag("C_kn", ROUNDS // 2)
        C_qn = flag("C_qn", ROUNDS)
        C_kturned = flag("C_kturned", ROUNDS // 2)
        C_kT = flag("C_kT", ROUNDS // 2)
        C_qturned = flag("C_qturned", ROUNDS)
        C_qT = flag("C_qT", ROUNDS)
        C_scores = flag("C_scores", ROUNDS)
        C_max = flag("C_max", ROUNDS)
        C_exp = flag("C_exp", ROUNDS)
        C_p = flag("C_p", ROUNDS)
        C_pturned = flag("C_pturned", ROUNDS)
        C_pT = flag("C_pT", ROUNDS)
        C_o = flag("C_o", ROUNDS)
        C_cat = flag("C_cat", ROUNDS)
        C_out = step_flag("C_out")
        WEIGHT_USERS.update({(2, 4), (2, 2)})
        KBANK, VBANK, QBANK, TBANK, SBANK, PBANK, OBANK, OUTBANK = range(NB)
        heads4 = lambda n: PS[:, n, :].rearrange("p (h d) -> p h d", h=4)
        over_head = lambda v: v.unsqueeze(2).broadcast_to([P, 4, P])
        flat = lambda v: v.rearrange("p a b -> p (a b)")

        unit = lambda u: (u % G, (u // G) % ROUNDS)
        brings_kv = lambda u: u % 4 < G
        kv_at = lambda u: G * (u // 4) + u % G
        last_step = lambda i: isinstance(i, int) and i == STEPS - 1

        def C_slots(ch, i, slots, stages, extra):
            for n in slots:
                for lag, stage in stages:
                    if n - lag >= 0 and not (last_step(i) and n - lag >= UNITS):
                        stage(ch, i, n - lag)
                extra(ch, i, n)

        def C_pipeline(eng, ch, first, stages, extra):
            first(ch)
            C_slots(ch, 0, range(0, DEPTH), stages, extra)
            if ch:
                ch.restart()
            with eng.Fori(0, STEPS - 1) as i:
                C_slots(ch, i, range(DEPTH, UNITS + DEPTH), stages, extra)
                if ch:
                    ch.restart()
            C_slots(ch, STEPS - 1, range(DEPTH, UNITS + DEPTH), stages, extra)

        def C_centre(ch, i):
            heads = 96 // STEPS
            w = late[:, bass.ds(i * (heads * DC), heads * DC)].rearrange("p (h d) -> p h d", d=DC)
            ch.link(nc.vector.tensor_reduce(centre[:], w, AX.X, ALU.add))
            ch.link(nc.vector.tensor_scalar(centre[:], centre[:], 1.0 / DC, None, ALU.mult))
            ch.mark(nc.vector.tensor_tensor(w, w, centre[:].unsqueeze(2).broadcast_to([P, heads, DC]), ALU.subtract))

        def C_before_vector(dve, ch):
            ch.mark(nc.vector.reciprocal(inv[:, 0:8], c_in))
            ch.mark(nc.vector.reciprocal(inv[:, 8:40], c_smooth))
            ch.link(nc.vector.memset(square[:].rearrange("p a b -> p (a b)"), 1.0))
            for cross, at, n in ((0, 0, 0), (1, 0, 1), (0, 4, 2)):
                sq, w_ln, scale = square[:, cross, at:at + 4], c_head[:, 4 * cross + at // 2:4 * cross + at // 2 + 1], scalar[:, n:n + 1]
                ch.link(nc.vector.tensor_scalar(sq, sq, scale, scale, ALU.mult, ALU.mult))
                ch.link(nc.vector.tensor_tensor(w_ln, w_ln, scale, ALU.mult))
            ch.link(nc.vector.tensor_scalar(square[:], square[:], 1.0 / DC, None, ALU.mult))
            ch.link(nc.vector.tensor_tensor(out_scale[:], scalar[:, 4:5], scalar[:, 5:6], ALU.mult))
            ch.link(nc.vector.tensor_tensor(out_scale[:], out_scale[:], gates[:, 0, 1:2], ALU.mult))

        BEFORE[2, 4] = C_before_vector

        def to_fp8(ch, y, m, t, out):
            ch.link(nc.vector.tensor_single_scalar(m.bitcast(U16), y.bitcast(U16), 0x7F80, ALU.bitwise_and))
            ch.link(nc.vector.tensor_scalar(m, m, 2.0 ** -6, 1.5 * 2.0 ** 20, ALU.max, ALU.mult))
            ch.link(nc.vector.tensor_tensor(t, y, m, ALU.add))
            return nc.vector.tensor_tensor(out, t, m, ALU.subtract)

        def C_vector(dve, ch):
            def again(ch, i):
                for g in range(G):
                    dve.wait_ge(rstd_ready.sem, rstd_ready.at(i, g))
                    ch.link(nc.vector.tensor_scalar(xn[:, g, :], X[:, i * G + g, :], moments[:, g, 0:1], rstd[:, g, :],
                                                    ALU.subtract, ALU.mult))
                    ch.link(nc.vector.bn_stats(stats[:, g, :], xn[:, g, :]))
                    nc.vector.bn_aggr(moments[:, g, :], stats[:, g, :]).then_inc(C_stats2.sem, 1)

            def twice_normed(ch, i):
                for g in range(G):
                    dve.wait_ge(C_rstd2.sem, C_rstd2.at(i, g))
                    nc.vector.tensor_scalar(xn[:, g, :], xn[:, g, :], moments[:, g, 0:1], rstd[:, g, :],
                                            ALU.subtract, ALU.mult).then_inc(xn_ready.sem, 1)

            def activations(ch, g, n):
                c = C_[g]
                for k in range(KC):
                    last = nc.vector.tensor_scalar(c["t_in"][:, k * P:(k + 1) * P], xT[:, k, g, :], inv[:, n * KC + k:n * KC + k + 1],
                                                   448.0, ALU.mult, ALU.min)
                ch.link(last)
                ch.link(nc.vector.tensor_scalar(c["y_in"], c["t_in"], -448.0, None, ALU.max))
                ch.link(to_fp8(ch, c["y_in"], c["m_in"], c["t_in"], c["t_in"]))
                for k in range(KC):
                    last = nc.vector.tensor_scalar(c["xs"][:, n, k, :], c["t_in"][:, k * P:(k + 1) * P], c_in[:, n * KC + k:n * KC + k + 1],
                                                   None, ALU.mult)
                last.then_inc(C_xs.sem, 1)

            def normed_k(ch, i, u):
                g, r = unit(u)
                if brings_kv(u):
                    dve.wait_ge(C_ksd.sem, C_ksd.nth(i, kv_at(u)))
                    nc.vector.tensor_tensor(C_[g]["kn"], heads4(KBANK), over_head(small[:, g, 4:8]), ALU.mult).then_inc(C_kn.sem, 1)

            def normed_q(ch, i, u):
                g, r = unit(u)
                dve.wait_ge(C_qsd.sem, C_qsd.nth(i, u))
                nc.vector.tensor_tensor(C_[g]["qn"], heads4(QBANK), over_head(small[:, g, 0:4]), ALU.mult).then_inc(C_qn.sem, 1)

            def largest(ch, i, u):
                g, r = unit(u)
                mx = small[:, g, 8:12]
                dve.wait_ge(C_scores.sem, C_scores.nth(i, u))
                ch.link(nc.vector.tensor_reduce(mx, heads4(SBANK), AX.X, ALU.max))
                nc.vector.tensor_scalar(mx, mx, -DC ** -0.5, None, ALU.mult).then_inc(C_max.sem, 1)

            def probabilities(ch, i, u):
                g, r = unit(u)
                c = C_[g]
                dve.wait_ge(C_exp.sem, C_exp.nth(i, u))
                ch.link(nc.vector.reciprocal(small[:, g, 16:20], small[:, g, 12:16]))
                nc.vector.tensor_tensor(c["p"], c["p"], over_head(small[:, g, 16:20]), ALU.mult).then_inc(C_p.sem, 1)

            def rounded(ch, i, u):
                g, r = unit(u)
                c = C_[g]
                dve.wait_ge(C_o.sem, C_o.nth(i, u))
                ch.link(nc.vector.tensor_tensor(c["t"], heads4(OBANK), over_head(inv[:, 8 + 4 * r:12 + 4 * r]), ALU.mult))
                ch.link(nc.vector.tensor_scalar(c["y"], c["t"], 448.0, -448.0, ALU.min, ALU.max))
                to_fp8(ch, c["y"], c["m"], c["t"], c["cat"]).then_inc(C_cat.sem, 1)

            def extra(ch, i, n):
                if n == UNITS + DEPTH - 1:
                    dve.wait_ge(C_out.sem, C_out.at(i))
                    for g in range(G):
                        add_to_x(dve, ch, i * G + g, PS[:, OUTBANK, g * D:(g + 1) * D], out_scale[:])
                if last_step(i):
                    return
                if 1 <= n % UNITS <= G:
                    activations(ch, n % UNITS - 1, 1)
                if n == DEPTH:
                    norm_stats(ch, i + 1)
                if n == DEPTH + 1:
                    again(ch, i + 1)
                if n == DEPTH + 2:
                    twice_normed(ch, i + 1)
                if 11 <= n < 17:
                    m, g = divmod(n - 11, G)
                    if m == 0:
                        dve.wait_ge(xT_ready.sem, xT_ready.at(i + 1, g))
                    activations(ch, g, (2, 3, 0)[m])

            def first(ch):
                norm_stats(ch, 0)
                again(ch, 0)
                twice_normed(ch, 0)
                for n in (2, 3, 0):
                    for g in range(G):
                        dve.wait_ge(xT_ready.sem, xT_ready.at(0, g))
                        activations(ch, g, n)

            C_pipeline(dve, ch, first, [(2, largest), (3, probabilities), (5, rounded), (0, normed_k), (0, normed_q)], extra)

        def C_gpsimd(pool, ch):
            def again(ch, i):
                for g in range(G):
                    pool.wait_ge(C_stats2.sem, C_stats2.at(i, g))
                    ch.link(nc.gpsimd.tensor_tensor(rstd[:, g, :], moments[:, g, 1:2], eps5[:], ALU.add))
                    nc.gpsimd.tensor_tensor(rstd[:, g, :], rstd[:, g, :], minus_half[:, 0:1], ALU.pow).then_inc(C_rstd2.sem, 1)

            def deviations(ch, i, u):
                g, r = unit(u)

                def power(rs, square):
                    ch.link(nc.gpsimd.tensor_tensor(rs, rs, square, ALU.mult))
                    ch.link(nc.gpsimd.tensor_tensor(rs, rs, eps5[:, 0:1].broadcast_to([P, 4]), ALU.add))
                    return nc.gpsimd.tensor_tensor(rs, rs, minus_half[:, 0:4], ALU.pow)

                if brings_kv(u):
                    pool.wait_ge(C_ksq.sem, C_ksq.nth(i, kv_at(u)))
                    power(small[:, g, 4:8], square[:, r // 4, 4:8]).then_inc(C_ksd.sem, 1)
                pool.wait_ge(C_qsq.sem, C_qsq.nth(i, u))
                power(small[:, g, 0:4], square[:, r // 4, 0:4]).then_inc(C_qsd.sem, 1)

            def extra(ch, i, n):
                if not last_step(i):
                    if n == DEPTH:
                        norm_gpsimd(pool, ch, i + 1)
                    if n == DEPTH + 1:
                        again(ch, i + 1)

            def first(ch):
                norm_gpsimd(pool, ch, 0)
                again(ch, 0)

            C_pipeline(pool, ch, first, [(0, deviations)], extra)

        def C_scalar(act, ch):
            def feature_major(i):
                act.wait_ge(xnT_done.sem, xnT_done.at(i, G - 1))
                for g in range(G):
                    for k in range(KC):
                        at = (g * KC + k) * P
                        last = nc.scalar.activation(xT[:, k, g, :], PS[:, VBANK, at:at + P], ACT.Identity,
                                                    scale=c_ln_w[:, k:k + 1], bias=c_ln_b[:, k:k + 1])
                    last.then_inc(xT_ready.sem, 1)

            def squares_k(ch, i, u):
                if brings_kv(u):
                    g, r = unit(u)
                    act.wait_ge(C_k.sem, C_k.nth(i, kv_at(u)))
                    for h in range(4):
                        last = nc.scalar.activation(C_[g]["kn"][:, h, :], PS[:, KBANK, h * P:(h + 1) * P], ACT.Square,
                                                    accum_out=small[:, g, 4 + h:5 + h])
                    last.then_inc(C_ksq.sem, 1)

            def squares_q(ch, i, u):
                g, r = unit(u)
                act.wait_ge(C_vq.sem, C_vq.nth(i, u))
                for h in range(4):
                    last = nc.scalar.activation(C_[g]["qn"][:, h, :], PS[:, QBANK, h * P:(h + 1) * P], ACT.Square,
                                                accum_out=small[:, g, h:h + 1])
                last.then_inc(C_qsq.sem, 1)

            def v_out(ch, i, u):
                if brings_kv(u):
                    g, r = unit(u)
                    nc.scalar.activation(flat(C_[g]["v"][:, (r // 2) % 2]), PS[:, VBANK, :], ACT.Copy,
                                         scale=scalar[:, 3:4] if r < 4 else 1.0).then_inc(C_v.sem, 1)

            def k_T(ch, i, u):
                if brings_kv(u):
                    g, r = unit(u)
                    h = 4 * (r // 4) + 2
                    act.wait_ge(C_kturned.sem, C_kturned.nth(i, kv_at(u)))
                    nc.scalar.activation(flat(C_[g]["kT"]), PS[:, TBANK, :], ACT.Identity, scale=c_head[:, h:h + 1],
                                         bias=c_head[:, h + 1:h + 2]).then_inc(C_kT.sem, 1)

            def q_T(ch, i, u):
                g, r = unit(u)
                h = 4 * (r // 4)
                act.wait_ge(C_qturned.sem, C_qturned.nth(i, u))
                nc.scalar.activation(flat(C_[g]["qT"]), PS[:, TBANK, :], ACT.Identity, scale=c_head[:, h:h + 1],
                                     bias=c_head[:, h + 1:h + 2]).then_inc(C_qT.sem, 1)

            def exps(ch, i, u):
                g, r = unit(u)
                act.wait_ge(C_max.sem, C_max.nth(i, u))
                for h in range(4):
                    last = nc.scalar.activation(C_[g]["p"][:, h, :], PS[:, SBANK, h * P:(h + 1) * P], ACT.Exp, scale=DC ** -0.5,
                                                bias=small[:, g, 8 + h:9 + h], accum_out=small[:, g, 12 + h:13 + h])
                last.then_inc(C_exp.sem, 1)

            def p_T(ch, i, u):
                act.wait_ge(C_pturned.sem, C_pturned.nth(i, u))
                nc.scalar.copy(flat(C_[u % G]["pT"]), PS[:, PBANK, :]).then_inc(C_pT.sem, 1)

            def extra(ch, i, n):
                if n == 10 and not last_step(i):
                    feature_major(i + 1)

            C_pipeline(act, ch, lambda ch: feature_major(0), [(2, exps), (0, squares_k), (0, squares_q), (1, k_T), (0, v_out), (1, q_T), (3, p_T)],
                       extra)

        def C_tensor(pe):
            def turn_x(i):
                for g in range(G):
                    pe.wait_ge(xn_ready.sem, xn_ready.at(i, g))
                    for k in range(KC):
                        at = (g * KC + k) * P
                        last = nc.tensor.transpose(PS[:, VBANK, at:at + P], xn[:, g, k * P:(k + 1) * P], ident[:])
                    last.then_inc(xnT_done.sem, 1)

            def project(n, src, w, c0):
                for k in range(KC):
                    last = nc.tensor.matmul(PS[:, n, :], src(k), w[:, k, c0:c0 + 512], start=k == 0, stop=k == KC - 1)
                return last

            def projections(ch, i, u):
                g, r = unit(u)
                cross, quad, half = r // 4, (r // 2) % 2, r % 2
                x_of = lambda n: (lambda k: C_[g]["xs"][:, n, k, :])
                ctx_of = lambda k: ctxT[:, g, k, :]
                if r == 0:
                    pe.wait_ge(C_xs.sem, C_xs.nth(i, 8 * (u // UNITS) + 4 + g))
                if r == 4:
                    pe.wait_ge(C_xs.sem, C_xs.nth(i, 6 + g))
                    ctx_loaded(pe, i, g)
                if half == 0:
                    if u:
                        pe.wait_ge(C_kn.sem, C_kn.nth(i, kv_at(u) - 1))
                        pe.wait_ge(C_v.sem, C_v.nth(i, kv_at(u) - 1))
                    if u == 12 and not last_step(i):
                        pe.wait_ge(xT_ready.sem, xT_ready.at(i + 1, G - 1))
                    project(KBANK, ctx_of if cross else x_of(2), wC["kx" if cross else "k"], 512 * quad).then_inc(C_k.sem, 1)
                    last = project(VBANK, ctx_of if cross else x_of(3), wC["vx" if cross else "v"], 512 * quad)
                    if cross and quad:
                        last.then_inc(ctx_read[g], 1)
                if u:
                    pe.wait_ge(C_qn.sem, C_qn.nth(i, u - 1))
                project(QBANK, x_of(cross), wC["qx" if cross else "q"], 1024 * quad + 512 * half).then_inc(C_vq.sem, 1)

            def turn_k(ch, i, u):
                if brings_kv(u):
                    pe.wait_ge(C_kn.sem, C_kn.nth(i, kv_at(u)))
                    if u:
                        pe.wait_ge(C_qT.sem, C_qT.nth(i, u - 1))
                    for h in range(4):
                        last = nc.tensor.transpose(PS[:, TBANK, h * P:(h + 1) * P], C_[u % G]["kn"][:, h, :], ident[:])
                    last.then_inc(C_kturned.sem, 1)

            def turn_q(ch, i, u):
                if brings_kv(u):
                    pe.wait_ge(C_kT.sem, C_kT.nth(i, kv_at(u)))
                else:
                    pe.wait_ge(C_qT.sem, C_qT.nth(i, u - 1))
                pe.wait_ge(C_qn.sem, C_qn.nth(i, u))
                for h in range(4):
                    last = nc.tensor.transpose(PS[:, TBANK, h * P:(h + 1) * P], C_[u % G]["qn"][:, h, :], ident[:])
                last.then_inc(C_qturned.sem, 1)

            def scores(ch, i, u):
                g, r = unit(u)
                c = C_[g]
                pe.wait_ge(C_qT.sem, C_qT.nth(i, u))
                if u:
                    pe.wait_ge(C_exp.sem, C_exp.nth(i, u - 1))
                for h in range(4):
                    last = nc.tensor.matmul(PS[:, SBANK, h * P:(h + 1) * P], c["qT"][:, h, :], c["kT"][:, 2 * (r % 2) + h // 2, :],
                                            start=True, stop=True)
                last.then_inc(C_scores.sem, 1)

            def turn_p(ch, i, u):
                pe.wait_ge(C_p.sem, C_p.nth(i, u))
                if u:
                    pe.wait_ge(C_pT.sem, C_pT.nth(i, u - 1))
                for h in range(4):
                    last = nc.tensor.transpose(PS[:, PBANK, h * P:(h + 1) * P], C_[u % G]["p"][:, h, :], ident[:])
                last.then_inc(C_pturned.sem, 1)

            def weigh(ch, i, u):
                g, r = unit(u)
                c = C_[g]
                pe.wait_ge(C_pT.sem, C_pT.nth(i, u))
                pe.wait_ge(C_v.sem, C_v.nth(i, kv_at(u)))
                if u:
                    pe.wait_ge(C_cat.sem, C_cat.nth(i, u - 1))
                for h in range(2):
                    last = nc.tensor.matmul(PS[:, OBANK, h * D:(h + 1) * D], c["v"][:, (r // 2) % 2, 2 * (r % 2) + h, :],
                                            c["pT"][:, 2 * h:2 * h + 2, :].rearrange("p a b -> p (a b)"), start=True, stop=True)
                last.then_inc(C_o.sem, 1)

            def out(ch, i, u):
                g, r = unit(u)
                pe.wait_ge(C_cat.sem, C_cat.nth(i, u))
                if u % UNITS == 0:
                    pe.wait_ge(x_done.sem, x_done.nth(i, -1))
                for h in range(4):
                    last = nc.tensor.matmul(PS[:, OUTBANK, g * D:(g + 1) * D], C_[g]["cat"][:, h, :], wC["proj"][:, 4 * r + h, :],
                                            start=u % UNITS == 0 and h == 0, stop=u % UNITS == UNITS - 1 and h == 3)
                if u % UNITS == UNITS - 1:
                    last.then_inc(C_out.sem, 1)

            def extra(ch, i, n):
                if n == 10 and not last_step(i):
                    pe.wait_ge(C_v.sem, C_v.nth(i, kv_at(9)))
                    turn_x(i + 1)

            C_pipeline(pe, None, lambda ch: turn_x(0),
                       [(2, scores), (0, projections), (1, turn_k), (6, out), (3, turn_p), (1, turn_q), (4, weigh)], extra)

        LOOPS[2] = (None, C_tensor, C_scalar, C_gpsimd, C_vector)
        SUB.append((ctx_sync, None, None, None, None))
        HD_, DD = 16, 16
        n_ = 0
        wD = {}
        for name, a, w in (("q", KC, 512), ("k", KC, 512), ("v", KC, D), ("o", KC, D), ("a", KC, 16)):
            wD[name], n_ = view(early, n_, a, w)
            LOADS["3 attention"].append((wD[name], "D_" + name))
        wD["b"], n_ = view(early, n_, FF)
        LOADS["3 attention"].append((wD["b"][0:16, :], "D_b"))
        n_ = 0
        for name, a, w in (("in", KC, FF), ("up", KC, FF), ("down", FC, D)):
            wD[name], n_ = view(late, n_, a, w)
            LOADS[3].append((wD[name], "D_" + name))
        LATE_4 = n_
        D_col = sb("D_col", [P, 4])
        D_mask = sb("D_mask", [P, P])
        D_mask4 = sb("D_mask4", [P, 4, P], BF16)
        LOADS["3 attention"] += [(D_col[:], "D_col"), (D_mask[:], "D_mask")]
        eps6 = sb("eps6", [P, 1])
        x2T = sb("x2T", [P, KC, G, P])
        D_ = [{} for _ in range(G)]
        for g in range(G):
            w, n_ = work[:, g, :], 0
            D_[g]["p"], n_ = view(w, n_, 16, P)
            D_[g]["pT"], n_ = view(w, n_, 16, P)
            D_[g]["xb"], n_ = view(w, n_, D)
            D_[g]["v"], n_ = view(w, n_, D)
            D_[g]["o"], n_ = view(w, n_, D)
            D_[g]["qk"], n_ = view(w, n_, 4, D)
        n_ = 5888
        D_oT = sb("D_oT", [P, KC, G, P])
        D_aoT, _ = view(work[:, 0, :], 0, KC, G * P)
        D_mod, _ = view(work[:, 0, :], 512, D)
        D_prod, _ = view(work[:, 0, :], 768, D)
        D_silu, _ = view(work[:, 1, :], 0, FC, D)
        D_m, _ = view(work[:, 1, :], 2048, FC, D)
        D_ms = flag("D_ms")
        D_rstd2 = flag("D_rstd2")
        D_qkv = flag("D_qkv")
        D_qkvs = flag("D_qkvs")
        D_scores = flag("D_scores")
        D_max = flag("D_max")
        D_exp = flag("D_exp")
        D_pturned = flag("D_pturned")
        D_pT = flag("D_pT")
        D_pv = flag("D_pv")
        D_o = flag("D_o")
        D_oturned = flag("D_oturned")
        D_oTs = flag("D_oTs")
        D_ao = step_flag("D_ao")
        D_aos = step_flag("D_aos")
        D_ranks = step_flag("D_ranks")
        D_tanh = step_flag("D_tanh")
        D_prods = step_flag("D_prods")
        D_gate = step_flag("D_gate")
        D_silus = step_flag("D_silus")
        D_up = step_flag("D_up")
        D_ms_ready = step_flag("D_ms_ready")
        D_down = flag("D_down")
        D_prepared = sem("D_prepared")
        WEIGHT_USERS.update({(3, 4), (3, 2)})

        def D_before_vector(dve, ch):
            for n in range(4):
                last = nc.vector.tensor_copy(D_mask4[:, n, :], D_mask[:])
            ch.mark(last)
            nc.vector.memset(eps6[:], 1e-6).then_inc(D_prepared, 1)

        BEFORE[3, 4] = D_before_vector
        BEFORE[3, 1] = lambda pe, ch: pe.wait_ge(D_prepared, 1)
        BEFORE[3, 3] = lambda pool, ch: pool.wait_ge(D_prepared, 1)

        def D_vector(dve, ch, i):
            def again(g):
                nc.vector.tensor_tensor_reduce(D_[g]["xb"], xn[:, g, :], xn[:, g, :], 1.0 / D, 0.0, ALU.mult, ALU.add,
                                               moments[:, g, 1:2]).then_inc(D_ms.sem, 1)

            norm_vector(dve, ch, i, again)
            for g in range(G):
                dve.wait_ge(D_rstd2.sem, D_rstd2.at(i, g))
                nc.vector.tensor_scalar(D_[g]["xb"], xn[:, g, :], rstd[:, g, :], None, ALU.mult).then_inc(xn_ready.sem, 1)
            for g in range(G):
                dve.wait_ge(D_scores.sem, D_scores.at(i, g))
                mx = small[:, g, 0:16]
                s = PS[:, 4 * g:4 * g + 4, :].rearrange("p j (t k) -> p (j t) k", t=4)
                ch.link(nc.vector.tensor_reduce(mx, s, AX.X, ALU.max))
                nc.vector.tensor_scalar(mx, mx, -DD ** -0.5, None, ALU.mult).then_inc(D_max.sem, 1)
            for g in range(G):
                dve.wait_ge(D_pturned.sem, D_pturned.at(i, g))
                s = PS[:, 4 * g:4 * g + 4, :].rearrange("p j x -> p (j x)")
                nc.vector.tensor_copy(D_[g]["pT"].rearrange("p a b -> p (a b)"), s).then_inc(D_pT.sem, 1)
            for g in range(G):
                dve.wait_ge(D_pv.sem, D_pv.at(i, g))
                ch.link(nc.vector.reciprocal(small[:, g, 32:48], small[:, g, 16:32]))
                nc.vector.tensor_tensor(
                    D_[g]["o"].rearrange("p (t j d) -> p j t d", t=4, j=4),
                    bank(g, 0)[:, 0:D].rearrange("p (t j d) -> p j t d", t=4, j=4),
                    small[:, g, 32:48].rearrange("p (j t) -> p j t", j=4).unsqueeze(3).broadcast_to([P, 4, 4, DD]),
                    ALU.mult).then_inc(D_o.sem, 1)
            dve.wait_ge(D_tanh.sem, D_tanh.at(i))
            nc.vector.scalar_tensor_tensor(D_prod[0:16, :], D_mod[0:16, :], 0.1, bank(1, 2)[0:16, 0:D], ALU.mult, ALU.mult).then_inc(D_prods.sem, 1)
            dve.wait_ge(D_silus.sem, D_silus.at(i))
            dve.wait_ge(D_up.sem, D_up.at(i))
            nc.vector.tensor_tensor(D_m.rearrange("p a b -> p (a b)"), D_silu.rearrange("p a b -> p (a b)"),
                                    PS[:, 4:8, :].rearrange("p j x -> p (j x)"), ALU.mult).then_inc(D_ms_ready.sem, 1)
            for g in range(G):
                dve.wait_ge(D_down.sem, D_down.at(i, g))
                ch.link(nc.vector.tensor_tensor(D_[g]["o"], xn[:, g, :], bank(g, 0)[:, 0:D], ALU.add))
                add_to_x(dve, ch, i * G + g, D_[g]["o"], gates[:, 1, 1:2])

        def D_gpsimd(pool, ch, i):
            norm_gpsimd(pool, ch, i)
            for g in range(G):
                pool.wait_ge(D_ms.sem, D_ms.at(i, g))
                ch.link(nc.gpsimd.tensor_tensor(rstd[:, g, :], moments[:, g, 1:2], eps6[:], ALU.add))
                nc.gpsimd.tensor_tensor(rstd[:, g, :], rstd[:, g, :], minus_half[:, 0:1], ALU.pow).then_inc(D_rstd2.sem, 1)

        def D_scalar(act, ch, i):
            for g in range(G):
                act.wait_ge(xnT_done.sem, xnT_done.at(i, g))
                for m, dst in enumerate((xT, x2T)):
                    for k in range(KC):
                        last = nc.scalar.activation(dst[:, k, g, :], bank(g, 0)[:, k * P:(k + 1) * P], ACT.Copy,
                                                    scale=D_col[:, 2 * m + k:2 * m + k + 1])
                last.then_inc(xT_ready.sem, 1)
            for g in range(G):
                act.wait_ge(D_qkv.sem, D_qkv.at(i, g))
                nc.scalar.copy(D_[g]["v"], bank(g, 3)[:, 0:D])
                nc.scalar.copy(D_[g]["qk"].rearrange("p a b -> p (a b)"), banks(g, 1)).then_inc(D_qkvs.sem, 1)
            for g in range(G):
                act.wait_ge(D_max.sem, D_max.at(i, g))
                for n in range(16):
                    last = nc.scalar.activation(D_[g]["p"][:, n, :], bank(g, n // 4)[:, (n % 4) * P:(n % 4 + 1) * P], ACT.Exp,
                                                scale=DD ** -0.5, bias=small[:, g, n:n + 1], accum_out=small[:, g, 16 + n:17 + n])
                last.then_inc(D_exp.sem, 1)
            for g in range(G):
                act.wait_ge(D_oturned.sem, D_oturned.at(i, g))
                nc.scalar.copy(D_oT[:, :, g, :], bank(g, 1)[:, 0:D].rearrange("p (k t) -> p k t", k=KC)).then_inc(D_oTs.sem, 1)
            act.wait_ge(D_ao.sem, D_ao.at(i))
            nc.scalar.copy(D_aoT.rearrange("p a b -> p (a b)"), bank(0, 2)).then_inc(D_aos.sem, 1)
            act.wait_ge(D_ranks.sem, D_ranks.at(i))
            nc.scalar.activation(D_mod[0:16, :], bank(0, 3)[0:16, 0:D], ACT.Tanh).then_inc(D_tanh.sem, 1)
            act.wait_ge(D_gate.sem, D_gate.at(i))
            nc.scalar.activation(D_silu.rearrange("p a b -> p (a b)"), PS[:, 0:4, :].rearrange("p j x -> p (j x)"), ACT.Silu).then_inc(D_silus.sem, 1)

        def D_tensor(pe, i):
            for g in range(G):
                pe.wait_ge(xn_ready.sem, xn_ready.at(i, g))
                for k in range(KC):
                    last = nc.tensor.transpose(bank(g, 0)[:, k * P:(k + 1) * P], D_[g]["xb"][:, k * P:(k + 1) * P], ident[:])
                last.then_inc(xnT_done.sem, 1)
            pair = lambda src, k: src[:, k].rearrange("p g t -> p (g t)")
            for g in range(G):
                pe.wait_ge(xT_ready.sem, xT_ready.at(i, 1))
                for tt in range(4):
                    for k in range(KC):
                        nc.tensor.matmul(banks(g, 1)[:, tt * D:(tt + 1) * D], wD["qk"[g]][:, k, tt * P:(tt + 1) * P], pair(xT, k),
                                         start=k == 0, stop=k == KC - 1)
                for k in range(KC):
                    last = nc.tensor.matmul(bank(g, 3)[:, 0:D], xT[:, k, g, :], wD["v"][:, k, :], start=k == 0, stop=k == KC - 1)
                last.then_inc(D_qkv.sem, 1)
            for g in range(G):
                pe.wait_ge(D_qkvs.sem, D_qkvs.at(i, 1))
                for j in range(4):
                    nc.tensor.matmul(bank(g, j), ident_b[:], D_mask4[:].rearrange("p a b -> p (a b)"), start=True, stop=False)
                    rows_ = slice(32 * j, 32 * j + DD)
                    for tt in range(4):
                        last = nc.tensor.matmul(bank(g, j)[:, tt * P:(tt + 1) * P], D_[0]["qk"][rows_, tt, g * P:(g + 1) * P],
                                                D_[1]["qk"][rows_, tt, g * P:(g + 1) * P], start=False, stop=tt == 3)
                last.then_inc(D_scores.sem, 1)
            for g in range(G):
                pe.wait_ge(D_exp.sem, D_exp.at(i, g))
                for n in range(16):
                    last = nc.tensor.transpose(bank(g, n // 4)[:, (n % 4) * P:(n % 4 + 1) * P], D_[g]["p"][:, n, :], ident[:])
                last.then_inc(D_pturned.sem, 1)
            for g in range(G):
                pe.wait_ge(D_pT.sem, D_pT.at(i, g))
                for n in range(16):
                    h = 4 * (n % 4) + n // 4
                    last = nc.tensor.matmul(bank(g, 0)[:, h * DD:(h + 1) * DD], D_[g]["pT"][:, n, :], D_[g]["v"][:, h * DD:(h + 1) * DD],
                                            start=True, stop=True)
                last.then_inc(D_pv.sem, 1)
            for g in range(G):
                pe.wait_ge(D_o.sem, D_o.at(i, g))
                for k in range(KC):
                    last = nc.tensor.transpose(bank(g, 1)[:, k * P:(k + 1) * P], D_[g]["o"][:, k * P:(k + 1) * P], ident[:])
                last.then_inc(D_oturned.sem, 1)
            pe.wait_ge(D_oTs.sem, D_oTs.at(i, 1))
            for m in range(KC):
                for k in range(KC):
                    last = nc.tensor.matmul(bank(0, 2)[:, m * D:(m + 1) * D], wD["o"][:, k, m * P:(m + 1) * P], pair(D_oT, k),
                                            start=k == 0, stop=k == KC - 1)
            last.then_inc(D_ao.sem, 1)
            for k in range(KC):
                nc.tensor.matmul(bank(1, 2)[0:16, 0:D], wD["a"][:, k, :], pair(x2T, k), start=k == 0, stop=k == KC - 1)
            pe.wait_ge(D_aos.sem, D_aos.at(i))
            for k in range(KC):
                last = nc.tensor.matmul(bank(0, 3)[0:16, 0:D], wD["a"][:, k, :], D_aoT[:, k, :], start=k == 0, stop=k == KC - 1)
            last.then_inc(D_ranks.sem, 1)
            pe.wait_ge(D_prods.sem, D_prods.at(i))
            for f in range(FC):
                dst = bank(0, f // 2)[:, (f % 2) * D:(f % 2 + 1) * D]
                for k in range(KC):
                    nc.tensor.matmul(dst, wD["in"][:, k, f * P:(f + 1) * P], pair(x2T, k), start=k == 0, stop=False)
                last = nc.tensor.matmul(dst, wD["b"][0:16, f * P:(f + 1) * P], D_prod[0:16, :], start=False, stop=True)
            last.then_inc(D_gate.sem, 1)
            for f in range(FC):
                dst = bank(1, f // 2)[:, (f % 2) * D:(f % 2 + 1) * D]
                for k in range(KC):
                    last = nc.tensor.matmul(dst, wD["up"][:, k, f * P:(f + 1) * P], pair(x2T, k), start=k == 0, stop=k == KC - 1)
            last.then_inc(D_up.sem, 1)
            pe.wait_ge(D_ms_ready.sem, D_ms_ready.at(i))
            for g in range(G):
                for f in range(FC):
                    last = nc.tensor.matmul(bank(g, 0)[:, 0:D], D_m[:, f, g * P:(g + 1) * P], wD["down"][:, f, :],
                                            start=f == 0, stop=f == FC - 1)
                last.then_inc(D_down.sem, 1)

        SUB.append((None, D_tensor, D_scalar, D_gpsimd, D_vector))

        HE, DE, TE = 16, 16, 8
        ROWS = 64
        n_ = LATE_4
        wE = {}
        for name, a, w in (("q", KC, D), ("kv", KC, 2 * D), ("p", KC, D)):
            wE[name], n_ = view(late, n_, a, w)
            LOADS[4].append((wE[name], "E_" + name))
        E_bias, n_ = view(late, n_, 4 * D)
        LOADS[4].append((E_bias, "E_bias"))
        LATE_5 = n_
        E_kT, _ = view(early, 0, TE, NB * P, dt=BF16)
        E_vs = sb("E_vs", [P, 2, D])
        E_v, _ = view(work[:, 0, :], 4096, NB, D)
        E_vq, _ = view(work[:, 1, :], 5120, NB, D, dt=BF16)
        E_ = [{} for _ in range(G)]
        for g in range(G):
            w, n_ = work[:, g, :], 0
            E_[g]["stack"], n_ = view(w, n_, HE, 4, DE, dt=BF16)
            E_[g]["qT"], n_ = view(w, n_, TE, P, dt=BF16)
            E_[g]["t"], n_ = view(w, n_, D)
            E_[g]["u"], n_ = view(w, n_, D)
            E_[g]["e"], n_ = view(w, n_, 1024)
            E_[g]["pb"], n_ = view(w, n_, 1024, dt=BF16)
            E_[g]["pT"], n_ = view(w, n_, NB, P, dt=BF16)
            E_[g]["oT"], n_ = view(w, n_, KC, P)
        assert n_ <= 4096
        E_kv = flag("E_kv")
        E_kstack = flag("E_kstack")
        E_kturned = flag("E_kturned")
        E_kTs = flag("E_kTs")
        E_vmax = sem("E_vmax")
        E_vall = sem("E_vall")
        E_prepared = sem("E_prepared")
        E_q = flag("E_q")
        E_qstack = flag("E_qstack")
        E_qturned = flag("E_qturned")
        E_qTs = flag("E_qTs")
        E_scores = flag("E_scores", HE)
        E_max = flag("E_max", HE)
        E_exp = flag("E_exp", HE)
        E_pb = flag("E_pb", HE)
        E_pturned = flag("E_pturned", HE)
        E_pT = flag("E_pT", HE)
        E_pv = flag("E_pv", HE)
        E_o = flag("E_o")
        E_oturned = flag("E_oturned")
        E_oTs = flag("E_oTs")
        E_out = flag("E_out")
        WEIGHT_USERS.add((4, 4))
        heads16 = lambda v: v.rearrange("p (h d) -> p h d", h=16)
        over_d = lambda v: v.unsqueeze(2).broadcast_to([P, HE, DE])

        def E_before_sync(sp):
            with sp.Fori(0, STEPS) as i:
                ctx_sync(sp, i)
            ctx_base[0] += STEPS

        def E_before_tensor(pe, ch):
            pe.wait_ge(x_done.sem, 4 * NB)
            with pe.Fori(0, STEPS) as i:
                for g in range(G):
                    ctx_loaded(pe, i, g)
                    for k in range(KC):
                        last = nc.tensor.matmul(bank(g, 0), ctxT[:, g, k, :], wE["kv"][:, k, :], start=k == 0, stop=k == KC - 1)
                    last.then_inc(E_kv.sem, 1)
                for g in range(G):
                    pe.wait_ge(E_kstack.sem, E_kstack.at(i, g))
                    for tt in range(TE):
                        last = nc.tensor.transpose(bank(g, 1).bitcast(BF16)[:, tt * P:(tt + 1) * P],
                                                   E_[g]["stack"][:, 2 * tt:2 * tt + 2].rearrange("p a b c -> p (a b c)"), ident_b[:])
                        if tt == 0:
                            last.then_inc(ctx_read[g], 1)
                    last.then_inc(E_kturned.sem, 1)
            pe.wait_ge(E_prepared, 1)

        def E_before_scalar(act, ch):
            with act.Fori(0, STEPS) as i:
                for g in range(G):
                    b = i * G + g
                    act.wait_ge(E_kturned.sem, E_kturned.at(i, g))
                    nc.scalar.copy(E_kT.rearrange("p t (b k) -> p t b k", b=NB)[:, :, b, :],
                                   bank(g, 1).bitcast(BF16).rearrange("p (t k) -> p t k", t=TE)).then_inc(E_kTs.sem, 1)

        def step_of(ch, x, s, r):
            ch.link(nc.vector.tensor_reduce(s, heads16(x), AX.X, ALU.max, apply_absolute_value=True))
            ch.link(nc.vector.tensor_scalar(s, s, 1.0 / 127, 1e-8, ALU.mult, ALU.max))
            ch.link(nc.vector.reciprocal(r, s))

        def E_before_vector(dve, ch):
            for g in range(G):
                ch.mark(nc.vector.memset(E_[g]["stack"].rearrange("p a b c -> p (a b c)"), 0.0))
            ch.restart()
            with dve.Fori(0, STEPS) as i:
                for g in range(G):
                    b = i * G + g
                    e = E_[g]
                    dve.wait_ge(E_kv.sem, E_kv.at(i, g))
                    nc.vector.tensor_tensor(E_v[:, b, :], bank(g, 0)[:, D:2 * D], E_bias[:, 2 * D:3 * D], ALU.add)
                    ch.link(nc.vector.tensor_tensor(e["t"], bank(g, 0)[:, 0:D], E_bias[:, D:2 * D], ALU.add))
                    s, r = small[:, g, 0:16], small[:, g, 16:32]
                    step_of(ch, e["t"], s, r)
                    ch.link(nc.vector.tensor_tensor(heads16(e["t"]), heads16(e["t"]), over_d(r), ALU.mult))
                    ch.link(nc.vector.tensor_scalar(e["t"], e["t"], MAGIC, MAGIC, ALU.add, ALU.subtract))
                    ch.link(nc.vector.tensor_tensor(heads16(e["t"]), heads16(e["t"]), over_d(s), ALU.mult))
                    ch.link(nc.vector.tensor_copy(e["stack"][:, :, 0, :], heads16(e["t"])))
                    ch.link(nc.vector.tensor_tensor(heads16(e["u"]), heads16(e["t"]), e["stack"][:, :, 0, :], ALU.subtract))
                    ch.link(nc.vector.tensor_copy(e["stack"][:, :, 1, :], heads16(e["u"])))
                    nc.vector.tensor_tensor(e["stack"][:, :, 2, :], heads16(e["u"]), e["stack"][:, :, 1, :], ALU.subtract).then_inc(E_kstack.sem, 1)
                for g in range(G):
                    dve.wait_ge(E_kTs.sem, E_kTs.at(i, g))
                    ch.link(nc.vector.memset(E_[g]["stack"][:, 0, 3, :], 0.0))
                ch.restart()
            vm = E_vs[:, 1, :]
            nc.vector.tensor_reduce(vm, E_v.rearrange("p b d -> p d b"), AX.X, ALU.max, apply_absolute_value=True).then_inc(E_vmax, 1)
            dve.wait_ge(E_vall, 1)
            ch.link(nc.vector.tensor_scalar(E_vs[:, 0, :], E_vs[:, 0, :], 1.0 / 127, 1e-8, ALU.mult, ALU.max))
            ch.link(nc.vector.reciprocal(E_vs[:, 1, :], E_vs[:, 0, :]))
            ch.link(nc.vector.tensor_tensor(E_v, E_v, E_vs[:, 1, :].unsqueeze(1).broadcast_to([P, NB, D]), ALU.mult))
            nc.vector.tensor_scalar(E_vq, E_v, MAGIC, MAGIC, ALU.add, ALU.subtract).then_inc(E_prepared, 1)

        def E_before_gpsimd(pool, ch):
            pool.wait_ge(E_vmax, 1)
            nc.gpsimd.partition_all_reduce(E_vs[:, 0, :], E_vs[:, 1, :], P, bass.bass_isa.ReduceOp.max).then_inc(E_vall, 1)

        BEFORE.update({(4, 0): E_before_sync, (4, 1): E_before_tensor, (4, 2): E_before_scalar, (4, 3): E_before_gpsimd, (4, 4): E_before_vector})

        def E_tensor(pe, i):
            norm_tensor(pe, i)
            for g in range(G):
                pe.wait_ge(xT_ready.sem, xT_ready.at(i, g))
                for k in range(KC):
                    last = nc.tensor.matmul(bank(g, 1)[:, 0:D], xT[:, k, g, :], wE["q"][:, k, :], start=k == 0, stop=k == KC - 1)
                last.then_inc(E_q.sem, 1)
            for g in range(G):
                pe.wait_ge(E_qstack.sem, E_qstack.at(i, g))
                for tt in range(TE):
                    last = nc.tensor.transpose(bank(g, 0).bitcast(BF16)[:, tt * P:(tt + 1) * P],
                                               E_[g]["stack"][:, 2 * tt:2 * tt + 2].rearrange("p a b c -> p (a b c)"), ident_b[:])
                last.then_inc(E_qturned.sem, 1)

            def scores(u):
                h, g = divmod(u, G)
                if h == 0:
                    pe.wait_ge(E_qTs.sem, E_qTs.at(i, g))
                else:
                    pe.wait_ge(E_exp.sem, E_exp.nth(i, u - G))
                r = slice(ROWS * (h % 2), ROWS * (h % 2) + ROWS)
                for n in range(2):
                    last = nc.tensor.matmul(bank(g, 2 + n), E_[g]["qT"][r, h // 2, :], E_kT[r, h // 2, n * 512:(n + 1) * 512],
                                            start=True, stop=True)
                last.then_inc(E_scores.sem, 1)

            def turn(u):
                g = u % G
                pe.wait_ge(E_pb.sem, E_pb.nth(i, u))
                if u >= G:
                    pe.wait_ge(E_pT.sem, E_pT.nth(i, u - G))
                for b in range(NB):
                    last = nc.tensor.transpose(bank(g, 1).bitcast(BF16)[:, b * P:(b + 1) * P], E_[g]["pb"][:, b * P:(b + 1) * P], ident_b[:])
                last.then_inc(E_pturned.sem, 1)

            def weigh(u):
                h, g = divmod(u, G)
                pe.wait_ge(E_pT.sem, E_pT.nth(i, u))
                for b in range(NB):
                    last = nc.tensor.matmul(bank(g, 0)[:, h * DE:(h + 1) * DE], E_[g]["pT"][:, b, :], E_vq[:, b, h * DE:(h + 1) * DE],
                                            start=b == 0, stop=b == NB - 1)
                last.then_inc(E_pv.sem, 1)

            U = HE * G
            for u in range(G):
                scores(u)
            for u in range(U):
                if u + G < U:
                    scores(u + G)
                turn(u)
                if u >= 1:
                    weigh(u - 1)
            weigh(U - 1)
            for g in range(G):
                pe.wait_ge(E_o.sem, E_o.at(i, g))
                for k in range(KC):
                    last = nc.tensor.transpose(bank(g, 1)[:, k * P:(k + 1) * P], E_[g]["t"][:, k * P:(k + 1) * P], ident[:])
                last.then_inc(E_oturned.sem, 1)
            for g in range(G):
                pe.wait_ge(E_oTs.sem, E_oTs.at(i, g))
                for k in range(KC):
                    last = nc.tensor.matmul(bank(g, 2)[:, 0:D], E_[g]["oT"][:, k, :], wE["p"][:, k, :], start=k == 0, stop=k == KC - 1)
                last.then_inc(E_out.sem, 1)

        def E_scalar(act, ch, i):
            norm_scalar(act, i)
            for g in range(G):
                act.wait_ge(E_qturned.sem, E_qturned.at(i, g))
                nc.scalar.copy(E_[g]["qT"].rearrange("p a b -> p (a b)"), bank(g, 0).bitcast(BF16)).then_inc(E_qTs.sem, 1)

            def turn(u):
                g = u % G
                act.wait_ge(E_pturned.sem, E_pturned.nth(i, u))
                if u >= G:
                    act.wait_ge(E_pv.sem, E_pv.nth(i, u - G))
                nc.scalar.copy(E_[g]["pT"].rearrange("p a b -> p (a b)"), bank(g, 1).bitcast(BF16)).then_inc(E_pT.sem, 1)

            for u in range(HE * G):
                h, g = divmod(u, G)
                act.wait_ge(E_max.sem, E_max.nth(i, u))
                if u >= G:
                    act.wait_ge(E_pb.sem, E_pb.nth(i, u - G))
                nc.scalar.activation(E_[g]["e"], banks(g, 2), ACT.Exp, scale=small[:, g, h:h + 1],
                                     bias=small[:, g, 48 + h:49 + h], accum_out=small[:, g, 64 + h:65 + h]).then_inc(E_exp.sem, 1)
                if u >= 1:
                    turn(u - 1)
            turn(HE * G - 1)
            for g in range(G):
                act.wait_ge(E_oturned.sem, E_oturned.at(i, g))
                nc.scalar.copy(E_[g]["oT"].rearrange("p a b -> p (a b)"), bank(g, 1)[:, 0:D]).then_inc(E_oTs.sem, 1)

        def E_vector(dve, ch, i):
            norm_vector(dve, ch, i)
            for g in range(G):
                e = E_[g]
                dve.wait_ge(E_q.sem, E_q.at(i, g))
                ch.link(nc.vector.tensor_tensor(e["t"], bank(g, 1)[:, 0:D], E_bias[:, 0:D], ALU.add))
                ch.link(nc.vector.tensor_scalar(e["t"], e["t"], DE ** -0.5, None, ALU.mult))
                s, r = small[:, g, 0:16], small[:, g, 16:32]
                step_of(ch, e["t"], s, r)
                ch.link(nc.vector.tensor_scalar(small[:, g, 32:48], s, -1.0, None, ALU.mult))
                ch.link(nc.vector.tensor_tensor(heads16(e["u"]), heads16(e["t"]), over_d(r), ALU.mult))
                for part in range(3):
                    last = nc.vector.tensor_scalar(e["stack"][:, :, part, :], heads16(e["u"]), MAGIC, MAGIC, ALU.add, ALU.subtract)
                last.then_inc(E_qstack.sem, 1)

            def maximum(h, g):
                dve.wait_ge(E_scores.sem, E_scores.at(i, g, h))
                ch.link(nc.vector.tensor_reduce(small[:, g, 80:81], banks(g, 2), AX.X, ALU.max))
                nc.vector.tensor_scalar(small[:, g, 48 + h:49 + h], small[:, g, 80:81], small[:, g, 32 + h:33 + h],
                                        5.541263545158426, ALU.mult, ALU.add).then_inc(E_max.sem, 1)

            for u in range(G):
                maximum(0, u)
            for u in range(HE * G):
                h, g = divmod(u, G)
                dve.wait_ge(E_exp.sem, E_exp.nth(i, u))
                if u >= G:
                    dve.wait_ge(E_pturned.sem, E_pturned.nth(i, u - G))
                nc.vector.tensor_scalar(E_[g]["pb"], E_[g]["e"], MAGIC, MAGIC, ALU.add, ALU.subtract).then_inc(E_pb.sem, 1)
                if h + 1 < HE:
                    maximum(h + 1, g)
            for g in range(G):
                e = E_[g]
                dve.wait_ge(E_pv.sem, E_pv.at(i, g, HE - 1))
                ch.link(nc.vector.reciprocal(small[:, g, 16:32], small[:, g, 64:80]))
                ch.link(nc.vector.tensor_tensor(heads16(e["t"]), heads16(bank(g, 0)[:, 0:D]), over_d(small[:, g, 16:32]), ALU.mult))
                nc.vector.tensor_tensor(e["t"], e["t"], E_vs[:, 0, :], ALU.mult).then_inc(E_o.sem, 1)
            for g in range(G):
                dve.wait_ge(E_out.sem, E_out.at(i, g))
                ch.link(nc.vector.tensor_tensor(E_[g]["u"], bank(g, 2)[:, 0:D], E_bias[:, 3 * D:4 * D], ALU.add))
                add_to_x(dve, ch, i * G + g, E_[g]["u"], gates[:, 0, 2:3])

        SUB.append((None, E_tensor, E_scalar, B_gpsimd, E_vector))

        NE = 8
        n_ = LATE_5
        wF = {}
        for name, a, w in (("gate", KC, NE), ("w1", KC, NE * P), ("w2", NE, D), ("sw1", KC, D), ("sw2", KC, D)):
            wF[name], n_ = view(late, n_, a, w)
            LOADS[5].append((wF[name], "F_" + name))
        wF["b2"], n_ = view(late, n_, D)
        wF["sb2"], n_ = view(late, n_, D)
        LOADS[5] += [(wF["b2"][0:NE, :], "F_b2"), (wF["sb2"][0:1, :], "F_sb2")]
        LATE_6 = n_
        F_col = sb("F_col", [P, 10])
        LOADS[5].append((F_col[:], "F_col"))
        F_h, _ = view(work[:, 0, :], 0, 10, D)
        F_ = [{} for _ in range(G)]
        for g in range(G):
            w, n_ = work[:, g, :], 2560
            F_[g]["acc"], n_ = view(w, n_, D)
            F_[g]["gT"], n_ = view(w, n_, P)
        F_logits = flag("F_logits")
        F_diff = flag("F_diff")
        F_ratio = flag("F_ratio")
        F_gates = flag("F_gates")
        F_gturned = flag("F_gturned")
        F_gTs = flag("F_gTs")
        F_hidden = step_flag("F_hidden", 5)
        F_hs = step_flag("F_hs", 5)
        F_shared = flag("F_shared")
        F_expert = flag("F_expert", 4)
        F_added = flag("F_added", 4)
        BIG = 3.0e38
        WEIGHT_USERS.add((5, 2))

        def F_vector(dve, ch, i):
            norm_vector(dve, ch, i)
            lo = [small[:, g, 0:8] for g in range(G)]
            top = [small[:, g, 8:16] for g in range(G)]
            look = [small[:, g, 16:32] for g in range(G)]
            rest = [small[:, g, 32:48] for g in range(G)]
            one = [small[:, g, 48:56] for g in range(G)]
            for g in range(G):
                dve.wait_ge(F_logits.sem, F_logits.at(i, g))
                nc.vector.memset(look[g], -BIG)
                ch.link(nc.vector.tensor_copy(lo[g], bank(g, 1)[:, 0:NE]))
                ch.link(nc.vector.max(top[g], lo[g]))
                for n in range(2):
                    last = nc.vector.tensor_copy(look[g][:, 8 * n:8 * n + 1], top[g][:, n:n + 1])
                ch.link(last)
                last = nc.vector.tensor_tensor(small[:, g, 56:57], top[g][:, 1:2], top[g][:, 0:1], ALU.subtract)
                last.then_inc(F_diff.sem, 1)
                ch.link(nc.vector.match_replace(rest[g][:, 0:8], look[g][:, 0:8], lo[g], BIG))
                ch.link(nc.vector.match_replace(rest[g][:, 8:16], look[g][:, 8:16], rest[g][:, 0:8], BIG))
            for g in range(G):
                dve.wait_ge(F_ratio.sem, F_ratio.at(i, g))
                e, s = small[:, g, 57:58], small[:, g, 58:59]
                ch.link(nc.vector.tensor_scalar(s, e, 1.0, None, ALU.add))
                ch.link(nc.vector.reciprocal(s, s))
                ch.link(nc.vector.tensor_tensor(small[:, g, 59:60], e, s, ALU.mult))
                ch.link(nc.vector.tensor_single_scalar(one[g], rest[g][:, 0:8], BIG, ALU.is_equal))
                ch.link(nc.vector.tensor_single_scalar(lo[g], rest[g][:, 8:16], BIG, ALU.is_equal))
                ch.link(nc.vector.tensor_tensor(lo[g], lo[g], one[g], ALU.subtract))
                ch.link(nc.vector.tensor_scalar(lo[g], lo[g], small[:, g, 59:60], None, ALU.mult))
                nc.vector.scalar_tensor_tensor(lo[g], one[g], s, lo[g], ALU.mult, ALU.add).then_inc(F_gates.sem, 1)
            for g in range(G):
                dve.wait_ge(F_shared.sem, F_shared.at(i, g))
                ch.link(nc.vector.tensor_copy(F_[g]["acc"], bank(g, 0)[:, 0:D]))
            for n in range(4):
                for g in range(G):
                    acc = F_[g]["acc"]
                    dve.wait_ge(F_expert.sem, F_expert.at(i, g, n))
                    for m in range(2):
                        last = nc.vector.scalar_tensor_tensor(acc, bank(g, 2 + n % 2)[:, m * D:(m + 1) * D], lo[g][:, 2 * n + m:2 * n + m + 1],
                                                              acc, ALU.mult, ALU.add)
                        if m == 0:
                            ch.link(last)
                    last.then_inc(F_added.sem, 1)
                    dve.wait_ge(F_added.sem, F_added.at(i, g, n))
            for g in range(G):
                add_to_x(dve, ch, i * G + g, F_[g]["acc"], gates[:, 1, 2:3])

        def F_scalar(act, ch, i):
            norm_scalar(act, i)
            for g in range(G):
                act.wait_ge(F_diff.sem, F_diff.at(i, g))
                nc.scalar.activation(small[:, g, 57:58], small[:, g, 56:57], ACT.Exp).then_inc(F_ratio.sem, 1)
            for n in range(5):
                act.wait_ge(F_hidden.sem, F_hidden.at(i, n))
                for m in range(2):
                    last = nc.scalar.activation(F_h[:, 2 * n + m, :], HIDDEN[n % 4][:, m * D:(m + 1) * D], ACT.Gelu,
                                                bias=F_col[:, 2 * n + m:2 * n + m + 1])
                last.then_inc(F_hs.sem, 1)
            for g in range(G):
                act.wait_ge(F_gturned.sem, F_gturned.at(i, g))
                nc.scalar.copy(F_[g]["gT"][0:NE, :], bank(g, 1)[0:NE, 0:P]).then_inc(F_gTs.sem, 1)

        HIDDEN = [bank(0, 2), bank(0, 3), bank(1, 2), bank(1, 3)]

        def F_tensor(pe, i):
            norm_tensor(pe, i)
            for g in range(G):
                pe.wait_ge(xT_ready.sem, xT_ready.at(i, g))
                for k in range(KC):
                    last = nc.tensor.matmul(bank(g, 1)[:, 0:NE], xT[:, k, g, :], wF["gate"][:, k, :], start=k == 0, stop=k == KC - 1)
                last.then_inc(F_logits.sem, 1)
            for n in range(5):
                if n == 4:
                    pe.wait_ge(F_hs.sem, F_hs.at(i, 0))
                for m in range(2):
                    e = 2 * n + m
                    w = wF["w1"][:, :, e * P:(e + 1) * P] if n < 4 else wF["sw1"][:, :, m * P:(m + 1) * P]
                    for k in range(KC):
                        last = nc.tensor.matmul(HIDDEN[n % 4][:, m * D:(m + 1) * D], w[:, k, :], xT[:, k].rearrange("p g t -> p (g t)"),
                                                start=k == 0, stop=k == KC - 1)
                last.then_inc(F_hidden.sem, 1)
            for g in range(G):
                pe.wait_ge(F_gates.sem, F_gates.at(i, g))
                nc.tensor.transpose(bank(g, 1)[0:NE, 0:P], small[:, g, 0:8], ident[:]).then_inc(F_gturned.sem, 1)
            pe.wait_ge(F_hs.sem, F_hs.at(i, 4))
            for g in range(G):
                pe.wait_ge(F_gTs.sem, F_gTs.at(i, g))
                out_ = bank(g, 0)[:, 0:D]
                for m in range(2):
                    nc.tensor.matmul(out_, F_h[:, 8 + m, g * P:(g + 1) * P], wF["sw2"][:, m, :], start=m == 0, stop=False)
                nc.tensor.matmul(out_, ones[0:1, :], wF["sb2"][0:1, :], start=False, stop=False)
                nc.tensor.matmul(out_, F_[g]["gT"][0:NE, :], wF["b2"][0:NE, :], start=False, stop=True).then_inc(F_shared.sem, 1)
            for n in range(4):
                for g in range(G):
                    if n >= 2:
                        pe.wait_ge(F_added.sem, F_added.at(i, g, n - 2))
                    for m in range(2):
                        e = 2 * n + m
                        last = nc.tensor.matmul(bank(g, 2 + n % 2)[:, m * D:(m + 1) * D], F_h[:, e, g * P:(g + 1) * P], wF["w2"][:, e, :],
                                                start=True, stop=True)
                    last.then_inc(F_expert.sem, 1)

        SUB.append((None, F_tensor, F_scalar, B_gpsimd, F_vector))

        LATE_7 = LATE_6
        G_mask8 = sb("G_mask8", [P, NB * P], U8)
        G_on, n_ = view(work[:, 0, :], 4096, NB, P)
        G_off, n_ = view(work[:, 0, :], n_, NB, P)
        LOADS[6].append((G_mask8[:], "G_mask"))
        G_valid = sb("G_valid", [P, NB])
        G_ = [{} for _ in range(G)]
        for g in range(G):
            w, n_ = work[:, g, :], 0
            G_[g]["v"], n_ = view(w, n_, D)
            G_[g]["s"], n_ = view(w, n_, P)
            G_[g]["p"], n_ = view(w, n_, P)
            G_[g]["pT"], n_ = view(w, n_, P)
        v_in = [sem(f"v_in{g}") for g in range(G)]
        G_scores = flag("G_scores")
        G_max = flag("G_max")
        G_exp = flag("G_exp")
        G_pturned = flag("G_pturned")
        G_pT = flag("G_pT")
        G_o = flag("G_o")
        WEIGHT_USERS.add((6, 4))

        def G_before_vector(dve, ch):
            flat = lambda v: v.rearrange("p a b -> p (a b)")
            ch.link(nc.vector.tensor_copy(flat(G_on), G_mask8[:]))
            ch.mark(nc.vector.tensor_scalar(flat(G_off), flat(G_on), 1.0, -NEG, ALU.subtract, ALU.mult))
            ch.mark(nc.vector.tensor_reduce(G_valid[:], G_on, AX.X, ALU.max))

        BEFORE[6, 4] = G_before_vector

        def G_sync(sp, i):
            sp.wait_ge(x_done.sem, i * G + 6 * NB)
            for g in range(G):
                b = i * G + g
                sp.dma_start(ctxT[:, g], t["ctxT"][:, :, b, :]).then_inc(ctx_in[g], 16)
                sp.dma_start(G_[g]["v"], t["ctx"][:, b, :]).then_inc(v_in[g], 16)

        def G_vector(dve, ch, i):
            norm_vector(dve, ch, i)
            for g in range(G):
                b = i * G + g
                dve.wait_ge(G_scores.sem, G_scores.at(i, g))
                s, mx = G_[g]["s"], small[:, g, 0:1]
                ch.link(nc.vector.scalar_tensor_tensor(s, bank(g, 1)[:, 0:P], 1.0 / 16, G_on[:, b, :], ALU.mult, ALU.mult))
                ch.link(nc.vector.tensor_tensor(s, s, G_off[:, b, :], ALU.add))
                nc.vector.tensor_reduce(mx, s, AX.X, ALU.max, negate=True).then_inc(G_max.sem, 1)
            for g in range(G):
                b = i * G + g
                dve.wait_ge(G_exp.sem, G_exp.at(i, g))
                r = small[:, g, 2:3]
                ch.link(nc.vector.reciprocal(r, small[:, g, 1:2]))
                ch.link(nc.vector.tensor_scalar(r, r, gates[:, 0, 3:4], None, ALU.mult))
                ch.link(nc.vector.tensor_tensor(r, r, G_valid[:, bass.ds(b, 1)], ALU.mult))
            for g in range(G):
                dve.wait_ge(G_o.sem, G_o.at(i, g))
                add_to_x(dve, ch, i * G + g, bank(g, 2)[:, 0:D], small[:, g, 2:3])

        def G_scalar(act, ch, i):
            norm_scalar(act, i)
            for g in range(G):
                act.wait_ge(G_max.sem, G_max.at(i, g))
                nc.scalar.activation(G_[g]["p"], G_[g]["s"], ACT.Exp, bias=small[:, g, 0:1], accum_out=small[:, g, 1:2]).then_inc(G_exp.sem, 1)
            for g in range(G):
                act.wait_ge(G_pturned.sem, G_pturned.at(i, g))
                nc.scalar.copy(G_[g]["pT"], bank(g, 1)[:, 0:P]).then_inc(G_pT.sem, 1)

        def G_tensor(pe, i):
            norm_tensor(pe, i)
            for g in range(G):
                ctx_loaded(pe, i, g)
                pe.wait_ge(v_in[g], i * 16 + 16)
                pe.wait_ge(xT_ready.sem, xT_ready.at(i, g))
                for k in range(KC):
                    last = nc.tensor.matmul(bank(g, 1)[:, 0:P], xT[:, k, g, :], ctxT[:, g, k, :], start=k == 0, stop=k == KC - 1)
                last.then_inc(G_scores.sem, 1)
            for g in range(G):
                pe.wait_ge(G_exp.sem, G_exp.at(i, g))
                nc.tensor.transpose(bank(g, 1)[:, 0:P], G_[g]["p"], ident[:]).then_inc(G_pturned.sem, 1)
            for g in range(G):
                pe.wait_ge(G_pT.sem, G_pT.at(i, g))
                nc.tensor.matmul(bank(g, 2)[:, 0:D], G_[g]["pT"], G_[g]["v"], start=True, stop=True).then_inc(G_o.sem, 1)

        SUB.append((G_sync, G_tensor, G_scalar, B_gpsimd, G_vector))

        n_ = LATE_7
        wH = {}
        for name, a, w in (("up", KC, FF), ("gate", KC, FF), ("down", FC, D)):
            wH[name], n_ = view(late, n_, a, w)
            LOADS[7].append((wH[name], "H_" + name))
        H_row, n_ = view(late, n_, D)
        LOADS[7].append((H_row, "H_row"))
        assert n_ <= 24576
        H_col = sb("H_col", [P, 26])
        LOADS[7].append((H_col[:], "H_col"))
        H_up = sb("H_up", [P, FC])
        H_gate = sb("H_gate", [P, FC])
        H_rT, _ = view(work[:, 0, :], 0, KC, D)
        H_silu, _ = view(work[:, 0, :], 512, FC, D)
        H_h, _ = view(work[:, 0, :], 2560, FC, D)
        H_h2, _ = view(work[:, 1, :], 0, FC, D)
        H_yT, _ = view(work[:, 1, :], 2048, FC, D)
        H_t = [view(work[:, g, :], 4608, D)[0] for g in range(G)]
        H_rot = step_flag("H_rot")
        H_rTs = step_flag("H_rTs")
        H_gates = step_flag("H_gates")
        H_ups = step_flag("H_ups")
        H_silus = step_flag("H_silus")
        H_hs = step_flag("H_hs")
        H_turned = step_flag("H_turned")
        H_yTs = step_flag("H_yTs")
        H_down = flag("H_down")
        WEIGHT_USERS.update({(7, 4), (7, 2)})
        H_prepared = sem("H_prepared")

        def H_before_vector(dve, ch):
            ch.link(nc.vector.tensor_scalar(H_up[:], H_col[:, 10:18], 64.0, None, ALU.mult))
            ch.mark(nc.vector.tensor_tensor(H_up[:], H_up[:], H_col[:, 2:10], ALU.mult))
            ch.mark(nc.vector.tensor_scalar(H_gate[:], H_col[:, 18:26], 64.0, None, ALU.mult))
            nc.vector.tensor_scalar(H_row, H_row, 64.0, None, ALU.mult).then_inc(H_prepared, 1)

        BEFORE[7, 4] = H_before_vector
        BEFORE[7, 2] = lambda act, ch: act.wait_ge(H_prepared, 1)
        BEFORE[7, 1] = lambda pe, ch: pe.wait_ge(H_prepared, 1)
        all4 = lambda g: PS[:, 4 * g:4 * g + 4, :].rearrange("p j x -> p (j x)")

        def H_vector(dve, ch, i):
            norm_vector(dve, ch, i)
            dve.wait_ge(H_silus.sem, H_silus.at(i))
            dve.wait_ge(H_ups.sem, H_ups.at(i))
            for f in range(FC):
                last = nc.vector.scalar_tensor_tensor(H_h[:, f, :], all4(1)[:, f * D:(f + 1) * D], H_up[:, f:f + 1], H_silu[:, f, :],
                                                      ALU.mult, ALU.mult)
            ch.link(last)
            h, h2 = H_h, H_h2
            for s in (4, 2, 1):
                a = h.rearrange("p (o two s) d -> p o two (s d)", two=2, s=s)
                b = h2.rearrange("p (o two s) d -> p o two (s d)", two=2, s=s)
                nc.vector.tensor_tensor(b[:, :, 0, :], a[:, :, 0, :], a[:, :, 1, :], ALU.add)
                sub = nc.vector.tensor_tensor(b[:, :, 1, :], a[:, :, 0, :], a[:, :, 1, :], ALU.subtract)
                if s == 1:
                    sub.then_inc(H_hs.sem, 1)
                else:
                    ch.link(sub)
                h, h2 = h2, h
            for g in range(G):
                dve.wait_ge(H_down.sem, H_down.at(i, g))
                ch.link(nc.vector.tensor_tensor(H_t[g], bank(1, g)[:, 0:D], H_row, ALU.mult))
                add_to_x(dve, ch, i * G + g, H_t[g], gates[:, 1, 3:4])

        def H_scalar(act, ch, i):
            for g in range(G):
                act.wait_ge(xnT_done.sem, xnT_done.at(i, g))
                for k in range(KC):
                    last = nc.scalar.activation(xT[:, k, g, :], bank(g, 0)[:, k * P:(k + 1) * P], ACT.Copy, scale=H_col[:, k:k + 1])
                last.then_inc(xT_ready.sem, 1)
            act.wait_ge(H_rot.sem, H_rot.at(i))
            nc.scalar.activation(H_rT.rearrange("p a b -> p (a b)"), bank(0, 1), ACT.Copy, scale=1.0 / (16 * 64)).then_inc(H_rTs.sem, 1)
            act.wait_ge(H_gates.sem, H_gates.at(i))
            for f in range(FC):
                last = nc.scalar.activation(H_silu[:, f, :], all4(0)[:, f * D:(f + 1) * D], ACT.Silu, scale=H_gate[:, f:f + 1])
            last.then_inc(H_silus.sem, 1)
            act.wait_ge(H_turned.sem, H_turned.at(i))
            nc.scalar.activation(H_yT.rearrange("p a b -> p (a b)"), all4(0), ACT.Copy, scale=1.0 / (32 * 64)).then_inc(H_yTs.sem, 1)

        def H_tensor(pe, i):
            norm_tensor(pe, i)
            pe.wait_ge(xT_ready.sem, xT_ready.at(i, 1))
            for m in range(KC):
                for k in range(KC):
                    last = nc.tensor.matmul(bank(0, 1)[:, m * D:(m + 1) * D], had256[:, k, m * P:(m + 1) * P],
                                            xT[:, k].rearrange("p g t -> p (g t)"), start=k == 0, stop=k == KC - 1)
            last.then_inc(H_rot.sem, 1)
            pe.wait_ge(H_rTs.sem, H_rTs.at(i))
            for n, (name, done) in enumerate((("gate", H_gates), ("up", H_ups))):
                for f in range(FC):
                    for k in range(KC):
                        last = nc.tensor.matmul(all4(n)[:, f * D:(f + 1) * D], wH[name][:, k, f * P:(f + 1) * P], H_rT[:, k, :],
                                                start=k == 0, stop=k == KC - 1)
                last.then_inc(done.sem, 1)
            pe.wait_ge(H_hs.sem, H_hs.at(i))
            for n in range(4):
                last = nc.tensor.matmul(bank(0, n), had128[:], H_h2[:, 2 * n:2 * n + 2, :].rearrange("p a b -> p (a b)"), start=True, stop=True)
            last.then_inc(H_turned.sem, 1)
            pe.wait_ge(H_yTs.sem, H_yTs.at(i))
            for g in range(G):
                for f in range(FC):
                    last = nc.tensor.matmul(bank(1, g)[:, 0:D], H_yT[:, f, g * P:(g + 1) * P], wH["down"][:, f, :],
                                            start=f == 0, stop=f == FC - 1)
                last.then_inc(H_down.sem, 1)

        SUB.append((None, H_tensor, H_scalar, B_gpsimd, H_vector))

        for n in range(8):
            weights_sent[n] = 16 * len(LOADS[n])
        weights_sent[2] += 16
        weights_sent[3] += 16 * len(LOADS["3 attention"])
        block = ctx.enter_context(nc.Block())

        @block.sync
        def _(sp):
            def const(dst, src):
                sp.dma_start(dst, src).then_inc(const_in, 16)

            sp.dma_start(X[:], t["x"]).then_inc(x_in, 16)
            load_weights(sp, 0)
            const(gates[:], t["gates"].rearrange("(o a) b -> o a b", o=1).broadcast_to([P, 2, 4]))
            const(had256[:], t["had256"])
            const(had128[:], t["had128"])
            ctx_base[0] = 0
            ctx_sync(sp, 0)
            load_weights(sp, 1)
            ctx_sync(sp, 1)
            load_weights(sp, 2)
            for n, (f, *_) in enumerate(SUB[:layers]):
                if n == 2:
                    sp.wait_ge(B_quantised, 1)
                    sp.dma_start(wC["proj"], t["C_proj"]).then_inc(weights_in[2], 16)
                if n in LOAD_AT:
                    for m, prior in LOAD_AT[n]:
                        if (3 if m == "3 attention" else m) < layers:
                            sp.wait_ge(x_done.sem, NB * (prior + 1))
                            load_weights(sp, m)
                if (n, 0) in BEFORE:
                    BEFORE[n, 0](sp)
                if f is None:
                    continue
                with sp.Fori(0 if n else 2, STEPS) as i:
                    f(sp, i)
                ctx_base[0] += STEPS
            sp.wait_ge(x_done.sem, NB * layers)
            sp.dma_start(out, X[:]).then_inc(out_stored, 16)
            sp.wait_ge(out_stored, 16)

        def run(eng, chain_sem, which):
            for f in shared:
                f.base = 0
            ctx_base[0] = 0
            ch = Chain(eng, chain_sem) if chain_sem is not None else None
            for n, fs in enumerate(SUB[:layers]):
                if weights_sent[n] and which == 1 or (n, which) in WEIGHT_USERS:
                    eng.wait_ge(weights_in[n], weights_sent[n])
                if (n, which) in BEFORE:
                    BEFORE[n, which](eng, ch)
                    if ch:
                        ch.restart()
                if (n, 0) in BEFORE:
                    ctx_base[0] += STEPS
                if n in LOOPS and ch:
                    LOOPS[n][which](eng, ch)
                    ch.restart()
                elif n in LOOPS:
                    LOOPS[n][which](eng)
                else:
                  with eng.Fori(0, STEPS) as i:
                    if ch:
                        fs[which](eng, ch, i)
                        ch.restart()
                    else:
                        fs[which](eng, i)
                for f in shared:
                    f.base += NB
                if fs[0] is not None:
                    ctx_base[0] += STEPS

        @block.gpsimd
        def _(pool):
            nc.gpsimd.memset(ident[:], 0.0).then_inc(pool_order, 1)
            nc.gpsimd.memset(minus_half[:], -0.5).then_inc(pool_order, 1)
            nc.gpsimd.memset(eps5[:], 1e-5).then_inc(pool_order, 1)
            nc.gpsimd.memset(ones[:], 1.0).then_inc(pool_order, 1)
            pool.wait_ge(pool_order, 4)
            nc.gpsimd.affine_select(out=ident[:], in_=ident[:], compare_op=ALU.not_equal, fill=1.0, base=0,
                                    pattern=[[-1, P]], channel_multiplier=1).then_inc(pool_order, 1)
            pool.wait_ge(pool_order, 5)
            nc.gpsimd.tensor_copy(ident_b[:], ident[:]).then_inc(ident_ready, 1)
            pool.sem_clear(pool_order)
            run(pool, pool_order, 3)

        @block.scalar
        def _(act):
            act.wait_ge(const_in, 48)
            nc.scalar.activation(gates[:], gates[:], ACT.Tanh).then_inc(gates_ready, 1)
            run(act, act_order, 2)

        @block.tensor
        def _(pe):
            for g in range(G):
                pe.sem_inc(ctx_read[g], 1)
            pe.wait_ge(ident_ready, 1)
            pe.wait_ge(const_in, 48)
            run(pe, None, 1)

        @block.vector
        def _(dve):
            dve.wait_ge(x_in, 16)
            dve.wait_ge(gates_ready, 1)
            run(dve, dve_order, 4)


def rows(w):
    k, n = w.shape
    return w.reshape(k // P, P, n).transpose(1, 0, 2)


def hadamard(n):
    import numpy as np
    h = np.ones((1, 1), np.float32)
    while h.shape[0] < n:
        h = np.block([[h, h], [h, -h]])
    return h.astype(np.float32)


def lay_out(i):
    import numpy as np
    a = {k: np.asarray(v) for k, v in i.items()}
    ctxs = a["ctx_2048"]
    r = {
        "x": a["x"].transpose(1, 0, 2),
        "ctxT": ctxs.transpose(2, 0, 1).reshape(KC, P, NB, P).transpose(1, 0, 2, 3),
        "gates": np.stack([a["g_xattn"], a["g_ffn"]]),
        "had256": rows(hadamard(D)),
        "had128": hadamard(P),
    }
    kv = np.concatenate([a["L0_xattn_Wk"], a["L0_xattn_Wv"]])
    r["A_q"] = rows(a["L0_xattn_Wq"].T)
    r["A_kv"] = rows(np.concatenate([kv[0::2], kv[1::2]]).T)
    r["B_gate"] = rows(a["L0_ffn_w_gate"].T)
    r["B_up"] = rows(a["L0_ffn_w_up"].T)
    r["B_down"] = rows(a["L0_ffn_w_down"].T)
    L = "L1_xattn_"
    for n, w in (("q", "wq"), ("qx", "wqx"), ("k", "wk"), ("v", "wv"), ("proj", "wproj")):
        r["C_" + n] = rows(a[L + w].T)
    for n, w in zip(("kx", "vx"), np.split(a[L + "w_kv_x"], 2)):
        r["C_" + n] = rows(w.T)
    col = lambda v: v.reshape(-1, P).T
    r["C_col"] = np.concatenate([col(a[L + n]) for n in (
        "ln_w", "ln_b", "q_in_scale", "qx_in_scale", "k_in_scale", "v_in_scale",
        "qln_w", "qln_b", "kln_w", "kln_b", "qxln_w", "qxln_b", "kxln_w", "kxln_b", "proj_smooth")], axis=1)
    r["C_scalar"] = np.stack([a[L + n].reshape(()) for n in (
        "wq_scale", "wqx_scale", "wk_scale", "wv_scale", "proj_w_scale", "proj_in_scale")]).reshape(1, 6)
    L = "L1_ffn_"
    for n, w in (("q", "Wq"), ("k", "Wk")):
        padded = np.zeros((16, 32, D), a[L + w].dtype)
        padded[:, :16] = a[L + w].reshape(16, 16, D)
        r["D_" + n] = rows(padded.reshape(512, D).T)
    for n, w in (("v", "Wv"), ("o", "Wo"), ("in", "W_in_base"), ("up", "W_up_base"), ("down", "W_down")):
        r["D_" + n] = rows(a[L + w].T)
    r["D_a"] = rows(a[L + "A"])
    r["D_b"] = a[L + "B"]
    r["D_col"] = np.concatenate([col(a[L + "ln1_w"]), col(a[L + "ln2_w"])], axis=1)
    r["D_mask"] = np.where(np.tril(np.ones((P, P), bool)), np.float32(0), np.float32(NEG))
    L = "L2_xattn_"
    for n, w in (("q", "Wq"), ("kv", "Wkv"), ("p", "Wp")):
        r["E_" + n] = rows(a[L + w])
    r["E_bias"] = np.concatenate([a[L + "bq"], a[L + "bkv"], a[L + "bp"]]).reshape(1, -1)
    L = "L2_ffn_"
    r["F_gate"] = rows(a[L + "gate_w"])
    r["F_w1"] = rows(a[L + "w1"].transpose(1, 0, 2).reshape(D, 8 * P))
    r["F_w2"] = a[L + "w2"].transpose(1, 0, 2)
    r["F_sw1"] = rows(a[L + "shared_w1"])
    r["F_sw2"] = rows(a[L + "shared_w2"])
    r["F_b2"] = a[L + "b2"]
    r["F_sb2"] = a[L + "shared_b2"].reshape(1, D)
    r["F_col"] = np.concatenate([a[L + "b1"].T, col(a[L + "shared_b1"])], axis=1)
    r["ctx"] = ctxs.transpose(1, 0, 2)
    r["G_mask"] = a["mask_BxS2_bk0"].reshape(1, NB * P)
    L = "L3_ffn_"
    for n, w in (("up", "W_up"), ("gate", "W_gate"), ("down", "W_down")):
        r["H_" + n] = rows(a[L + w].T)
    r["H_col"] = np.concatenate([col(a[L + n]) for n in ("SU_ug", "SU_dp", "Wscale_ug")], axis=1)
    r["H_row"] = a[L + "Wscale_dp"].reshape(1, D)
    for f in LAYOUTS:
        r.update(f(a, np))
    return {k: np.ascontiguousarray(v) for k, v in r.items()}


LAYOUTS = []


def kernel(**inputs):
    import concourse.bacc as bacc
    from concourse.bass_utils import run_bass_kernel_spmd

    nc = bacc.Bacc("TRN2", target_bir_lowering=False, num_devices=1)
    arrays = lay_out(inputs)
    t = {k: nc.dram_tensor(f"in_{k}", v.shape, mybir.dt.from_np(v.dtype), kind="ExternalInput").ap() for k, v in arrays.items()}
    out = nc.dram_tensor("out", (P, NB, D), F32, kind="ExternalOutput").ap()
    program(nc, t, out)
    r = run_bass_kernel_spmd(nc, [{f"in_{k}": v for k, v in arrays.items()}], core_ids=[0])
    return r.results[0]["out"].transpose(1, 0, 2)
```

```python
from contextlib import ExitStack

import concourse.bass as bass
from concourse import mybir

ALU = mybir.AluOpType
ACT = mybir.ActivationFunctionType
AX = mybir.AxisListType
F32 = mybir.dt.float32
BF16 = mybir.dt.bfloat16
U8 = mybir.dt.uint8
U16 = mybir.dt.uint16

P = 128
NB = 8
D = 256
KC = D // P
G = 2
STEPS = NB // G
FF = 1024
FC = FF // P
MAGIC = 1.5 * 2.0 ** 23
NEG = -1.0e30


class Flag:

    def __init__(self, sem, per=1):
        self.sem, self.per, self.base = sem, per, 0

    def at(self, i, g, k=0):
        return self.nth(i, G * k + g)

    def nth(self, i, n):
        return i * (G * self.per) + (self.base + n + 1)


class StepFlag(Flag):

    def at(self, i, k=0):
        return i * self.per + (self.base + k + 1)


class Chain:

    def __init__(self, eng, sem):
        self.eng, self.sem, self.n = eng, sem, 0

    def link(self, ins):
        ins.then_inc(self.sem, 1)
        self.n += 1
        self.eng.wait_ge(self.sem, self.n)

    def mark(self, ins):
        ins.then_inc(self.sem, 1)
        self.n += 1
        return self.n

    def wait(self, n):
        self.eng.wait_ge(self.sem, n)

    def restart(self):
        if self.n:
            self.eng.wait_ge(self.sem, self.n)
            self.eng.sem_clear(self.sem)
            self.n = 0


def program(nc, t, out, layers=8):
    with ExitStack() as ctx:
        def sb(name, shape, dt=F32):
            return ctx.enter_context(nc.sbuf_tensor(name, shape, dt))

        def sem(name):
            return ctx.enter_context(nc.semaphore(name))

        def flag(name, per=1):
            return Flag(sem(name), per)

        def step_flag(name, per=1):
            return StepFlag(sem(name), per)

        X = sb("X", [P, NB, D])
        xn = sb("xn", [P, G, D])
        xT = sb("xT", [P, KC, G, P])
        stats = sb("stats", [P, G, 6])
        moments = sb("moments", [P, G, 2])
        rstd = sb("rstd", [P, G, 1])
        small = sb("small", [P, G, 112])
        eps5 = sb("eps5", [P, 1])
        minus_half = sb("minus_half", [P, 96])
        ident = sb("ident", [P, P])
        ident_b = sb("ident_b", [P, P], BF16)
        gates = sb("gates", [P, 2, 4])
        had256 = sb("had256", [P, KC, D])
        had128 = sb("had128", [P, P])
        ones = sb("ones", [P, P])
        root = sb("root", [P, 2, 64])
        ctxT = sb("ctxT", [P, G, KC, P])
        PS = ctx.enter_context(nc.psum_tensor("PS", [P, NB, 512], F32))

        def bank(g, n):
            return PS[:, 4 * g + n, :]

        def banks(g, n):
            return PS[:, 4 * g + n:4 * g + n + 2, :].rearrange("p a b -> p (a b)")

        work = sb("work", [P, G, 6144])
        spare = sb("spare", [P, 2048])
        early = sb("early", [P, 4608])
        late = sb("late", [P, 24576])

        def view(tile, at, *shape, dt=F32):
            n = 1
            for s in shape:
                n *= s
            words = n * (2 if dt in (BF16, U16) else 4) // 4
            v = tile[:, at:at + words]
            if dt != F32:
                v = v.bitcast(dt)
            names = ["a", "b", "c", "d", "e"][:len(shape)]
            if len(shape) > 1:
                v = v.rearrange(f"p ({' '.join(names)}) -> p {' '.join(names)}", **dict(zip(names, shape)))
            return v, at + words

        const_in = sem("const_in")
        const_sent = [0]
        ident_ready = sem("ident_ready")
        x_in = sem("x_in")
        gates_ready = sem("gates_ready")
        weights_in = [sem(f"weights_in{n}") for n in range(8)]
        weights_sent = [0] * 8
        prepared = sem("prepared")
        PREPARED = {3: 1, 4: 2, 7: 3}
        out_stored = sem("out_stored")
        ctx_in = [sem(f"ctx_in{g}") for g in range(G)]
        ctx_read = [sem(f"ctx_read{g}") for g in range(G)]
        ctx_base = [0]

        def ctx_loaded(eng, i, g):
            eng.wait_ge(ctx_in[g], i * 16 + 16 * (ctx_base[0] + 1))


        stats_ready = flag("stats_ready")
        rstd_ready = flag("rstd_ready")
        xn_ready = flag("xn_ready")
        xnT_done = flag("xnT_done")
        xT_ready = flag("xT_ready")
        x_done = flag("x_done")
        shared = (stats_ready, rstd_ready, xn_ready, xnT_done, xT_ready, x_done)
        dve_order = sem("dve_order")
        act_order = sem("act_order")
        pool_order = sem("pool_order")

        def norm_stats(ch, i, units=range(G)):
            for u in units:
                ch.link(nc.vector.bn_stats(stats[:, u % G, :], X[:, i * G + u, :]))
                nc.vector.bn_aggr(moments[:, u % G, :], stats[:, u % G, :]).then_inc(stats_ready.sem, 1)

        def norm_vector(dve, ch, i, again=None):
            norm_stats(ch, i)
            for g in range(G):
                b = i * G + g
                dve.wait_ge(rstd_ready.sem, rstd_ready.at(i, g))
                normed = nc.vector.tensor_scalar(xn[:, g, :], X[:, b, :], moments[:, g, 0:1], rstd[:, g, :],
                                                 ALU.subtract, ALU.mult)
                if again:
                    ch.link(normed)
                    again(g)
                else:
                    normed.then_inc(xn_ready.sem, 1)

        def norm_gpsimd(pool, ch, i, units=range(G)):
            for u in units:
                g = u % G
                pool.wait_ge(stats_ready.sem, stats_ready.nth(i, u))
                ch.link(nc.gpsimd.tensor_tensor(rstd[:, g, :], moments[:, g, 1:2], eps5[:], ALU.add))
                nc.gpsimd.tensor_tensor(rstd[:, g, :], rstd[:, g, :], minus_half[:, 0:1],
                                        ALU.pow).then_inc(rstd_ready.sem, 1)

        def norm_tensor(pe, i):
            for g in range(G):
                pe.wait_ge(xn_ready.sem, xn_ready.at(i, g))
                for k in range(KC):
                    last = nc.tensor.transpose(bank(g, 0)[:, k * P:(k + 1) * P], xn[:, g, k * P:(k + 1) * P], ident[:])
                last.then_inc(xnT_done.sem, 1)

        def norm_scalar(act, i):
            for g in range(G):
                act.wait_ge(xnT_done.sem, xnT_done.at(i, g))
                nc.scalar.copy(xT[:, :, g, :], bank(g, 0)[:, 0:D].rearrange("p (k t) -> p k t", k=KC)).then_inc(xT_ready.sem, 1)

        def rsqrt_vector(ch, x, n):
            y, z = root[:, 0, 0:n], root[:, 1, 0:n]
            i32 = mybir.dt.int32
            ch.link(nc.vector.tensor_single_scalar(y.bitcast(i32), x.bitcast(i32), 1, ALU.arith_shift_right))
            ch.link(nc.vector.tensor_scalar(y.bitcast(i32), y.bitcast(i32), -1.0, float(0x5F3759DF), ALU.mult, ALU.add))
            for step in range(3):
                ch.link(nc.vector.scalar_tensor_tensor(z, y, -0.5, y, ALU.mult, ALU.mult))
                ch.link(nc.vector.tensor_tensor(z, z, x, ALU.mult))
                ch.link(nc.vector.scalar_tensor_tensor(y, z, 1.5, y, ALU.add, ALU.mult))
            return y

        SUB = []
        LOADS = {n: [] for n in [*range(8), "3 attention"]}
        LOAD_AT = {2: [("3 attention", 1)], 3: [(3, 2), (4, 2), (5, 2), (6, 2), (7, 2)]}
        WEIGHT_USERS = set()
        LOOPS = {}
        BEFORE = {}

        def load_weights(sp, n):
            for dst, name in LOADS[n]:
                src = t[name]
                if src.shape[0] == 1:
                    src = src.broadcast_to(dst.shape)
                sp.dma_start(dst, src).then_inc(weights_in[3 if n == "3 attention" else n], 16)

        HA, DA = 32, 8
        TA = HA // 4
        wA_q, n_ = view(early, 0, KC, D)
        wA_kv, n_ = view(early, n_, KC, 2 * D)
        A_ = [{} for _ in range(G)]
        A_qkn = []
        for g in range(G):
            w, n_ = work[:, g, :], 0
            A_[g]["sq"], n_ = view(w, n_, 2, D)
            A_[g]["v1"], _ = view(spare, 1024 * g, HA, 32)
            A_[g]["oT"], n_ = view(w, n_, 4, P)
            A_[g]["qT"], n_ = view(w, n_, TA, P)
            A_[g]["kT"], n_ = view(w, n_, TA, P)
            A_[g]["p"], n_ = view(w, n_, 4, 4, P)
            qkn, n_ = view(w, n_, TA, 4, 32)
            A_qkn.append(qkn)
        A_res = sb("A_res", [P, D])
        LOADS[0] += [(wA_q, "A_q"), (wA_kv, "A_kv")]

        def A_prepare(dve, ch):
            for g in range(G):
                ch.link(nc.vector.memset(A_[g]["v1"].rearrange("p h d -> p (h d)"), 0.0))
                ch.mark(nc.vector.memset(A_[g]["v1"][:, :, DA:DA + 1], 1.0))
                ch.mark(nc.vector.memset(A_qkn[g].rearrange("p t j r -> p (t j r)"), 0.0))

        BEFORE[0, 4] = A_prepare
        A_qkv = flag("A_qkv")
        A_sq = flag("A_sq")
        A_vs = flag("A_vs")
        A_normed = flag("A_normed")
        A_turned = flag("A_turned", 4)
        A_turned_act = flag("A_turned_act", 2)
        A_turned_dve = flag("A_turned_dve", 2)
        A_scores = flag("A_scores", 8)
        A_exp = flag("A_exp", 8)
        A_pv = flag("A_pv", 2)
        A_oTs = flag("A_oTs", 2)
        A_o = flag("A_o", 2)
        A_read = flag("A_read")
        A_read.base = 1
        PREP = (6, 7)

        def ctx_sync(sp, i):
            for g in range(G):
                sp.wait_ge(ctx_read[g], i + (ctx_base[0] + 1))
                sp.dma_start(ctxT[:, g], t["ctxT"][:, :, i * G + g, :]).then_inc(ctx_in[g], 16)

        def A_pipeline(eng, ch, first, slot):
            first(ch)
            if ch:
                ch.restart()
            with eng.Fori(0, STEPS - 1) as i:
                for u in range(G):
                    slot(ch, i, u, 2)
                if ch:
                    ch.restart()
            slot(ch, STEPS - 1, 0, 1)
            slot(ch, STEPS - 1, 1, 0)

        def A_tensor(pe):
            def turn_x(i, u):
                pe.wait_ge(xn_ready.sem, xn_ready.nth(i, u))
                for k in range(KC):
                    last = nc.tensor.transpose(PS[:, PREP[0], k * P:(k + 1) * P], xn[:, u % G, k * P:(k + 1) * P], ident[:])
                last.then_inc(xnT_done.sem, 1)

            def projections(i, u):
                g = u % G
                ctx_loaded(pe, i + u // G, g)
                for c in range(2):
                    for k in range(KC):
                        last = nc.tensor.matmul(PS[:, PREP[1], c * D:(c + 1) * D], ctxT[:, g, k, :], wA_kv[:, k, c * D:(c + 1) * D],
                                                start=k == 0, stop=k == KC - 1)
                last.then_inc(ctx_read[g], 1)
                pe.wait_ge(xT_ready.sem, xT_ready.nth(i, u))
                for k in range(KC):
                    last = nc.tensor.matmul(PS[:, PREP[0], 0:D], xT[:, k, g, :], wA_q[:, k, :], start=k == 0, stop=k == KC - 1)
                last.then_inc(A_qkv.sem, 1)

            def turn(i, u, n):
                if n == 0:
                    pe.wait_ge(A_normed.sem, A_normed.nth(i, u))
                else:
                    pe.wait_ge(A_turned_act.sem, A_turned_act.nth(i, 2 * u))
                    pe.wait_ge(A_turned_dve.sem, A_turned_dve.nth(i, 2 * u))
                for c in range(2):
                    for tt in range(4):
                        last = nc.tensor.transpose(PS[:, PREP[c], tt * P:(tt + 1) * P],
                                                   A_qkn[n][:, 4 * c + tt].rearrange("p j r -> p (j r)"), ident[:])
                    last.then_inc(A_turned.sem, 1)

            def scores(i, u, half):
                g, r = u % G, 2 * u + half
                if half == 0:
                    pe.wait_ge(A_turned_act.sem, A_turned_act.nth(i, 2 * u + 1))
                    pe.wait_ge(A_turned_dve.sem, A_turned_dve.nth(i, 2 * u + 1))
                for j in range(4):
                    if r:
                        pe.wait_ge(A_exp.sem, A_exp.nth(i, 4 * r - 4 + j))
                    rows = slice(32 * j, 32 * j + DA)
                    for m in range(4):
                        last = nc.tensor.matmul(PS[:, j, m * P:(m + 1) * P], A_[g]["kT"][rows, 4 * half + m, :],
                                                A_[g]["qT"][rows, 4 * half + m, :], start=True, stop=True)
                    last.then_inc(A_scores.sem, 1)

            def weigh(i, u, half):
                g, r = u % G, 2 * u + half
                if half == 0:
                    pe.wait_ge(A_read.sem, A_read.nth(i, u - 1))
                for j in range(4):
                    pe.wait_ge(A_exp.sem, A_exp.nth(i, 4 * r + j))
                    for m in range(4):
                        last = nc.tensor.matmul(PS[32 * j:32 * j + 32, 4 + half, m * P:(m + 1) * P],
                                                A_[g]["v1"][:, 4 * half + m + TA * j, :], A_[half]["p"][:, j, m, :], start=True, stop=True)
                last.then_inc(A_pv.sem, 1)

            def turn_back(i, u, half):
                pe.wait_ge(A_oTs.sem, A_oTs.nth(i, 2 * u + half))
                for m in range(4):
                    last = nc.tensor.transpose(PS[:, 4 + half, m * P:(m + 1) * P], A_[half]["oT"][:, m, :], ident[:])
                last.then_inc(A_o.sem, 1)

            def first(ch):
                turn_x(0, 0)
                projections(0, 0)
                turn(0, 0, 0)
                turn(0, 0, 1)

            def slot(ch, i, u, ahead):
                if ahead:
                    pe.wait_ge(A_turned_act.sem, A_turned_act.nth(i, 2 * u + 1))
                    pe.wait_ge(A_turned_dve.sem, A_turned_dve.nth(i, 2 * u + 1))
                    turn_x(i, u + 1)
                elif layers > 1:
                    pe.wait_ge(A_turned_act.sem, A_turned_act.nth(i, 2 * u + 1))
                    B_weight_total(pe, PS[:, PREP[0], 0:3])
                scores(i, u, 0)
                if ahead:
                    projections(i, u + 1)
                scores(i, u, 1)
                weigh(i, u, 0)
                if ahead:
                    turn(i, u + 1, 0)
                weigh(i, u, 1)
                if ahead:
                    turn(i, u + 1, 1)
                turn_back(i, u, 0)
                turn_back(i, u, 1)

            A_pipeline(pe, None, first, slot)

        def A_scalar(act, ch):
            def feature_major(i, u):
                act.wait_ge(xnT_done.sem, xnT_done.nth(i, u))
                nc.scalar.copy(xT[:, :, u % G, :], PS[:, PREP[0], 0:D].rearrange("p (k t) -> p k t", k=KC)).then_inc(xT_ready.sem, 1)

            def squares(i, u):
                g = u % G
                act.wait_ge(A_qkv.sem, A_qkv.nth(i, u))
                nc.scalar.activation(A_[g]["sq"][:, 0, :], PS[:, PREP[0], 0:D], ACT.Square)
                nc.scalar.activation(A_[g]["sq"][:, 1, :], PS[:, PREP[1], 0:D], ACT.Square).then_inc(A_sq.sem, 1)
                nc.scalar.copy(A_[g]["v1"][:, :, 0:DA], PS[:, PREP[1], D:2 * D].rearrange("p (h d) -> p h d", h=HA)).then_inc(A_vs.sem, 1)

            def turned(i, u):
                for n, name in enumerate(("qT", "kT")):
                    act.wait_ge(A_turned.sem, A_turned.nth(i, 4 * u + 2 * n))
                    nc.scalar.copy(A_[u % G][name][:, 0:4, :].rearrange("p a b -> p (a b)"), PS[:, PREP[0], :]).then_inc(A_turned_act.sem, 1)

            def exps(i, u, half):
                r = 2 * u + half
                for j in range(4):
                    if j == 0 and r >= 2:
                        act.wait_ge(A_pv.sem, A_pv.nth(i, r - 2))
                    act.wait_ge(A_scores.sem, A_scores.nth(i, 4 * r + j))
                    nc.scalar.activation(A_[half]["p"][:, j].rearrange("p a b -> p (a b)"), PS[:, j, :], ACT.Exp,
                                         scale=DA ** -0.5).then_inc(A_exp.sem, 1)

            def first(ch):
                feature_major(0, 0)
                squares(0, 0)
                turned(0, 0)
                act.wait_ge(const_in, 64)
                nc.scalar.activation(gates[:], gates[:], ACT.Tanh).then_inc(gates_ready, 1)

            def slot(ch, i, u, ahead):
                if ahead:
                    feature_major(i, u + 1)
                exps(i, u, 0)
                if ahead:
                    squares(i, u + 1)
                exps(i, u, 1)
                if ahead:
                    turned(i, u + 1)

            A_pipeline(act, ch, first, slot)

        def A_gpsimd(pool, ch):
            def slot(ch, i, u, ahead):
                if ahead == 2:
                    norm_gpsimd(pool, ch, i, [u + 2])

            A_pipeline(pool, ch, lambda ch: norm_gpsimd(pool, ch, 0), slot)

        def normed_batch(dve, i, u):
            dve.wait_ge(rstd_ready.sem, rstd_ready.nth(i, u))
            nc.vector.tensor_scalar(xn[:, u % G, :], X[:, i * G + u, :], moments[:, u % G, 0:1], rstd[:, u % G, :],
                                    ALU.subtract, ALU.mult).then_inc(xn_ready.sem, 1)

        def A_vector(dve, ch):
            def normed(ch, i, u):
                g = u % G
                dve.wait_ge(A_sq.sem, A_sq.nth(i, u))
                ch.link(nc.vector.tensor_reduce(small[:, g, 0:2 * HA], A_[g]["sq"].rearrange("p a (h d) -> p (a h) d", d=DA), AX.X, ALU.add))
                ch.link(nc.vector.tensor_scalar(small[:, g, 0:2 * HA], small[:, g, 0:2 * HA], 1.0 / DA, 1e-6, ALU.mult, ALU.add))
                rms = rsqrt_vector(ch, small[:, g, 0:2 * HA], 2 * HA)
                dve.wait_ge(A_vs.sem, A_vs.nth(i, u))
                for n in range(2):
                    last = nc.vector.tensor_tensor(
                        A_qkn[n][:, :, :, 0:DA].rearrange("p t j d -> p j t d"),
                        PS[:, PREP[n], 0:D].rearrange("p (j t d) -> p j t d", j=4, t=TA),
                        rms[:, n * HA:(n + 1) * HA].rearrange("p (j t) -> p j t", j=4).unsqueeze(3).broadcast_to([P, 4, TA, DA]), ALU.mult)
                last.then_inc(A_normed.sem, 1)

            def turned(i, u, n):
                dve.wait_ge(A_turned.sem, A_turned.nth(i, 4 * u + 2 * n + 1))
                nc.vector.tensor_copy(A_[u % G][("qT", "kT")[n]][:, 4:8, :].rearrange("p a b -> p (a b)"),
                                      PS[:, PREP[1], :]).then_inc(A_turned_dve.sem, 1)

            def out(ch, i, u):
                dve.wait_ge(A_o.sem, A_o.nth(i, 2 * u + 1))
                o = PS[:, 4:6, :].rearrange("p half (m j d) -> p j (half m) d", m=4, j=4)
                sums = small[:, u % G, 64:96].rearrange("p (j t) -> p j t", j=4)
                res = A_res[:].rearrange("p (j t d) -> p j t d", j=4, t=TA)
                ch.link(nc.vector.reciprocal(sums, o[:, :, :, DA]))
                last = nc.vector.tensor_tensor(res, o[:, :, :, 0:DA], sums.unsqueeze(3).broadcast_to([P, 4, TA, DA]), ALU.mult)
                last.then_inc(A_read.sem, 1)
                dve.wait_ge(A_read.sem, A_read.nth(i, u))
                add_to_x(dve, ch, i * G + u, A_res[:], gates[:, 0, 0:1])

            def out_T(i, u, half):
                dve.wait_ge(A_pv.sem, A_pv.nth(i, 2 * u + half))
                nc.vector.tensor_copy(A_[half]["oT"].rearrange("p a b -> p (a b)"), PS[:, 4 + half, :]).then_inc(A_oTs.sem, 1)

            def first(ch):
                dve.sem_inc(A_read.sem, 1)
                norm_stats(ch, 0)
                for u in range(G):
                    normed_batch(dve, 0, u)
                normed(ch, 0, 0)
                turned(0, 0, 0)
                turned(0, 0, 1)
                dve.wait_ge(const_in, 64)
                dve.wait_ge(gates_ready, 1)

            def slot(ch, i, u, ahead):
                if ahead == 2:
                    norm_stats(ch, i, [u + 2])
                if ahead == 1 and layers > 1:
                    B_weight_sums(dve, ch)
                if ahead:
                    normed(ch, i, u + 1)
                elif layers > 1:
                    B_quantise_weights(dve, ch, PS[:, PREP[0], 0:3])
                out_T(i, u, 0)
                if ahead:
                    turned(i, u + 1, 0)
                if ahead == 2:
                    normed_batch(dve, i, u + 2)
                out_T(i, u, 1)
                if ahead:
                    turned(i, u + 1, 1)
                out(ch, i, u)

            A_pipeline(dve, ch, first, slot)

        def add_to_x(dve, ch, b, res, scale):
            nc.vector.scalar_tensor_tensor(X[:, b, :], res, scale, X[:, b, :], ALU.mult, ALU.add).then_inc(x_done.sem, 1)

        LOOPS[0] = (None, A_tensor, A_scalar, A_gpsimd, A_vector)
        SUB.append((ctx_sync, None, None, None, None))

        WPROJ = 16384
        n_ = WPROJ
        wB = []
        for name, a, w in (("B_gate", KC, FF), ("B_up", KC, FF), ("B_down", FC, D)):
            full, n_ = view(late, n_, a, w)
            wB.append(full)
            LOADS[1].append((full, name))
        qB = []
        n_ = 1536
        for a, w in ((KC, FF), (KC, FF), (FC, D)):
            q, n_ = view(early, n_, a, w, dt=BF16)
            qB.append(q)
        B_wscale = sb("B_wscale", [P, 2, 4])
        B_ = [{} for _ in range(G)]
        for g in range(G):
            w, n_ = work[:, g, :], 0
            B_[g]["q"], n_ = view(w, n_, D, dt=BF16)
            B_[g]["qT"], n_ = view(w, n_, KC, P, dt=BF16)
            B_[g]["silu"], n_ = view(w, n_, FF)
            B_[g]["h"], n_ = view(w, n_, FF)
            B_[g]["h2"], n_ = view(w, n_, FF)
            B_[g]["hT"], n_ = view(w, n_, FC, P)
            B_[g]["hq"], n_ = view(w, n_, FF, dt=BF16)
            B_[g]["hqT"], n_ = view(w, n_, FC, P, dt=BF16)
        B_sum = sem("B_sum")
        B_total = sem("B_total")
        B_quantised = sem("B_quantised")
        B_had = flag("B_had")
        B_q = flag("B_q")
        B_qturned = flag("B_qturned")
        B_qT = flag("B_qT")
        B_gateup = flag("B_gateup")
        B_silu = flag("B_silu")
        B_h = flag("B_h")
        B_hturned = flag("B_hturned")
        B_hT = flag("B_hT")
        B_hhad = flag("B_hhad")
        B_hq = flag("B_hq")
        B_hqturned = flag("B_hqturned")
        B_hqT = flag("B_hqT")
        B_down = flag("B_down")
        WEIGHT_USERS.add((1, 4))

        def B_weight_sums(dve, ch):
            dve.wait_ge(weights_in[1], weights_sent[1])
            for n in range(3):
                last = nc.vector.tensor_reduce(B_wscale[:, 0, n:n + 1], wB[n].rearrange("p a b -> p (a b)"), AX.X, ALU.add,
                                               apply_absolute_value=True)
            last.then_inc(B_sum, 1)

        def B_weight_total(pe, dst):
            pe.wait_ge(B_sum, 1)
            nc.tensor.matmul(dst, ones[:], B_wscale[:, 0, 0:3], start=True, stop=True).then_inc(B_total, 1)

        def B_quantise_weights(dve, ch, total):
            dve.wait_ge(B_total, 1)
            ch.link(nc.vector.tensor_scalar(B_wscale[:, 0, 0:3], total, 1.0 / (FF * D), 1e-5, ALU.mult, ALU.max))
            ch.link(nc.vector.reciprocal(B_wscale[:, 1, 0:3], B_wscale[:, 0, 0:3]))
            for n in range(3):
                w = wB[n].rearrange("p a b -> p (a b)")
                ch.link(nc.vector.tensor_scalar(w, w, B_wscale[:, 1, n:n + 1], MAGIC, ALU.mult, ALU.add))
                ch.link(nc.vector.tensor_scalar(w, w, MAGIC, 1.0, ALU.subtract, ALU.min))
                ch.link(nc.vector.tensor_scalar(qB[n].rearrange("p a b -> p (a b)"), w, -1.0, None, ALU.max))
            dve.wait_ge(weights_in[2], 16 * len(LOADS[2]))
            dve.sem_inc(B_quantised, 1)

        BEFORE[1, 1] = lambda pe, ch: (pe.wait_ge(const_in, 64), pe.wait_ge(B_quantised, 1))

        B_GATE, B_UP, B_HT, B_HAD = 0, 2, 4, 6
        B_DOWN = 5
        two = lambda n: PS[:, n:n + 2, :].rearrange("p a b -> p (a b)")

        def B_tensor(pe):
            def turn_x(i, u):
                pe.wait_ge(xn_ready.sem, xn_ready.nth(i, u))
                for k in range(KC):
                    last = nc.tensor.transpose(PS[:, 0, k * P:(k + 1) * P], xn[:, u % G, k * P:(k + 1) * P], ident[:])
                last.then_inc(xnT_done.sem, 1)

            def rotate_x(i, u):
                pe.wait_ge(xT_ready.sem, xT_ready.nth(i, u))
                for k in range(KC):
                    last = nc.tensor.matmul(PS[:, 1, 0:D], xT[:, k, u % G, :], had256[:, k, :], start=k == 0, stop=k == KC - 1)
                last.then_inc(B_had.sem, 1)

            def gate_and_up(i, u):
                g = u % G
                pe.wait_ge(B_q.sem, B_q.nth(i, u))
                dst = PS[:, 0, 0:P].bitcast(BF16)
                for k in range(KC):
                    last = nc.tensor.transpose(dst[:, k * P:(k + 1) * P], B_[g]["q"][:, k * P:(k + 1) * P], ident_b[:])
                last.then_inc(B_qturned.sem, 1)
                pe.wait_ge(B_qT.sem, B_qT.nth(i, u))
                for w, at in ((0, B_GATE), (1, B_UP)):
                    for n in range(2):
                        for k in range(KC):
                            last = nc.tensor.matmul(PS[:, at + n, :], B_[g]["qT"][:, k, :], qB[w][:, k, n * 512:(n + 1) * 512],
                                                    start=k == 0, stop=k == KC - 1)
                last.then_inc(B_gateup.sem, 1)

            def first(ch):
                turn_x(0, 0)
                rotate_x(0, 0)
                gate_and_up(0, 0)

            def slot(ch, i, u, ahead):
                g = u % G
                pe.wait_ge(B_h.sem, B_h.nth(i, u))
                if ahead:
                    turn_x(i, u + 1)
                pe.wait_ge(x_done.sem, x_done.nth(i, u - 1))
                for a in range(FC):
                    last = nc.tensor.transpose(two(B_HT)[:, a * P:(a + 1) * P], B_[g]["h2"][:, a * P:(a + 1) * P], ident[:])
                last.then_inc(B_hturned.sem, 1)
                if ahead:
                    rotate_x(i, u + 1)
                pe.wait_ge(B_hT.sem, B_hT.nth(i, u))
                for a in range(FC):
                    last = nc.tensor.matmul(two(B_HAD)[:, a * P:(a + 1) * P], B_[g]["hT"][:, a, :], had128[:], start=True, stop=True)
                last.then_inc(B_hhad.sem, 1)
                if ahead:
                    gate_and_up(i, u + 1)
                pe.wait_ge(B_hq.sem, B_hq.nth(i, u))
                dst = PS[:, B_HT, :].bitcast(BF16)
                for a in range(FC):
                    last = nc.tensor.transpose(dst[:, a * P:(a + 1) * P], B_[g]["hq"][:, a * P:(a + 1) * P], ident_b[:])
                last.then_inc(B_hqturned.sem, 1)
                pe.wait_ge(B_hqT.sem, B_hqT.nth(i, u))
                for a in range(FC):
                    last = nc.tensor.matmul(PS[:, B_DOWN, 0:D], B_[g]["hqT"][:, a, :], qB[2][:, a, :], start=a == 0, stop=a == FC - 1)
                last.then_inc(B_down.sem, 1)

            A_pipeline(pe, None, first, slot)

        def B_scalar(act, ch):
            def x_T(i, u):
                act.wait_ge(xnT_done.sem, xnT_done.nth(i, u))
                nc.scalar.copy(xT[:, :, u % G, :], PS[:, 0, 0:D].rearrange("p (k t) -> p k t", k=KC)).then_inc(xT_ready.sem, 1)

            def silu(i, u):
                g = u % G
                act.wait_ge(B_qturned.sem, B_qturned.nth(i, u))
                nc.scalar.copy(B_[g]["qT"].rearrange("p a b -> p (a b)"), PS[:, 0, 0:P].bitcast(BF16)).then_inc(B_qT.sem, 1)
                act.wait_ge(B_gateup.sem, B_gateup.nth(i, u))
                nc.scalar.activation(B_[g]["silu"], two(B_GATE), ACT.Silu, scale=small[:, g, 4:5]).then_inc(B_silu.sem, 1)

            def first(ch):
                x_T(0, 0)
                silu(0, 0)

            def slot(ch, i, u, ahead):
                g = u % G
                if ahead:
                    x_T(i, u + 1)
                act.wait_ge(B_hturned.sem, B_hturned.nth(i, u))
                nc.scalar.copy(B_[g]["hT"].rearrange("p a b -> p (a b)"), two(B_HT)).then_inc(B_hT.sem, 1)
                if ahead:
                    silu(i, u + 1)
                act.wait_ge(B_hqturned.sem, B_hqturned.nth(i, u))
                nc.scalar.copy(B_[g]["hqT"].rearrange("p a b -> p (a b)"), PS[:, B_HT, :].bitcast(BF16)).then_inc(B_hqT.sem, 1)

            A_pipeline(act, ch, first, slot)

        def B_gpsimd(pool, ch, i):
            norm_gpsimd(pool, ch, i)

        def quantize(ch, g, src, scaled, whole, norm, done, at, scales):
            s = small[:, g, at:at + 1]
            r = small[:, g, at + 1:at + 2]
            ch.link(nc.vector.tensor_reduce(s, src, AX.X, ALU.max, apply_absolute_value=True))
            ch.link(nc.vector.tensor_scalar(s, s, norm, 1e-5, ALU.mult, ALU.max))
            ch.link(nc.vector.reciprocal(r, s))
            ch.link(nc.vector.tensor_scalar(r, r, 127.0 * norm, None, ALU.mult))
            ch.link(nc.vector.tensor_scalar(scaled, src, r, MAGIC, ALU.mult, ALU.add))
            scales()
            nc.vector.tensor_scalar(whole, scaled, MAGIC, 127.0, ALU.subtract, ALU.min).then_inc(done, 1)

        def B_vector(dve, ch):
            def quantise_x(ch, i, u):
                g = u % G
                dve.wait_ge(B_had.sem, B_had.nth(i, u))

                def scales():
                    for n in range(2):
                        nc.vector.tensor_scalar(small[:, g, 4 + n:5 + n], small[:, g, 0:1], B_wscale[:, 0, n:n + 1], 1.0 / 127,
                                                ALU.mult, ALU.mult)

                quantize(ch, g, PS[:, 1, 0:D], B_[g]["h"][:, 0:D], B_[g]["q"], 1.0 / 16, B_q.sem, 0, scales)

            def hidden(ch, i, u):
                g = u % G
                dve.wait_ge(B_silu.sem, B_silu.nth(i, u))
                h, h2 = B_[g]["h"], B_[g]["h2"]
                ch.link(nc.vector.scalar_tensor_tensor(h, two(B_UP), small[:, g, 5:6], B_[g]["silu"], ALU.mult, ALU.mult))
                for s in (4, 2, 1):
                    a = h.rearrange("p (o two s) -> p o two s", two=2, s=s * P)
                    b = h2.rearrange("p (o two s) -> p o two s", two=2, s=s * P)
                    nc.vector.tensor_tensor(b[:, :, 0, :], a[:, :, 0, :], a[:, :, 1, :], ALU.add)
                    sub = nc.vector.tensor_tensor(b[:, :, 1, :], a[:, :, 0, :], a[:, :, 1, :], ALU.subtract)
                    if s == 1:
                        sub.then_inc(B_h.sem, 1)
                    else:
                        ch.link(sub)
                    h, h2 = h2, h

            def first(ch):
                norm_stats(ch, 0)
                for u in range(G):
                    normed_batch(dve, 0, u)
                quantise_x(ch, 0, 0)
                hidden(ch, 0, 0)

            def slot(ch, i, u, ahead):
                g = u % G
                if ahead == 2:
                    norm_stats(ch, i, [u + 2])
                C_centre(ch, i, u)
                if ahead:
                    quantise_x(ch, i, u + 1)
                dve.wait_ge(B_hhad.sem, B_hhad.nth(i, u))

                def scales():
                    ch.link(nc.vector.tensor_scalar(small[:, g, 10:11], small[:, g, 8:9], B_wscale[:, 0, 2:3], 1.0 / 127, ALU.mult, ALU.mult))
                    ch.link(nc.vector.tensor_scalar(small[:, g, 11:12], small[:, g, 10:11], gates[:, 1, 0:1], None, ALU.mult))

                quantize(ch, g, two(B_HAD), B_[g]["h"], B_[g]["hq"], 1.0 / 32, B_hq.sem, 8, scales)
                if ahead == 2:
                    normed_batch(dve, i, u + 2)
                if ahead:
                    hidden(ch, i, u + 1)
                dve.wait_ge(B_down.sem, B_down.nth(i, u))
                add_to_x(dve, ch, i * G + u, PS[:, B_DOWN, 0:D], small[:, g, 11:12])

            A_pipeline(dve, ch, first, slot)

        LOOPS[1] = (None, B_tensor, B_scalar, A_gpsimd, B_vector)
        SUB.append((None, None, None, None, None))
        HC, KVH, DC = 16, 8, 128
        ROUNDS = 8
        UNITS, DEPTH = G * ROUNDS, 6
        wC, n_ = {}, 0
        for name, a, w in (("q", KC, 2048), ("qx", KC, 2048), ("k", KC, 1024), ("kx", KC, 1024), ("v", KC, 1024), ("vx", KC, 1024),
                           ("proj", 32, D)):
            wC[name], n_ = view(late, n_, a, w)
            if name != "proj":
                LOADS[2].append((wC[name], "C_" + name))
        col = sb("C_col", [P, 52])
        c_ln_w, c_ln_b, c_in, c_head, c_smooth = col[:, 0:2], col[:, 2:4], col[:, 4:12], col[:, 12:20], col[:, 20:52]
        inv = sb("C_inv", [P, 40])
        scalar = sb("C_scalar", [P, 6])
        square = sb("C_square", [P, 2, 8])
        out_scale = sb("C_out_scale", [P, 1])
        LOADS[2] += [(col[:], "C_col"), (scalar[:], "C_scalar")]
        centre = sb("C_centre", [P, 12])
        C_ = [{} for _ in range(G)]
        for g in range(G):
            w, n_ = work[:, g, :], 0
            for name in ("kn", "qn", "kT", "qT", "cat", "p", "pT", "t"):
                C_[g][name], n_ = view(w, n_, 4, P)
            C_[g]["y"], n_ = view(w, n_, 4, P, dt=BF16)
            C_[g]["m"], n_ = view(w, n_, 4, P, dt=BF16)
            C_[g]["v"], n_ = view(w, n_, 2, 4, P)
            C_[g]["t_in"], n_ = view(w, n_, KC * P)
            C_[g]["y_in"], n_ = view(w, n_, KC * P, dt=BF16)
            C_[g]["m_in"], n_ = view(w, n_, KC * P, dt=BF16)
            C_[g]["xs"], _ = view(spare, 1024 * g, 4, KC, P)
        C_stats2 = flag("C_stats2")
        C_rstd2 = flag("C_rstd2")
        C_xs = flag("C_xs", 4)
        C_k = flag("C_k", ROUNDS // 2)
        C_vq = flag("C_vq", ROUNDS)
        C_ksq = flag("C_ksq", ROUNDS // 2)
        C_qsq = flag("C_qsq", ROUNDS)
        C_v = flag("C_v", ROUNDS // 2)
        C_ksd = flag("C_ksd", ROUNDS // 2)
        C_qsd = flag("C_qsd", ROUNDS)
        C_kn = flag("C_kn", ROUNDS // 2)
        C_qn = flag("C_qn", ROUNDS)
        C_kturned = flag("C_kturned", ROUNDS // 2)
        C_kT = flag("C_kT", ROUNDS // 2)
        C_qturned = flag("C_qturned", ROUNDS)
        C_qT = flag("C_qT", ROUNDS)
        C_scores = flag("C_scores", ROUNDS)
        C_max = flag("C_max", ROUNDS)
        C_exp = flag("C_exp", ROUNDS)
        C_p = flag("C_p", ROUNDS)
        C_pturned = flag("C_pturned", ROUNDS)
        C_pT = flag("C_pT", ROUNDS)
        C_o = flag("C_o", ROUNDS)
        C_cat = flag("C_cat", ROUNDS)
        C_out = step_flag("C_out")
        WEIGHT_USERS.update({(2, 4), (2, 2)})
        KBANK, VBANK, QBANK, TBANK, SBANK, PBANK, OBANK, OUTBANK = range(NB)
        heads4 = lambda n: PS[:, n, :].rearrange("p (h d) -> p h d", h=4)
        over_head = lambda v: v.unsqueeze(2).broadcast_to([P, 4, P])
        flat = lambda v: v.rearrange("p a b -> p (a b)")

        unit = lambda u: (u % G, (u // G) % ROUNDS)
        brings_kv = lambda u: u % 4 < G
        kv_at = lambda u: G * (u // 4) + u % G
        last_step = lambda i: isinstance(i, int) and i == STEPS - 1

        def C_slots(ch, i, slots, stages, extra):
            for n in slots:
                for lag, stage in stages:
                    if n - lag >= 0 and not (last_step(i) and n - lag >= UNITS):
                        stage(ch, i, n - lag)
                extra(ch, i, n)

        def C_pipeline(eng, ch, first, stages, extra):
            first(ch)
            C_slots(ch, 0, range(0, DEPTH), stages, extra)
            if ch:
                ch.restart()
            with eng.Fori(0, STEPS - 1) as i:
                C_slots(ch, i, range(DEPTH, UNITS + DEPTH), stages, extra)
                if ch:
                    ch.restart()
            C_slots(ch, STEPS - 1, range(DEPTH, UNITS + DEPTH), stages, extra)

        def C_centre(ch, i, u):
            heads = 96 // NB
            w = late[:, bass.ds((i * G + u) * (heads * DC), heads * DC)].rearrange("p (h d) -> p h d", d=DC)
            ch.link(nc.vector.tensor_reduce(centre[:], w, AX.X, ALU.add))
            ch.link(nc.vector.tensor_scalar(centre[:], centre[:], 1.0 / DC, None, ALU.mult))
            ch.mark(nc.vector.tensor_tensor(w, w, centre[:].unsqueeze(2).broadcast_to([P, heads, DC]), ALU.subtract))

        def C_prepare(ch):
            ch.mark(nc.vector.reciprocal(inv[:, 0:8], c_in))
            ch.mark(nc.vector.reciprocal(inv[:, 8:40], c_smooth))
            ch.link(nc.vector.memset(square[:].rearrange("p a b -> p (a b)"), 1.0))
            for cross, at, n in ((0, 0, 0), (1, 0, 1), (0, 4, 2)):
                sq, w_ln, scale = square[:, cross, at:at + 4], c_head[:, 4 * cross + at // 2:4 * cross + at // 2 + 1], scalar[:, n:n + 1]
                ch.link(nc.vector.tensor_scalar(sq, sq, scale, scale, ALU.mult, ALU.mult))
                ch.link(nc.vector.tensor_tensor(w_ln, w_ln, scale, ALU.mult))
            ch.link(nc.vector.tensor_scalar(square[:], square[:], 1.0 / DC, None, ALU.mult))
            ch.link(nc.vector.tensor_tensor(out_scale[:], scalar[:, 4:5], scalar[:, 5:6], ALU.mult))
            ch.link(nc.vector.tensor_tensor(out_scale[:], out_scale[:], gates[:, 0, 1:2], ALU.mult))


        BEFORE[2, 4] = lambda dve, ch: C_prepare(ch)

        def to_fp8(ch, y, m, t, out):
            ch.link(nc.vector.tensor_single_scalar(m.bitcast(U16), y.bitcast(U16), 0x7F80, ALU.bitwise_and))
            ch.link(nc.vector.tensor_scalar(m, m, 2.0 ** -6, 1.5 * 2.0 ** 20, ALU.max, ALU.mult))
            ch.link(nc.vector.tensor_tensor(t, y, m, ALU.add))
            return nc.vector.tensor_tensor(out, t, m, ALU.subtract)

        def C_vector(dve, ch):
            def again(ch, i):
                for g in range(G):
                    dve.wait_ge(rstd_ready.sem, rstd_ready.at(i, g))
                    ch.link(nc.vector.tensor_scalar(xn[:, g, :], X[:, i * G + g, :], moments[:, g, 0:1], rstd[:, g, :],
                                                    ALU.subtract, ALU.mult))
                    ch.link(nc.vector.bn_stats(stats[:, g, :], xn[:, g, :]))
                    nc.vector.bn_aggr(moments[:, g, :], stats[:, g, :]).then_inc(C_stats2.sem, 1)

            def twice_normed(ch, i):
                for g in range(G):
                    dve.wait_ge(C_rstd2.sem, C_rstd2.at(i, g))
                    nc.vector.tensor_scalar(xn[:, g, :], xn[:, g, :], moments[:, g, 0:1], rstd[:, g, :],
                                            ALU.subtract, ALU.mult).then_inc(xn_ready.sem, 1)

            def activations(ch, g, n):
                c = C_[g]
                for k in range(KC):
                    last = nc.vector.tensor_scalar(c["t_in"][:, k * P:(k + 1) * P], xT[:, k, g, :], inv[:, n * KC + k:n * KC + k + 1],
                                                   448.0, ALU.mult, ALU.min)
                ch.link(last)
                ch.link(nc.vector.tensor_scalar(c["y_in"], c["t_in"], -448.0, None, ALU.max))
                ch.link(to_fp8(ch, c["y_in"], c["m_in"], c["t_in"], c["t_in"]))
                for k in range(KC):
                    last = nc.vector.tensor_scalar(c["xs"][:, n, k, :], c["t_in"][:, k * P:(k + 1) * P], c_in[:, n * KC + k:n * KC + k + 1],
                                                   None, ALU.mult)
                last.then_inc(C_xs.sem, 1)

            def normed_k(ch, i, u):
                g, r = unit(u)
                if brings_kv(u):
                    dve.wait_ge(C_ksd.sem, C_ksd.nth(i, kv_at(u)))
                    nc.vector.tensor_tensor(C_[g]["kn"], heads4(KBANK), over_head(small[:, g, 4:8]), ALU.mult).then_inc(C_kn.sem, 1)

            def normed_q(ch, i, u):
                g, r = unit(u)
                dve.wait_ge(C_qsd.sem, C_qsd.nth(i, u))
                nc.vector.tensor_tensor(C_[g]["qn"], heads4(QBANK), over_head(small[:, g, 0:4]), ALU.mult).then_inc(C_qn.sem, 1)

            def largest(ch, i, u):
                g, r = unit(u)
                mx = small[:, g, 8:12]
                dve.wait_ge(C_scores.sem, C_scores.nth(i, u))
                ch.link(nc.vector.tensor_reduce(mx, heads4(SBANK), AX.X, ALU.max))
                nc.vector.tensor_scalar(mx, mx, -DC ** -0.5, None, ALU.mult).then_inc(C_max.sem, 1)

            def probabilities(ch, i, u):
                g, r = unit(u)
                c = C_[g]
                dve.wait_ge(C_exp.sem, C_exp.nth(i, u))
                ch.link(nc.vector.reciprocal(small[:, g, 16:20], small[:, g, 12:16]))
                nc.vector.tensor_tensor(c["p"], c["p"], over_head(small[:, g, 16:20]), ALU.mult).then_inc(C_p.sem, 1)

            def rounded(ch, i, u):
                g, r = unit(u)
                c = C_[g]
                dve.wait_ge(C_o.sem, C_o.nth(i, u))
                ch.link(nc.vector.tensor_tensor(c["t"], heads4(OBANK), over_head(inv[:, 8 + 4 * r:12 + 4 * r]), ALU.mult))
                ch.link(nc.vector.tensor_scalar(c["y"], c["t"], 448.0, -448.0, ALU.min, ALU.max))
                to_fp8(ch, c["y"], c["m"], c["t"], c["cat"]).then_inc(C_cat.sem, 1)

            def extra(ch, i, n):
                if n == UNITS + DEPTH - 1:
                    dve.wait_ge(C_out.sem, C_out.at(i))
                    for g in range(G):
                        add_to_x(dve, ch, i * G + g, PS[:, OUTBANK, g * D:(g + 1) * D], out_scale[:])
                if last_step(i):
                    return
                if 1 <= n % UNITS <= G:
                    activations(ch, n % UNITS - 1, 1)
                if n == DEPTH:
                    norm_stats(ch, i + 1)
                if n == DEPTH + 1:
                    again(ch, i + 1)
                if n == DEPTH + 2:
                    twice_normed(ch, i + 1)
                if 11 <= n < 17:
                    m, g = divmod(n - 11, G)
                    if m == 0:
                        dve.wait_ge(xT_ready.sem, xT_ready.at(i + 1, g))
                    activations(ch, g, (2, 3, 0)[m])

            def first(ch):
                norm_stats(ch, 0)
                again(ch, 0)
                twice_normed(ch, 0)
                for n in (2, 3, 0):
                    for g in range(G):
                        dve.wait_ge(xT_ready.sem, xT_ready.at(0, g))
                        activations(ch, g, n)

            C_pipeline(dve, ch, first, [(2, largest), (3, probabilities), (5, rounded), (0, normed_k), (0, normed_q)], extra)

        def C_gpsimd(pool, ch):
            def again(ch, i):
                for g in range(G):
                    pool.wait_ge(C_stats2.sem, C_stats2.at(i, g))
                    ch.link(nc.gpsimd.tensor_tensor(rstd[:, g, :], moments[:, g, 1:2], eps5[:], ALU.add))
                    nc.gpsimd.tensor_tensor(rstd[:, g, :], rstd[:, g, :], minus_half[:, 0:1], ALU.pow).then_inc(C_rstd2.sem, 1)

            def deviations(ch, i, u):
                g, r = unit(u)

                def power(rs, square):
                    ch.link(nc.gpsimd.tensor_tensor(rs, rs, square, ALU.mult))
                    ch.link(nc.gpsimd.tensor_tensor(rs, rs, eps5[:, 0:1].broadcast_to([P, 4]), ALU.add))
                    return nc.gpsimd.tensor_tensor(rs, rs, minus_half[:, 0:4], ALU.pow)

                if brings_kv(u):
                    pool.wait_ge(C_ksq.sem, C_ksq.nth(i, kv_at(u)))
                    power(small[:, g, 4:8], square[:, r // 4, 4:8]).then_inc(C_ksd.sem, 1)
                pool.wait_ge(C_qsq.sem, C_qsq.nth(i, u))
                power(small[:, g, 0:4], square[:, r // 4, 0:4]).then_inc(C_qsd.sem, 1)

            def extra(ch, i, n):
                if not last_step(i):
                    if n == DEPTH:
                        norm_gpsimd(pool, ch, i + 1)
                    if n == DEPTH + 1:
                        again(ch, i + 1)

            def first(ch):
                norm_gpsimd(pool, ch, 0)
                again(ch, 0)

            C_pipeline(pool, ch, first, [(0, deviations)], extra)

        def C_scalar(act, ch):
            def feature_major(i):
                act.wait_ge(xnT_done.sem, xnT_done.at(i, G - 1))
                for g in range(G):
                    for k in range(KC):
                        at = (g * KC + k) * P
                        last = nc.scalar.activation(xT[:, k, g, :], PS[:, VBANK, at:at + P], ACT.Identity,
                                                    scale=c_ln_w[:, k:k + 1], bias=c_ln_b[:, k:k + 1])
                    last.then_inc(xT_ready.sem, 1)

            def squares_k(ch, i, u):
                if brings_kv(u):
                    g, r = unit(u)
                    act.wait_ge(C_k.sem, C_k.nth(i, kv_at(u)))
                    for h in range(4):
                        last = nc.scalar.activation(C_[g]["kn"][:, h, :], PS[:, KBANK, h * P:(h + 1) * P], ACT.Square,
                                                    accum_out=small[:, g, 4 + h:5 + h])
                    last.then_inc(C_ksq.sem, 1)

            def squares_q(ch, i, u):
                g, r = unit(u)
                act.wait_ge(C_vq.sem, C_vq.nth(i, u))
                for h in range(4):
                    last = nc.scalar.activation(C_[g]["qn"][:, h, :], PS[:, QBANK, h * P:(h + 1) * P], ACT.Square,
                                                accum_out=small[:, g, h:h + 1])
                last.then_inc(C_qsq.sem, 1)

            def v_out(ch, i, u):
                if brings_kv(u):
                    g, r = unit(u)
                    nc.scalar.activation(flat(C_[g]["v"][:, (r // 2) % 2]), PS[:, VBANK, :], ACT.Copy,
                                         scale=scalar[:, 3:4] if r < 4 else 1.0).then_inc(C_v.sem, 1)

            def k_T(ch, i, u):
                if brings_kv(u):
                    g, r = unit(u)
                    h = 4 * (r // 4) + 2
                    act.wait_ge(C_kturned.sem, C_kturned.nth(i, kv_at(u)))
                    nc.scalar.activation(flat(C_[g]["kT"]), PS[:, TBANK, :], ACT.Identity, scale=c_head[:, h:h + 1],
                                         bias=c_head[:, h + 1:h + 2]).then_inc(C_kT.sem, 1)

            def q_T(ch, i, u):
                g, r = unit(u)
                h = 4 * (r // 4)
                act.wait_ge(C_qturned.sem, C_qturned.nth(i, u))
                nc.scalar.activation(flat(C_[g]["qT"]), PS[:, TBANK, :], ACT.Identity, scale=c_head[:, h:h + 1],
                                     bias=c_head[:, h + 1:h + 2]).then_inc(C_qT.sem, 1)

            def exps(ch, i, u):
                g, r = unit(u)
                act.wait_ge(C_max.sem, C_max.nth(i, u))
                for h in range(4):
                    last = nc.scalar.activation(C_[g]["p"][:, h, :], PS[:, SBANK, h * P:(h + 1) * P], ACT.Exp, scale=DC ** -0.5,
                                                bias=small[:, g, 8 + h:9 + h], accum_out=small[:, g, 12 + h:13 + h])
                last.then_inc(C_exp.sem, 1)

            def p_T(ch, i, u):
                act.wait_ge(C_pturned.sem, C_pturned.nth(i, u))
                nc.scalar.copy(flat(C_[u % G]["pT"]), PS[:, PBANK, :]).then_inc(C_pT.sem, 1)

            def extra(ch, i, n):
                if n == 10 and not last_step(i):
                    feature_major(i + 1)

            C_pipeline(act, ch, lambda ch: feature_major(0), [(2, exps), (0, squares_k), (0, squares_q), (1, k_T), (0, v_out), (1, q_T), (3, p_T)],
                       extra)

        def C_tensor(pe):
            def turn_x(i):
                for g in range(G):
                    pe.wait_ge(xn_ready.sem, xn_ready.at(i, g))
                    for k in range(KC):
                        at = (g * KC + k) * P
                        last = nc.tensor.transpose(PS[:, VBANK, at:at + P], xn[:, g, k * P:(k + 1) * P], ident[:])
                    last.then_inc(xnT_done.sem, 1)

            def project(n, src, w, c0):
                for k in range(KC):
                    last = nc.tensor.matmul(PS[:, n, :], src(k), w[:, k, c0:c0 + 512], start=k == 0, stop=k == KC - 1)
                return last

            def projections(ch, i, u):
                g, r = unit(u)
                cross, quad, half = r // 4, (r // 2) % 2, r % 2
                x_of = lambda n: (lambda k: C_[g]["xs"][:, n, k, :])
                ctx_of = lambda k: ctxT[:, g, k, :]
                if r == 0:
                    pe.wait_ge(C_xs.sem, C_xs.nth(i, 8 * (u // UNITS) + 4 + g))
                if r == 4:
                    pe.wait_ge(C_xs.sem, C_xs.nth(i, 6 + g))
                    ctx_loaded(pe, i, g)
                if half == 0:
                    if u:
                        pe.wait_ge(C_kn.sem, C_kn.nth(i, kv_at(u) - 1))
                        pe.wait_ge(C_v.sem, C_v.nth(i, kv_at(u) - 1))
                    if u == 12 and not last_step(i):
                        pe.wait_ge(xT_ready.sem, xT_ready.at(i + 1, G - 1))
                    project(KBANK, ctx_of if cross else x_of(2), wC["kx" if cross else "k"], 512 * quad).then_inc(C_k.sem, 1)
                    last = project(VBANK, ctx_of if cross else x_of(3), wC["vx" if cross else "v"], 512 * quad)
                    if cross and quad:
                        last.then_inc(ctx_read[g], 1)
                if u:
                    pe.wait_ge(C_qn.sem, C_qn.nth(i, u - 1))
                project(QBANK, x_of(cross), wC["qx" if cross else "q"], 1024 * quad + 512 * half).then_inc(C_vq.sem, 1)

            def turn_k(ch, i, u):
                if brings_kv(u):
                    pe.wait_ge(C_kn.sem, C_kn.nth(i, kv_at(u)))
                    if u:
                        pe.wait_ge(C_qT.sem, C_qT.nth(i, u - 1))
                    for h in range(4):
                        last = nc.tensor.transpose(PS[:, TBANK, h * P:(h + 1) * P], C_[u % G]["kn"][:, h, :], ident[:])
                    last.then_inc(C_kturned.sem, 1)

            def turn_q(ch, i, u):
                if brings_kv(u):
                    pe.wait_ge(C_kT.sem, C_kT.nth(i, kv_at(u)))
                else:
                    pe.wait_ge(C_qT.sem, C_qT.nth(i, u - 1))
                pe.wait_ge(C_qn.sem, C_qn.nth(i, u))
                for h in range(4):
                    last = nc.tensor.transpose(PS[:, TBANK, h * P:(h + 1) * P], C_[u % G]["qn"][:, h, :], ident[:])
                last.then_inc(C_qturned.sem, 1)

            def scores(ch, i, u):
                g, r = unit(u)
                c = C_[g]
                pe.wait_ge(C_qT.sem, C_qT.nth(i, u))
                if u:
                    pe.wait_ge(C_exp.sem, C_exp.nth(i, u - 1))
                for h in range(4):
                    last = nc.tensor.matmul(PS[:, SBANK, h * P:(h + 1) * P], c["qT"][:, h, :], c["kT"][:, 2 * (r % 2) + h // 2, :],
                                            start=True, stop=True)
                last.then_inc(C_scores.sem, 1)

            def turn_p(ch, i, u):
                pe.wait_ge(C_p.sem, C_p.nth(i, u))
                if u:
                    pe.wait_ge(C_pT.sem, C_pT.nth(i, u - 1))
                for h in range(4):
                    last = nc.tensor.transpose(PS[:, PBANK, h * P:(h + 1) * P], C_[u % G]["p"][:, h, :], ident[:])
                last.then_inc(C_pturned.sem, 1)

            def weigh(ch, i, u):
                g, r = unit(u)
                c = C_[g]
                pe.wait_ge(C_pT.sem, C_pT.nth(i, u))
                pe.wait_ge(C_v.sem, C_v.nth(i, kv_at(u)))
                if u:
                    pe.wait_ge(C_cat.sem, C_cat.nth(i, u - 1))
                for h in range(2):
                    last = nc.tensor.matmul(PS[:, OBANK, h * D:(h + 1) * D], c["v"][:, (r // 2) % 2, 2 * (r % 2) + h, :],
                                            c["pT"][:, 2 * h:2 * h + 2, :].rearrange("p a b -> p (a b)"), start=True, stop=True)
                last.then_inc(C_o.sem, 1)

            def out(ch, i, u):
                g, r = unit(u)
                pe.wait_ge(C_cat.sem, C_cat.nth(i, u))
                if u % UNITS == 0:
                    pe.wait_ge(x_done.sem, x_done.nth(i, -1))
                for h in range(4):
                    last = nc.tensor.matmul(PS[:, OUTBANK, g * D:(g + 1) * D], C_[g]["cat"][:, h, :], wC["proj"][:, 4 * r + h, :],
                                            start=u % UNITS == 0 and h == 0, stop=u % UNITS == UNITS - 1 and h == 3)
                if u % UNITS == UNITS - 1:
                    last.then_inc(C_out.sem, 1)

            def extra(ch, i, n):
                if n == 10 and not last_step(i):
                    pe.wait_ge(C_v.sem, C_v.nth(i, kv_at(9)))
                    turn_x(i + 1)

            C_pipeline(pe, None, lambda ch: turn_x(0),
                       [(2, scores), (0, projections), (1, turn_k), (3, turn_p), (6, out), (1, turn_q), (4, weigh)], extra)

        LOOPS[2] = (None, C_tensor, C_scalar, C_gpsimd, C_vector)
        SUB.append((ctx_sync, None, None, None, None))

        DD = 16
        n_ = 0
        wD = {}
        for name, a, w in (("q", KC, 512), ("k", KC, 512), ("v", KC, D), ("o", 4, D)):
            wD[name], n_ = view(early, n_, a, w)
            LOADS["3 attention"].append((wD[name], "D_" + name))
        wD["a"] = sb("D_a", [P, KC, 16])
        wD["b"], n_ = view(early, n_, FF)
        LOADS["3 attention"] += [(wD["a"][:], "D_a"), (wD["b"][0:16, :], "D_b")]
        n_ = 0
        for name, a, w in (("in", KC, FF), ("up", KC, FF), ("down", FC, D)):
            wD[name], n_ = view(late, n_, a, w)
            LOADS[3].append((wD[name], "D_" + name))
        LATE_4 = n_
        D_col = sb("D_col", [P, 4])
        D_mask = sb("D_mask", [P, P])
        D_mask4 = sb("D_mask4", [P, 4, P], BF16)
        LOADS["3 attention"] += [(D_col[:], "D_col"), (D_mask[:], "D_mask")]
        eps6 = sb("eps6", [P, 1])
        x2T = sb("x2T", [P, KC, G, P])
        D_p, n_ = view(work[:, 0, :], 0, 4, 4, P)
        D_pT, n_ = view(work[:, 0, :], n_, 2, 4, P)
        D_aoT, n_ = view(work[:, 0, :], n_, KC, G * P)
        D_mod, n_ = view(work[:, 0, :], n_, D)
        D_prod, n_ = view(work[:, 0, :], n_, D)
        D_xb, n_ = view(work[:, 0, :], n_, G, D)
        D_raw, n_ = view(work[:, 1, :], 0, KC, G, P)
        D_oT, n_ = view(work[:, 1, :], n_, 4, G, P)
        D_qk, n_ = view(work[:, 1, :], n_, 2, 4, D)
        D_v, n_ = view(work[:, 1, :], n_, G, 16, 32)
        D_silu, n_ = view(spare, 0, 2, 2 * D)
        D_m, n_ = view(spare, n_, 2, 2 * D)
        D_UNITS = 4 * G
        CHUNKS = FC // 2
        D_ms = flag("D_ms")
        D_rstd2 = flag("D_rstd2")
        D_qkv = step_flag("D_qkv")
        D_qkvs = step_flag("D_qkvs")
        D_scores = step_flag("D_scores", D_UNITS)
        D_max = step_flag("D_max", D_UNITS)
        D_exp = step_flag("D_exp", D_UNITS)
        D_ps = step_flag("D_ps", D_UNITS)
        D_pturned = step_flag("D_pturned", D_UNITS)
        D_pTs = step_flag("D_pTs", D_UNITS)
        D_pv = step_flag("D_pv", D_UNITS)
        D_oTs = step_flag("D_oTs", G)
        D_ao = step_flag("D_ao")
        D_aos = step_flag("D_aos")
        D_x2 = step_flag("D_x2")
        D_ranks = step_flag("D_ranks")
        D_tanh = step_flag("D_tanh")
        D_prods = step_flag("D_prods")
        D_gate = step_flag("D_gate", CHUNKS)
        D_silus = step_flag("D_silus", CHUNKS)
        D_ms_ready = step_flag("D_ms_ready", CHUNKS)
        D_down = step_flag("D_down")
        WEIGHT_USERS.update({(3, 4), (3, 2)})
        TBANK_D, OBANK_D, GATE, UP, DOWN, MISC = 2, 3, 4, 5, 6, 7

        def D_before_vector(dve, ch):
            for n in range(4):
                ch.mark(nc.vector.tensor_copy(D_mask4[:, n, :], D_mask[:]))
            ch.link(nc.vector.memset(D_v.rearrange("p g h d -> p (g h d)"), 0.0))
            ch.link(nc.vector.memset(eps6[:], 1e-6))
            dve.sem_inc(prepared, 1)

        BEFORE[3, 4] = D_before_vector
        for engine in (1, 2, 3):
            BEFORE[3, engine] = lambda eng, ch: eng.wait_ge(prepared, PREPARED[3])

        def D_pipeline(eng, ch, body):
            body(ch, None, 0)
            if ch:
                ch.restart()
            with eng.Fori(0, STEPS - 1) as i:
                body(ch, i, i + 1)
                if ch:
                    ch.restart()
            body(ch, STEPS - 1, None)

        def D_units(units, forward):
            for n in range(D_UNITS + 3):
                units(n)
                forward(n)

        def D_vector(dve, ch):
            def body(ch, i, s):
                if s is not None:
                    norm_stats(ch, s)
                if i is not None:
                    dve.wait_ge(D_tanh.sem, D_tanh.at(i))
                    nc.vector.scalar_tensor_tensor(D_prod[0:16, :], D_mod[0:16, :], 0.1, PS[0:16, MISC, 0:D],
                                                   ALU.mult, ALU.mult).then_inc(D_prods.sem, 1)
                if s is not None:
                    for g in range(G):
                        dve.wait_ge(rstd_ready.sem, rstd_ready.at(s, g))
                        ch.link(nc.vector.tensor_scalar(xn[:, g, :], X[:, s * G + g, :], moments[:, g, 0:1], rstd[:, g, :],
                                                        ALU.subtract, ALU.mult))
                        nc.vector.tensor_tensor_reduce(D_xb[:, g, :], xn[:, g, :], xn[:, g, :], 1.0 / D, 0.0, ALU.mult, ALU.add,
                                                       moments[:, g, 1:2]).then_inc(D_ms.sem, 1)
                    for g in range(G):
                        dve.wait_ge(D_rstd2.sem, D_rstd2.at(s, g))
                        nc.vector.tensor_scalar(D_xb[:, g, :], xn[:, g, :], rstd[:, g, :], None, ALU.mult).then_inc(xn_ready.sem, 1)

                def product(c):
                    dve.wait_ge(D_silus.sem, D_silus.at(i, c))
                    nc.vector.tensor_tensor(D_m[:, c % 2], D_silu[:, c % 2], PS[:, UP, :], ALU.mult).then_inc(D_ms_ready.sem, 1)

                def units(n):
                    if s is None:
                        return
                    if n < D_UNITS:
                        g, j = divmod(n, 4)
                        mx = small[:, g, 4 * j:4 * j + 4]
                        dve.wait_ge(D_scores.sem, D_scores.at(s, n))
                        ch.link(nc.vector.tensor_reduce(mx, heads4(n % 2), AX.X, ALU.max))
                        nc.vector.tensor_scalar(mx, mx, -DD ** -0.5, None, ALU.mult).then_inc(D_max.sem, 1)
                    if 0 <= n - 1 < D_UNITS:
                        u = n - 1
                        g, j = divmod(u, 4)
                        rs = small[:, g, 32 + 4 * j:36 + 4 * j]
                        dve.wait_ge(D_exp.sem, D_exp.at(s, u))
                        ch.link(nc.vector.reciprocal(rs, small[:, g, 16 + 4 * j:20 + 4 * j]))
                        nc.vector.tensor_tensor(D_p[:, u % 4], D_p[:, u % 4], over_head(rs), ALU.mult).then_inc(D_ps.sem, 1)

                def forward(n):
                    if i is not None and n in (2, 5):
                        product(2 if n == 2 else 3)
                    if s is not None and n == 6:
                        dve.wait_ge(xT_ready.sem, xT_ready.at(s, G - 1))
                        for g in range(G):
                            ch.mark(nc.vector.scalar_tensor_tensor(X[:, s * G + g, :], xn[:, g, :], gates[:, 1, 1:2],
                                                                   X[:, s * G + g, :], ALU.mult, ALU.add))
                        for k in range(KC):
                            last = nc.vector.tensor_scalar(x2T[:, k].rearrange("p g t -> p (g t)"), D_raw[:, k].rearrange("p g t -> p (g t)"),
                                                           D_col[:, 2 + k:3 + k], None, ALU.mult)
                        last.then_inc(D_x2.sem, 1)
                    if i is not None and n == 8:
                        dve.wait_ge(D_down.sem, D_down.at(i))
                        for g in range(G):
                            add_to_x(dve, ch, i * G + g, PS[:, DOWN, g * D:(g + 1) * D], gates[:, 1, 1:2])

                if i is not None:
                    product(0)
                    product(1)
                D_units(units, forward)

            D_pipeline(dve, ch, body)

        def D_gpsimd(pool, ch):
            def body(ch, i, s):
                if s is None:
                    return
                norm_gpsimd(pool, ch, s)
                for g in range(G):
                    pool.wait_ge(D_ms.sem, D_ms.at(s, g))
                    ch.link(nc.gpsimd.tensor_tensor(rstd[:, g, :], moments[:, g, 1:2], eps6[:], ALU.add))
                    nc.gpsimd.tensor_tensor(rstd[:, g, :], rstd[:, g, :], minus_half[:, 0:1], ALU.pow).then_inc(D_rstd2.sem, 1)

            D_pipeline(pool, ch, body)

        def D_scalar(act, ch):
            def body(ch, i, s):
                def silu(c):
                    act.wait_ge(D_gate.sem, D_gate.at(i, c))
                    nc.scalar.activation(D_silu[:, c % 2], PS[:, GATE, :], ACT.Silu).then_inc(D_silus.sem, 1)

                if i is not None:
                    act.wait_ge(D_ranks.sem, D_ranks.at(i))
                    nc.scalar.activation(D_mod[0:16, :], PS[0:16, MISC, D:2 * D], ACT.Tanh).then_inc(D_tanh.sem, 1)
                    silu(0)
                if s is not None:
                    act.wait_ge(xnT_done.sem, xnT_done.at(s, G - 1))
                    src = PS[:, MISC, :].rearrange("p (k x) -> p k x", k=KC)
                    for k in range(KC):
                        nc.scalar.activation(xT[:, k].rearrange("p g t -> p (g t)"), src[:, k], ACT.Copy, scale=D_col[:, k:k + 1])
                    last = nc.scalar.copy(D_raw.rearrange("p k g t -> p (k g t)"), PS[:, MISC, :])
                    last.then_inc(xT_ready.sem, G)
                    act.wait_ge(D_qkv.sem, D_qkv.at(s))
                    nc.scalar.copy(D_qk.rearrange("p n t x -> p (n t x)"), PS[:, 0:4, :].rearrange("p a b -> p (a b)"))
                    nc.scalar.copy(D_v[:, :, :, 0:DD], PS[:, MISC, :].rearrange("p (g h d) -> p g h d", g=G, h=16)).then_inc(D_qkvs.sem, 1)
                if i is not None:
                    silu(1)

                def units(n):
                    if s is None:
                        return
                    if n < D_UNITS:
                        g, j = divmod(n, 4)
                        act.wait_ge(D_max.sem, D_max.at(s, n))
                        if n >= 4:
                            act.wait_ge(D_pturned.sem, D_pturned.at(s, n - 4))
                        for tt in range(4):
                            m = 4 * j + tt
                            last = nc.scalar.activation(D_p[:, n % 4, tt, :], PS[:, n % 2, tt * P:(tt + 1) * P], ACT.Exp,
                                                        scale=DD ** -0.5, bias=small[:, g, m:m + 1], accum_out=small[:, g, 16 + m:17 + m])
                        last.then_inc(D_exp.sem, 1)
                    if 0 <= n - 2 < D_UNITS:
                        u = n - 2
                        act.wait_ge(D_pturned.sem, D_pturned.at(s, u))
                        if u >= 2:
                            act.wait_ge(D_pv.sem, D_pv.at(s, u - 2))
                        nc.scalar.copy(D_pT[:, u % 2].rearrange("p a b -> p (a b)"), PS[:, TBANK_D, :]).then_inc(D_pTs.sem, 1)
                    if n - 3 in (3, 7):
                        g = (n - 3) // 4
                        act.wait_ge(D_pv.sem, D_pv.at(s, n - 3))
                        nc.scalar.copy(D_oT[:, :, g, :], PS[:, OBANK_D, :].rearrange("p (t q) -> p t q", t=4)).then_inc(D_oTs.sem, 1)

                def forward(n):
                    if i is not None and n in (2, 5):
                        silu(2 if n == 2 else 3)

                D_units(units, forward)
                if s is not None:
                    act.wait_ge(D_ao.sem, D_ao.at(s))
                    nc.scalar.copy(D_aoT.rearrange("p a b -> p (a b)"), PS[:, MISC, :]).then_inc(D_aos.sem, 1)

            D_pipeline(act, ch, body)

        def D_tensor(pe):
            pair = lambda src, k: src[:, k].rearrange("p g t -> p (g t)")

            def body(ch, i, s):
                def ranks():
                    pe.wait_ge(D_x2.sem, D_x2.at(i))
                    pe.wait_ge(D_aos.sem, D_aos.at(i))
                    for k in range(KC):
                        nc.tensor.matmul(PS[0:16, MISC, 0:D], wD["a"][:, k, :], pair(x2T, k), start=k == 0, stop=k == KC - 1)
                    for k in range(KC):
                        last = nc.tensor.matmul(PS[0:16, MISC, D:2 * D], wD["a"][:, k, :], D_aoT[:, k, :], start=k == 0, stop=k == KC - 1)
                    last.then_inc(D_ranks.sem, 1)

                def up(c):
                    if c:
                        pe.wait_ge(D_ms_ready.sem, D_ms_ready.at(i, c - 1))
                    for f in range(2):
                        for k in range(KC):
                            at = (2 * c + f) * P
                            nc.tensor.matmul(PS[:, UP, f * D:(f + 1) * D], wD["up"][:, k, at:at + P], pair(x2T, k),
                                             start=k == 0, stop=k == KC - 1)

                def gate(c):
                    if c == 0:
                        pe.wait_ge(D_prods.sem, D_prods.at(i))
                    for f in range(2):
                        dst, at = PS[:, GATE, f * D:(f + 1) * D], (2 * c + f) * P
                        for k in range(KC):
                            nc.tensor.matmul(dst, wD["in"][:, k, at:at + P], pair(x2T, k), start=k == 0, stop=False)
                        last = nc.tensor.matmul(dst, wD["b"][0:16, at:at + P], D_prod[0:16, :], start=False, stop=True)
                    last.then_inc(D_gate.sem, 1)

                def down(c):
                    pe.wait_ge(D_ms_ready.sem, D_ms_ready.at(i, c))
                    if c == 0:
                        pe.wait_ge(x_done.sem, x_done.nth(i, -1))
                    for f in range(2):
                        for g in range(G):
                            last = nc.tensor.matmul(PS[:, DOWN, g * D:(g + 1) * D], D_m[:, c % 2, f * D + g * P:f * D + (g + 1) * P],
                                                    wD["down"][:, 2 * c + f, :], start=c == 0 and f == 0 and g == 0,
                                                    stop=c == CHUNKS - 1 and f == 1 and g == G - 1)
                    if c == CHUNKS - 1:
                        last.then_inc(D_down.sem, 1)

                if i is not None:
                    ranks()
                    up(0)
                    gate(0)
                if s is not None:
                    for g in range(G):
                        pe.wait_ge(xn_ready.sem, xn_ready.at(s, g))
                        for k in range(KC):
                            at = (k * G + g) * P
                            last = nc.tensor.transpose(PS[:, MISC, at:at + P], D_xb[:, g, k * P:(k + 1) * P], ident[:])
                        last.then_inc(xnT_done.sem, 1)
                if i is not None:
                    down(0)
                if s is not None:
                    pe.wait_ge(xT_ready.sem, xT_ready.at(s, G - 1))
                    for n in range(2):
                        for tt in range(4):
                            for k in range(KC):
                                nc.tensor.matmul(PS[:, 2 * n + tt // 2, (tt % 2) * D:(tt % 2 + 1) * D], wD["qk"[n]][:, k, tt * P:(tt + 1) * P],
                                                 pair(xT, k), start=k == 0, stop=k == KC - 1)
                    for g in range(G):
                        for k in range(KC):
                            last = nc.tensor.matmul(PS[:, MISC, g * D:(g + 1) * D], xT[:, k, g, :], wD["v"][:, k, :], start=k == 0, stop=k == KC - 1)
                    last.then_inc(D_qkv.sem, 1)
                if i is not None:
                    up(1)
                    gate(1)

                def scores(u):
                    g, j = divmod(u, 4)
                    if u >= 2:
                        pe.wait_ge(D_exp.sem, D_exp.at(s, u - 2))
                    elif u == 0:
                        pe.wait_ge(D_qkvs.sem, D_qkvs.at(s))
                    nc.tensor.matmul(PS[:, u % 2, :], ident_b[:], D_mask4[:].rearrange("p a b -> p (a b)"), start=True, stop=False)
                    rows_ = slice(32 * j, 32 * j + DD)
                    for tt in range(4):
                        last = nc.tensor.matmul(PS[:, u % 2, tt * P:(tt + 1) * P], D_qk[rows_, 0, tt, g * P:(g + 1) * P],
                                                D_qk[rows_, 1, tt, g * P:(g + 1) * P], start=False, stop=tt == 3)
                    last.then_inc(D_scores.sem, 1)

                def turn(u):
                    pe.wait_ge(D_ps.sem, D_ps.at(s, u))
                    if u:
                        pe.wait_ge(D_pTs.sem, D_pTs.at(s, u - 1))
                    for tt in range(4):
                        last = nc.tensor.transpose(PS[:, TBANK_D, tt * P:(tt + 1) * P], D_p[:, u % 4, tt, :], ident[:])
                    last.then_inc(D_pturned.sem, 1)

                def weigh(u):
                    g, j = divmod(u, 4)
                    pe.wait_ge(D_pTs.sem, D_pTs.at(s, u))
                    if u == 4:
                        pe.wait_ge(D_oTs.sem, D_oTs.at(s, 0))
                    for tt in range(4):
                        last = nc.tensor.matmul(PS[32 * j:32 * j + 32, OBANK_D, tt * P:(tt + 1) * P], D_v[:, g, 4 * tt + j, :],
                                                D_pT[:, u % 2, tt, :], start=True, stop=True)
                    last.then_inc(D_pv.sem, 1)

                def units(n):
                    if s is None:
                        return
                    for lag, stage in ((0, scores), (2, turn), (3, weigh)):
                        if 0 <= n - lag < D_UNITS:
                            stage(n - lag)

                def forward(n):
                    if i is None:
                        return
                    if n in (1, 4, 7):
                        down({1: 1, 4: 2, 7: 3}[n])
                    if n in (2, 5):
                        up(2 if n == 2 else 3)
                        gate(2 if n == 2 else 3)

                D_units(units, forward)
                if s is not None:
                    pe.wait_ge(D_oTs.sem, D_oTs.at(s, 1))
                    for m in range(KC):
                        for tt in range(4):
                            last = nc.tensor.matmul(PS[:, MISC, m * D:(m + 1) * D], wD["o"][:, tt, m * P:(m + 1) * P], pair(D_oT, tt),
                                                    start=tt == 0, stop=tt == 3)
                    last.then_inc(D_ao.sem, 1)

            D_pipeline(pe, None, body)

        LOOPS[3] = (None, D_tensor, D_scalar, D_gpsimd, D_vector)
        SUB.append((None, None, None, None, None))
        HE, DE, TE = 16, 16, 8
        ROWS = 64
        n_ = LATE_4
        wE = {}
        for name, a, w in (("q", KC, D), ("kv", KC, 2 * D), ("p", KC, D)):
            wE[name], n_ = view(late, n_, a, w)
            LOADS[4].append((wE[name], "E_" + name))
        E_bias, n_ = view(late, n_, 4 * D)
        LOADS[4].append((E_bias, "E_bias"))
        LATE_5 = n_
        E_kT, _ = view(early, 0, TE, NB * P, dt=BF16)
        E_vs = sb("E_vs", [P, 2, D])
        E_v, _ = view(work[:, 0, :], 4096, NB, D)
        E_vq, _ = view(work[:, 1, :], 5120, NB, D, dt=BF16)
        E_ = [{} for _ in range(G)]
        for g in range(G):
            w, n_ = work[:, g, :], 0
            E_[g]["stack"], n_ = view(w, n_, HE, 4, DE, dt=BF16)
            E_[g]["qT"], n_ = view(w, n_, TE, P, dt=BF16)
            E_[g]["t"], n_ = view(w, n_, D)
            E_[g]["u"], n_ = view(w, n_, D)
            E_[g]["e"], n_ = view(w, n_, 1024)
            E_[g]["pb"], n_ = view(w, n_, 1024, dt=BF16)
            E_[g]["pT"], n_ = view(w, n_, NB, P, dt=BF16)
            E_[g]["oT"], n_ = view(w, n_, KC, P)
        assert n_ <= 4096
        E_kv = flag("E_kv")
        E_kstack = flag("E_kstack")
        E_kturned = flag("E_kturned")
        E_kTs = flag("E_kTs")
        E_vmax = sem("E_vmax")
        E_vall = sem("E_vall")
        E_q = flag("E_q")
        E_qread = flag("E_qread")
        E_outread = flag("E_outread")
        E_qstack = flag("E_qstack")
        E_qturned = flag("E_qturned")
        E_qTs = flag("E_qTs")
        E_scores = flag("E_scores", HE)
        E_max = flag("E_max", HE)
        E_exp = flag("E_exp", HE)
        E_pb = flag("E_pb", HE)
        E_pturned = flag("E_pturned", HE)
        E_pT = flag("E_pT", HE)
        E_pv = flag("E_pv", HE)
        E_o = flag("E_o")
        E_oturned = flag("E_oturned")
        E_oTs = flag("E_oTs")
        E_out = flag("E_out")
        WEIGHT_USERS.add((4, 4))
        heads16 = lambda v: v.rearrange("p (h d) -> p h d", h=16)
        over_d = lambda v: v.unsqueeze(2).broadcast_to([P, HE, DE])

        def E_before_sync(sp):
            with sp.Fori(0, STEPS) as i:
                ctx_sync(sp, i)
            ctx_base[0] += STEPS

        def E_before_tensor(pe, ch):
            pe.wait_ge(x_done.sem, 4 * NB)
            with pe.Fori(0, STEPS) as i:
                for g in range(G):
                    ctx_loaded(pe, i, g)
                    for k in range(KC):
                        last = nc.tensor.matmul(bank(g, 0), ctxT[:, g, k, :], wE["kv"][:, k, :], start=k == 0, stop=k == KC - 1)
                    last.then_inc(E_kv.sem, 1)
                for g in range(G):
                    pe.wait_ge(E_kstack.sem, E_kstack.at(i, g))
                    for tt in range(TE):
                        last = nc.tensor.transpose(bank(g, 1).bitcast(BF16)[:, tt * P:(tt + 1) * P],
                                                   E_[g]["stack"][:, 2 * tt:2 * tt + 2].rearrange("p a b c -> p (a b c)"), ident_b[:])
                        if tt == 0:
                            last.then_inc(ctx_read[g], 1)
                    last.then_inc(E_kturned.sem, 1)
            pe.wait_ge(prepared, PREPARED[4])

        def E_before_scalar(act, ch):
            with act.Fori(0, STEPS) as i:
                for g in range(G):
                    b = i * G + g
                    act.wait_ge(E_kturned.sem, E_kturned.at(i, g))
                    nc.scalar.copy(E_kT.rearrange("p t (b k) -> p t b k", b=NB)[:, :, b, :],
                                   bank(g, 1).bitcast(BF16).rearrange("p (t k) -> p t k", t=TE)).then_inc(E_kTs.sem, 1)

        def step_of(ch, x, s, r):
            ch.link(nc.vector.tensor_reduce(s, heads16(x), AX.X, ALU.max, apply_absolute_value=True))
            ch.link(nc.vector.tensor_scalar(s, s, 1.0 / 127, 1e-8, ALU.mult, ALU.max))
            ch.link(nc.vector.reciprocal(r, s))

        def E_before_vector(dve, ch):
            for g in range(G):
                ch.mark(nc.vector.memset(E_[g]["stack"].rearrange("p a b c -> p (a b c)"), 0.0))
            ch.restart()
            with dve.Fori(0, STEPS) as i:
                for g in range(G):
                    b = i * G + g
                    e = E_[g]
                    dve.wait_ge(E_kv.sem, E_kv.at(i, g))
                    nc.vector.tensor_tensor(E_v[:, b, :], bank(g, 0)[:, D:2 * D], E_bias[:, 2 * D:3 * D], ALU.add)
                    ch.link(nc.vector.tensor_tensor(e["t"], bank(g, 0)[:, 0:D], E_bias[:, D:2 * D], ALU.add))
                    s, r = small[:, g, 0:16], small[:, g, 16:32]
                    step_of(ch, e["t"], s, r)
                    ch.link(nc.vector.tensor_tensor(heads16(e["t"]), heads16(e["t"]), over_d(r), ALU.mult))
                    ch.link(nc.vector.tensor_scalar(e["t"], e["t"], MAGIC, MAGIC, ALU.add, ALU.subtract))
                    ch.link(nc.vector.tensor_tensor(heads16(e["t"]), heads16(e["t"]), over_d(s), ALU.mult))
                    ch.link(nc.vector.tensor_copy(e["stack"][:, :, 0, :], heads16(e["t"])))
                    ch.link(nc.vector.tensor_tensor(heads16(e["u"]), heads16(e["t"]), e["stack"][:, :, 0, :], ALU.subtract))
                    ch.link(nc.vector.tensor_copy(e["stack"][:, :, 1, :], heads16(e["u"])))
                    nc.vector.tensor_tensor(e["stack"][:, :, 2, :], heads16(e["u"]), e["stack"][:, :, 1, :], ALU.subtract).then_inc(E_kstack.sem, 1)
                for g in range(G):
                    dve.wait_ge(E_kTs.sem, E_kTs.at(i, g))
                    ch.link(nc.vector.memset(E_[g]["stack"][:, 0, 3, :], 0.0))
                ch.restart()
            vm = E_vs[:, 1, :]
            nc.vector.tensor_reduce(vm, E_v.rearrange("p b d -> p d b"), AX.X, ALU.max, apply_absolute_value=True).then_inc(E_vmax, 1)
            dve.wait_ge(E_vall, 1)
            ch.link(nc.vector.tensor_scalar(E_vs[:, 0, :], E_vs[:, 0, :], 1.0 / 127, 1e-8, ALU.mult, ALU.max))
            ch.link(nc.vector.reciprocal(E_vs[:, 1, :], E_vs[:, 0, :]))
            ch.link(nc.vector.tensor_tensor(E_v, E_v, E_vs[:, 1, :].unsqueeze(1).broadcast_to([P, NB, D]), ALU.mult))
            nc.vector.tensor_scalar(E_vq, E_v, MAGIC, MAGIC, ALU.add, ALU.subtract).then_inc(prepared, 1)

        def E_before_gpsimd(pool, ch):
            pool.wait_ge(E_vmax, 1)
            nc.gpsimd.partition_all_reduce(E_vs[:, 0, :], E_vs[:, 1, :], P, bass.bass_isa.ReduceOp.max).then_inc(E_vall, 1)

        BEFORE.update({(4, 0): E_before_sync, (4, 1): E_before_tensor, (4, 2): E_before_scalar, (4, 3): E_before_gpsimd, (4, 4): E_before_vector})

        E_UNITS, E_DEPTH = HE * G, 8
        E_X, E_Q, E_STACK, E_OT, E_PROJ = 14, 16, 30, 36, 38

        def piece(n):
            g = n % G
            return (n - g if n - g in (E_X, E_Q, E_STACK, E_OT, E_PROJ) else None), g

        def E_slots(ch, i, slots, stages):
            for n in slots:
                what, g = piece(n)
                if last_step(i) and what in (E_X, E_Q, E_STACK):
                    what = None
                for lag, stage in stages:
                    if lag is None:
                        stage(ch, i, n, what, g)
                    elif n - lag >= 0 and not (last_step(i) and n - lag >= E_UNITS):
                        stage(ch, i, n - lag)

        def E_pipeline(eng, ch, first, stages):
            first(ch)
            E_slots(ch, 0, range(0, E_DEPTH), stages)
            if ch:
                ch.restart()
            with eng.Fori(0, STEPS - 1) as i:
                E_slots(ch, i, range(E_DEPTH, E_UNITS + E_DEPTH), stages)
                if ch:
                    ch.restart()
            E_slots(ch, STEPS - 1, range(E_DEPTH, E_UNITS + E_DEPTH), stages)

        head_of = lambda u: (u % E_UNITS) // G

        def E_tensor(pe):
            def turn_x(i, g):
                pe.wait_ge(xn_ready.sem, xn_ready.at(i, g))
                for k in range(KC):
                    last = nc.tensor.transpose(bank(g, 1)[:, k * P:(k + 1) * P], xn[:, g, k * P:(k + 1) * P], ident[:])
                last.then_inc(xnT_done.sem, 1)

            def project_q(i, g):
                pe.wait_ge(xT_ready.sem, xT_ready.at(i, g))
                for k in range(KC):
                    last = nc.tensor.matmul(bank(g, 1)[:, 0:D], xT[:, k, g, :], wE["q"][:, k, :], start=k == 0, stop=k == KC - 1)
                last.then_inc(E_q.sem, 1)

            def turn_stack(i, g):
                pe.wait_ge(E_qstack.sem, E_qstack.at(i, g))
                for tt in range(TE):
                    last = nc.tensor.transpose(bank(g, 1).bitcast(BF16)[:, tt * P:(tt + 1) * P],
                                               E_[g]["stack"][:, 2 * tt:2 * tt + 2].rearrange("p a b c -> p (a b c)"), ident_b[:])
                last.then_inc(E_qturned.sem, 1)

            def scores(ch, i, u):
                h, g = head_of(u), u % G
                if h == 0:
                    pe.wait_ge(E_qTs.sem, E_qTs.nth(i, g + G * (u // E_UNITS)))
                if u >= G:
                    pe.wait_ge(E_exp.sem, E_exp.nth(i, u - G))
                r = slice(ROWS * (h % 2), ROWS * (h % 2) + ROWS)
                for n in range(2):
                    last = nc.tensor.matmul(bank(g, 2 + n), E_[g]["qT"][r, h // 2, :], E_kT[r, h // 2, n * 512:(n + 1) * 512],
                                            start=True, stop=True)
                last.then_inc(E_scores.sem, 1)

            def turn(ch, i, u):
                g = u % G
                pe.wait_ge(E_pb.sem, E_pb.nth(i, u))
                if u >= G:
                    pe.wait_ge(E_pT.sem, E_pT.nth(i, u - G))
                what, _ = piece(u + 2)
                if what == E_OT:
                    pe.wait_ge(E_oTs.sem, E_oTs.at(i, g))
                elif what == E_PROJ:
                    pe.wait_ge(E_outread.sem, E_outread.at(i, g))
                elif not last_step(i):
                    read = {E_X: xT_ready, E_Q: E_qread, E_STACK: E_qTs, None: None}[what]
                    if read:
                        pe.wait_ge(read.sem, read.at(i + 1, g))
                for b in range(NB):
                    last = nc.tensor.transpose(bank(g, 1).bitcast(BF16)[:, b * P:(b + 1) * P], E_[g]["pb"][:, b * P:(b + 1) * P], ident_b[:])
                last.then_inc(E_pturned.sem, 1)

            def weigh(ch, i, u):
                h, g = head_of(u), u % G
                pe.wait_ge(E_pT.sem, E_pT.nth(i, u))
                if u >= E_UNITS and h == 0:
                    pe.wait_ge(E_o.sem, E_o.at(i, g))
                for b in range(NB):
                    last = nc.tensor.matmul(bank(g, 0)[:, h * DE:(h + 1) * DE], E_[g]["pT"][:, b, :], E_vq[:, b, h * DE:(h + 1) * DE],
                                            start=b == 0, stop=b == NB - 1)
                last.then_inc(E_pv.sem, 1)

            def extra(ch, i, n, what, g):
                if what is None:
                    return
                if not (last_step(i) and n - 4 >= E_UNITS):
                    pe.wait_ge(E_pT.sem, E_pT.nth(i, n - 4))
                if what == E_X:
                    turn_x(i + 1, g)
                if what == E_Q:
                    project_q(i + 1, g)
                if what == E_STACK:
                    turn_stack(i + 1, g)
                if what == E_OT:
                    pe.wait_ge(E_o.sem, E_o.at(i, g))
                    for k in range(KC):
                        last = nc.tensor.transpose(bank(g, 1)[:, k * P:(k + 1) * P], E_[g]["t"][:, k * P:(k + 1) * P], ident[:])
                    last.then_inc(E_oturned.sem, 1)
                if what == E_PROJ:
                    pe.wait_ge(E_oTs.sem, E_oTs.at(i, g))
                    for k in range(KC):
                        last = nc.tensor.matmul(bank(g, 1)[:, 0:D], E_[g]["oT"][:, k, :], wE["p"][:, k, :], start=k == 0, stop=k == KC - 1)
                    last.then_inc(E_out.sem, 1)

            def first(ch):
                for part in (turn_x, project_q, turn_stack):
                    for g in range(G):
                        part(0, g)

            E_pipeline(pe, None, first, [(None, extra), (0, scores), (2, turn), (3, weigh)])

        def E_scalar(act, ch):
            def x_T(i, g):
                act.wait_ge(xnT_done.sem, xnT_done.at(i, g))
                nc.scalar.copy(xT[:, :, g, :], bank(g, 1)[:, 0:D].rearrange("p (k t) -> p k t", k=KC)).then_inc(xT_ready.sem, 1)

            def q_T(i, g):
                act.wait_ge(E_qturned.sem, E_qturned.at(i, g))
                nc.scalar.copy(E_[g]["qT"].rearrange("p a b -> p (a b)"), bank(g, 1).bitcast(BF16)).then_inc(E_qTs.sem, 1)

            def p_T(ch, i, u):
                g = u % G
                act.wait_ge(E_pturned.sem, E_pturned.nth(i, u))
                if u >= G:
                    act.wait_ge(E_pv.sem, E_pv.nth(i, u - G))
                nc.scalar.copy(E_[g]["pT"].rearrange("p a b -> p (a b)"), bank(g, 1).bitcast(BF16)).then_inc(E_pT.sem, 1)

            def exps(ch, i, u):
                h, g = head_of(u), u % G
                act.wait_ge(E_max.sem, E_max.nth(i, u))
                if u >= G:
                    act.wait_ge(E_pb.sem, E_pb.nth(i, u - G))
                nc.scalar.activation(E_[g]["e"], banks(g, 2), ACT.Exp, scale=small[:, g, h:h + 1],
                                     bias=small[:, g, 48 + h:49 + h], accum_out=small[:, g, 64 + h:65 + h]).then_inc(E_exp.sem, 1)

            def extra(ch, i, n, what, g):
                if what == E_X:
                    x_T(i + 1, g)
                if what == E_STACK:
                    act.wait_ge(E_scores.sem, E_scores.nth(i, E_UNITS - G + g))
                    q_T(i + 1, g)
                if what == E_OT:
                    act.wait_ge(E_oturned.sem, E_oturned.at(i, g))
                    nc.scalar.copy(E_[g]["oT"].rearrange("p a b -> p (a b)"), bank(g, 1)[:, 0:D]).then_inc(E_oTs.sem, 1)

            def first(ch):
                for part in (x_T, q_T):
                    for g in range(G):
                        part(0, g)

            E_pipeline(act, ch, first, [(2, exps), (3, p_T), (None, extra)])

        def E_gpsimd(pool, ch):
            def extra(ch, i, n, what, g):
                if n == E_DEPTH and not last_step(i):
                    norm_gpsimd(pool, ch, i + 1)

            E_pipeline(pool, ch, lambda ch: norm_gpsimd(pool, ch, 0), [(None, extra)])

        def E_vector(dve, ch):
            def normed_x(i):
                for g in range(G):
                    dve.wait_ge(rstd_ready.sem, rstd_ready.at(i, g))
                    nc.vector.tensor_scalar(xn[:, g, :], X[:, i * G + g, :], moments[:, g, 0:1], rstd[:, g, :],
                                            ALU.subtract, ALU.mult).then_inc(xn_ready.sem, 1)

            def read_q(i, g):
                dve.wait_ge(E_q.sem, E_q.at(i, g))
                nc.vector.tensor_tensor(E_[g]["t"], bank(g, 1)[:, 0:D], E_bias[:, 0:D], ALU.add).then_inc(E_qread.sem, 1)

            def quantised_q(ch, i, g):
                e = E_[g]
                dve.wait_ge(E_qread.sem, E_qread.at(i, g))
                ch.link(nc.vector.tensor_scalar(e["t"], e["t"], DE ** -0.5, None, ALU.mult))
                s, r = small[:, g, 96:112], small[:, g, 16:32]
                step_of(ch, e["t"], s, r)
                ch.link(nc.vector.tensor_tensor(heads16(e["u"]), heads16(e["t"]), over_d(r), ALU.mult))
                for part in range(3):
                    last = nc.vector.tensor_scalar(e["stack"][:, :, part, :], heads16(e["u"]), MAGIC, MAGIC, ALU.add, ALU.subtract)
                last.then_inc(E_qstack.sem, 1)

            def switch(ch, i, g):
                ch.mark(nc.vector.tensor_copy(small[:, g, 0:16], small[:, g, 96:112]))
                ch.link(nc.vector.tensor_scalar(small[:, g, 32:48], small[:, g, 96:112], -1.0, None, ALU.mult))

            def maximum(ch, i, u):
                h, g = head_of(u), u % G
                if u >= E_UNITS and h == 0:
                    switch(ch, i, g)
                dve.wait_ge(E_scores.sem, E_scores.nth(i, u))
                ch.link(nc.vector.tensor_reduce(small[:, g, 80:81], banks(g, 2), AX.X, ALU.max))
                nc.vector.tensor_scalar(small[:, g, 48 + h:49 + h], small[:, g, 80:81], small[:, g, 32 + h:33 + h],
                                        5.541263545158426, ALU.mult, ALU.add).then_inc(E_max.sem, 1)

            def whole(ch, i, u):
                h, g = head_of(u), u % G
                dve.wait_ge(E_exp.sem, E_exp.nth(i, u))
                if u >= G:
                    dve.wait_ge(E_pturned.sem, E_pturned.nth(i, u - G))
                nc.vector.tensor_scalar(E_[g]["pb"], E_[g]["e"], MAGIC, MAGIC, ALU.add, ALU.subtract).then_inc(E_pb.sem, 1)
                if h == HE - 1:
                    ch.link(nc.vector.reciprocal(small[:, g, 16:32], small[:, g, 64:80]))

            def reads(ch, i, n, what, g):
                if what == E_PROJ:
                    dve.wait_ge(E_out.sem, E_out.at(i, g))
                    nc.vector.tensor_tensor(E_[g]["u"], bank(g, 1)[:, 0:D], E_bias[:, 3 * D:4 * D], ALU.add).then_inc(E_outread.sem, 1)
                    dve.wait_ge(E_outread.sem, E_outread.at(i, g))
                    add_to_x(dve, ch, i * G + g, E_[g]["u"], gates[:, 0, 2:3])
                if what == E_Q:
                    read_q(i + 1, g)

            def extra(ch, i, n, what, g):
                if n in (E_UNITS + 2, E_UNITS + 3):
                    b = n - E_UNITS - 2
                    e = E_[b]
                    dve.wait_ge(E_pv.sem, E_pv.at(i, b, HE - 1))
                    ch.link(nc.vector.tensor_tensor(heads16(e["t"]), heads16(bank(b, 0)[:, 0:D]), over_d(small[:, b, 16:32]), ALU.mult))
                    nc.vector.tensor_tensor(e["t"], e["t"], E_vs[:, 0, :], ALU.mult).then_inc(E_o.sem, 1)
                if last_step(i):
                    return
                if n == E_DEPTH:
                    norm_stats(ch, i + 1)
                if n == E_DEPTH + 2:
                    normed_x(i + 1)
                if n in (E_Q + 3, E_Q + 6):
                    quantised_q(ch, i + 1, (n - E_Q) // 3 - 1)

            def first(ch):
                norm_stats(ch, 0)
                normed_x(0)
                for g in range(G):
                    read_q(0, g)
                for g in range(G):
                    quantised_q(ch, 0, g)
                    switch(ch, 0, g)

            E_pipeline(dve, ch, first, [(None, reads), (2, whole), (None, extra), (0, maximum)])

        LOOPS[4] = (None, E_tensor, E_scalar, E_gpsimd, E_vector)
        SUB.append((None, None, None, None, None))
        NE = 8
        n_ = LATE_5
        wF = {}
        for name, a, w in (("gate", KC, NE), ("w1", KC, NE * P), ("w2", NE, D), ("sw1", KC, D), ("sw2", KC, D)):
            wF[name], n_ = view(late, n_, a, w)
            LOADS[5].append((wF[name], "F_" + name))
        wF["b2"], n_ = view(late, n_, D)
        wF["sb2"], n_ = view(late, n_, D)
        LOADS[5] += [(wF["b2"][0:NE, :], "F_b2"), (wF["sb2"][0:1, :], "F_sb2")]
        LATE_6 = n_
        F_col = sb("F_col", [P, 10])
        LOADS[5].append((F_col[:], "F_col"))
        F_h, _ = view(work[:, 0, :], 0, 10, D)
        F_ = [{} for _ in range(G)]
        for g in range(G):
            w, n_ = work[:, g, :], 2560
            F_[g]["acc"], n_ = view(w, n_, D)
            F_[g]["gT"], n_ = view(w, n_, P)
        F_logits = flag("F_logits")
        F_diff = flag("F_diff")
        F_ratio = flag("F_ratio")
        F_gates = flag("F_gates")
        F_gturned = flag("F_gturned")
        F_gTs = flag("F_gTs")
        F_hidden = step_flag("F_hidden", 5)
        F_hs = step_flag("F_hs", 5)
        F_shared = flag("F_shared")
        F_expert = flag("F_expert", 4)
        F_added = flag("F_added", 4)
        BIG = 3.0e38
        WEIGHT_USERS.add((5, 2))

        def F_vector(dve, ch, i):
            norm_vector(dve, ch, i)
            lo = [small[:, g, 0:8] for g in range(G)]
            top = [small[:, g, 8:16] for g in range(G)]
            look = [small[:, g, 16:32] for g in range(G)]
            rest = [small[:, g, 32:48] for g in range(G)]
            one = [small[:, g, 48:56] for g in range(G)]
            for g in range(G):
                dve.wait_ge(F_logits.sem, F_logits.at(i, g))
                nc.vector.memset(look[g], -BIG)
                ch.link(nc.vector.tensor_copy(lo[g], bank(g, 1)[:, 0:NE]))
                ch.link(nc.vector.max(top[g], lo[g]))
                for n in range(2):
                    last = nc.vector.tensor_copy(look[g][:, 8 * n:8 * n + 1], top[g][:, n:n + 1])
                ch.link(last)
                last = nc.vector.tensor_tensor(small[:, g, 56:57], top[g][:, 1:2], top[g][:, 0:1], ALU.subtract)
                last.then_inc(F_diff.sem, 1)
                ch.link(nc.vector.match_replace(rest[g][:, 0:8], look[g][:, 0:8], lo[g], BIG))
                ch.link(nc.vector.match_replace(rest[g][:, 8:16], look[g][:, 8:16], rest[g][:, 0:8], BIG))
            for g in range(G):
                dve.wait_ge(F_ratio.sem, F_ratio.at(i, g))
                e, s = small[:, g, 57:58], small[:, g, 58:59]
                ch.link(nc.vector.tensor_scalar(s, e, 1.0, None, ALU.add))
                ch.link(nc.vector.reciprocal(s, s))
                ch.link(nc.vector.tensor_tensor(small[:, g, 59:60], e, s, ALU.mult))
                ch.link(nc.vector.tensor_single_scalar(one[g], rest[g][:, 0:8], BIG, ALU.is_equal))
                ch.link(nc.vector.tensor_single_scalar(lo[g], rest[g][:, 8:16], BIG, ALU.is_equal))
                ch.link(nc.vector.tensor_tensor(lo[g], lo[g], one[g], ALU.subtract))
                ch.link(nc.vector.tensor_scalar(lo[g], lo[g], small[:, g, 59:60], None, ALU.mult))
                nc.vector.scalar_tensor_tensor(lo[g], one[g], s, lo[g], ALU.mult, ALU.add).then_inc(F_gates.sem, 1)
            for g in range(G):
                dve.wait_ge(F_shared.sem, F_shared.at(i, g))
                ch.link(nc.vector.tensor_copy(F_[g]["acc"], bank(g, 0)[:, 0:D]))
            for n in range(4):
                for g in range(G):
                    acc = F_[g]["acc"]
                    dve.wait_ge(F_expert.sem, F_expert.at(i, g, n))
                    for m in range(2):
                        last = nc.vector.scalar_tensor_tensor(acc, bank(g, 2 + n % 2)[:, m * D:(m + 1) * D], lo[g][:, 2 * n + m:2 * n + m + 1],
                                                              acc, ALU.mult, ALU.add)
                        if m == 0:
                            ch.link(last)
                    last.then_inc(F_added.sem, 1)
                    dve.wait_ge(F_added.sem, F_added.at(i, g, n))
            for g in range(G):
                add_to_x(dve, ch, i * G + g, F_[g]["acc"], gates[:, 1, 2:3])

        def F_scalar(act, ch, i):
            norm_scalar(act, i)
            for g in range(G):
                act.wait_ge(F_diff.sem, F_diff.at(i, g))
                nc.scalar.activation(small[:, g, 57:58], small[:, g, 56:57], ACT.Exp).then_inc(F_ratio.sem, 1)
            for n in range(5):
                act.wait_ge(F_hidden.sem, F_hidden.at(i, n))
                for m in range(2):
                    last = nc.scalar.activation(F_h[:, 2 * n + m, :], HIDDEN[n % 4][:, m * D:(m + 1) * D], ACT.Gelu,
                                                bias=F_col[:, 2 * n + m:2 * n + m + 1])
                last.then_inc(F_hs.sem, 1)
            for g in range(G):
                act.wait_ge(F_gturned.sem, F_gturned.at(i, g))
                nc.scalar.copy(F_[g]["gT"][0:NE, :], bank(g, 1)[0:NE, 0:P]).then_inc(F_gTs.sem, 1)

        HIDDEN = [bank(0, 2), bank(0, 3), bank(1, 2), bank(1, 3)]

        def F_tensor(pe, i):
            norm_tensor(pe, i)
            for g in range(G):
                pe.wait_ge(xT_ready.sem, xT_ready.at(i, g))
                for k in range(KC):
                    last = nc.tensor.matmul(bank(g, 1)[:, 0:NE], xT[:, k, g, :], wF["gate"][:, k, :], start=k == 0, stop=k == KC - 1)
                last.then_inc(F_logits.sem, 1)
            for n in range(5):
                if n == 4:
                    pe.wait_ge(F_hs.sem, F_hs.at(i, 0))
                for m in range(2):
                    e = 2 * n + m
                    w = wF["w1"][:, :, e * P:(e + 1) * P] if n < 4 else wF["sw1"][:, :, m * P:(m + 1) * P]
                    for k in range(KC):
                        last = nc.tensor.matmul(HIDDEN[n % 4][:, m * D:(m + 1) * D], w[:, k, :], xT[:, k].rearrange("p g t -> p (g t)"),
                                                start=k == 0, stop=k == KC - 1)
                last.then_inc(F_hidden.sem, 1)
            for g in range(G):
                pe.wait_ge(F_gates.sem, F_gates.at(i, g))
                nc.tensor.transpose(bank(g, 1)[0:NE, 0:P], small[:, g, 0:8], ident[:]).then_inc(F_gturned.sem, 1)
            pe.wait_ge(F_hs.sem, F_hs.at(i, 4))
            for g in range(G):
                pe.wait_ge(F_gTs.sem, F_gTs.at(i, g))
                out_ = bank(g, 0)[:, 0:D]
                for m in range(2):
                    nc.tensor.matmul(out_, F_h[:, 8 + m, g * P:(g + 1) * P], wF["sw2"][:, m, :], start=m == 0, stop=False)
                nc.tensor.matmul(out_, ones[0:1, :], wF["sb2"][0:1, :], start=False, stop=False)
                nc.tensor.matmul(out_, F_[g]["gT"][0:NE, :], wF["b2"][0:NE, :], start=False, stop=True).then_inc(F_shared.sem, 1)
            for n in range(4):
                for g in range(G):
                    if n >= 2:
                        pe.wait_ge(F_added.sem, F_added.at(i, g, n - 2))
                    for m in range(2):
                        e = 2 * n + m
                        last = nc.tensor.matmul(bank(g, 2 + n % 2)[:, m * D:(m + 1) * D], F_h[:, e, g * P:(g + 1) * P], wF["w2"][:, e, :],
                                                start=True, stop=True)
                    last.then_inc(F_expert.sem, 1)

        SUB.append((None, F_tensor, F_scalar, B_gpsimd, F_vector))

        LATE_7 = LATE_6
        G_mask8 = sb("G_mask8", [P, NB * P], U8)
        G_on, n_ = view(work[:, 0, :], 4096, NB, P)
        G_off, n_ = view(work[:, 0, :], n_, NB, P)
        LOADS[6].append((G_mask8[:], "G_mask"))
        G_valid = sb("G_valid", [P, NB])
        G_ = [{} for _ in range(G)]
        for g in range(G):
            w, n_ = work[:, g, :], 0
            G_[g]["v"], n_ = view(w, n_, D)
            G_[g]["s"], n_ = view(w, n_, P)
            G_[g]["p"], n_ = view(w, n_, P)
            G_[g]["pT"], n_ = view(w, n_, P)
        v_in = [sem(f"v_in{g}") for g in range(G)]
        G_scores = flag("G_scores")
        G_max = flag("G_max")
        G_exp = flag("G_exp")
        G_pturned = flag("G_pturned")
        G_pT = flag("G_pT")
        G_o = flag("G_o")
        WEIGHT_USERS.add((6, 4))

        def G_before_vector(dve, ch):
            flat = lambda v: v.rearrange("p a b -> p (a b)")
            ch.link(nc.vector.tensor_copy(flat(G_on), G_mask8[:]))
            ch.mark(nc.vector.tensor_scalar(flat(G_off), flat(G_on), 1.0, -NEG, ALU.subtract, ALU.mult))
            ch.mark(nc.vector.tensor_reduce(G_valid[:], G_on, AX.X, ALU.max))

        BEFORE[6, 4] = G_before_vector

        def G_sync(sp, i):
            sp.wait_ge(x_done.sem, i * G + 6 * NB)
            for g in range(G):
                b = i * G + g
                sp.dma_start(ctxT[:, g], t["ctxT"][:, :, b, :]).then_inc(ctx_in[g], 16)
                sp.dma_start(G_[g]["v"], t["ctx"][:, b, :]).then_inc(v_in[g], 16)

        def G_vector(dve, ch, i):
            norm_vector(dve, ch, i)
            for g in range(G):
                b = i * G + g
                dve.wait_ge(G_scores.sem, G_scores.at(i, g))
                s, mx = G_[g]["s"], small[:, g, 0:1]
                ch.link(nc.vector.scalar_tensor_tensor(s, bank(g, 1)[:, 0:P], 1.0 / 16, G_on[:, b, :], ALU.mult, ALU.mult))
                ch.link(nc.vector.tensor_tensor(s, s, G_off[:, b, :], ALU.add))
                nc.vector.tensor_reduce(mx, s, AX.X, ALU.max, negate=True).then_inc(G_max.sem, 1)
            for g in range(G):
                b = i * G + g
                dve.wait_ge(G_exp.sem, G_exp.at(i, g))
                r = small[:, g, 2:3]
                ch.link(nc.vector.reciprocal(r, small[:, g, 1:2]))
                ch.link(nc.vector.tensor_scalar(r, r, gates[:, 0, 3:4], None, ALU.mult))
                ch.link(nc.vector.tensor_tensor(r, r, G_valid[:, bass.ds(b, 1)], ALU.mult))
            for g in range(G):
                dve.wait_ge(G_o.sem, G_o.at(i, g))
                add_to_x(dve, ch, i * G + g, bank(g, 2)[:, 0:D], small[:, g, 2:3])

        def G_scalar(act, ch, i):
            norm_scalar(act, i)
            for g in range(G):
                act.wait_ge(G_max.sem, G_max.at(i, g))
                nc.scalar.activation(G_[g]["p"], G_[g]["s"], ACT.Exp, bias=small[:, g, 0:1], accum_out=small[:, g, 1:2]).then_inc(G_exp.sem, 1)
            for g in range(G):
                act.wait_ge(G_pturned.sem, G_pturned.at(i, g))
                nc.scalar.copy(G_[g]["pT"], bank(g, 1)[:, 0:P]).then_inc(G_pT.sem, 1)

        def G_tensor(pe, i):
            norm_tensor(pe, i)
            for g in range(G):
                ctx_loaded(pe, i, g)
                pe.wait_ge(v_in[g], i * 16 + 16)
                pe.wait_ge(xT_ready.sem, xT_ready.at(i, g))
                for k in range(KC):
                    last = nc.tensor.matmul(bank(g, 1)[:, 0:P], xT[:, k, g, :], ctxT[:, g, k, :], start=k == 0, stop=k == KC - 1)
                last.then_inc(G_scores.sem, 1)
            for g in range(G):
                pe.wait_ge(G_exp.sem, G_exp.at(i, g))
                nc.tensor.transpose(bank(g, 1)[:, 0:P], G_[g]["p"], ident[:]).then_inc(G_pturned.sem, 1)
            for g in range(G):
                pe.wait_ge(G_pT.sem, G_pT.at(i, g))
                nc.tensor.matmul(bank(g, 2)[:, 0:D], G_[g]["pT"], G_[g]["v"], start=True, stop=True).then_inc(G_o.sem, 1)

        SUB.append((G_sync, G_tensor, G_scalar, B_gpsimd, G_vector))

        n_ = LATE_7
        wH = {}
        for name, a, w in (("up", KC, FF), ("gate", KC, FF), ("down", FC, D)):
            wH[name], n_ = view(late, n_, a, w)
            LOADS[7].append((wH[name], "H_" + name))
        H_row, n_ = view(late, n_, D)
        LOADS[7].append((H_row, "H_row"))
        assert n_ <= 24576
        H_col = sb("H_col", [P, 26])
        LOADS[7].append((H_col[:], "H_col"))
        H_up = sb("H_up", [P, FC])
        H_gate = sb("H_gate", [P, FC])
        H_rT, n_ = view(work[:, 0, :], 0, KC, D)
        H_silu, n_ = view(work[:, 0, :], n_, 2, 2 * D)
        H_h, n_ = view(work[:, 0, :], n_, FC, D)
        H_t, n_ = view(work[:, 0, :], n_, G, D)
        H_h2, n_ = view(work[:, 1, :], 0, FC, D)
        H_yT, n_ = view(work[:, 1, :], n_, FC, D)
        H_rot = step_flag("H_rot")
        H_rTs = step_flag("H_rTs")
        H_gates = step_flag("H_gates", CHUNKS)
        H_ups = step_flag("H_ups", CHUNKS)
        H_silus = step_flag("H_silus", CHUNKS)
        H_chunks = step_flag("H_chunks", CHUNKS)
        H_hs = step_flag("H_hs")
        H_turned = step_flag("H_turned", CHUNKS)
        H_yTs = step_flag("H_yTs", CHUNKS)
        H_down = step_flag("H_down")
        H_GATE, H_UP, H_ROT, H_DOWN, H_X = 0, 2, 4, 6, 7
        WEIGHT_USERS.update({(7, 4), (7, 2)})

        def H_before_vector(dve, ch):
            ch.link(nc.vector.tensor_scalar(H_up[:], H_col[:, 10:18], 64.0, None, ALU.mult))
            ch.mark(nc.vector.tensor_tensor(H_up[:], H_up[:], H_col[:, 2:10], ALU.mult))
            ch.mark(nc.vector.tensor_scalar(H_gate[:], H_col[:, 18:26], 64.0, None, ALU.mult))
            nc.vector.tensor_scalar(H_row, H_row, 64.0, None, ALU.mult).then_inc(prepared, 1)

        BEFORE[7, 4] = H_before_vector
        BEFORE[7, 2] = lambda act, ch: act.wait_ge(prepared, PREPARED[7])
        BEFORE[7, 1] = lambda pe, ch: pe.wait_ge(prepared, PREPARED[7])

        def H_vector(dve, ch):
            def body(ch, i, s):
                if s is not None:
                    norm_vector(dve, ch, s)
                if i is not None:
                    h, h2 = H_h, H_h2
                    for n in (4, 2, 1):
                        a = h.rearrange("p (o two s) d -> p o two (s d)", two=2, s=n)
                        b = h2.rearrange("p (o two s) d -> p o two (s d)", two=2, s=n)
                        nc.vector.tensor_tensor(b[:, :, 0, :], a[:, :, 0, :], a[:, :, 1, :], ALU.add)
                        sub = nc.vector.tensor_tensor(b[:, :, 1, :], a[:, :, 0, :], a[:, :, 1, :], ALU.subtract)
                        if n == 1:
                            sub.then_inc(H_hs.sem, 1)
                        else:
                            ch.link(sub)
                        h, h2 = h2, h
                    dve.wait_ge(H_hs.sem, H_hs.at(i))
                if s is not None:
                    for c in range(CHUNKS):
                        dve.wait_ge(H_silus.sem, H_silus.at(s, c))
                        dve.wait_ge(H_ups.sem, H_ups.at(s, c))
                        for n in range(2):
                            f = 2 * c + n
                            last = nc.vector.scalar_tensor_tensor(H_h[:, f, :], PS[:, H_UP + c % 2, n * D:(n + 1) * D], H_up[:, f:f + 1],
                                                                  H_silu[:, c % 2, n * D:(n + 1) * D], ALU.mult, ALU.mult)
                        last.then_inc(H_chunks.sem, 1)
                    dve.wait_ge(H_chunks.sem, H_chunks.at(s, CHUNKS - 1))
                if i is not None:
                    dve.wait_ge(H_down.sem, H_down.at(i))
                    for g in range(G):
                        last = nc.vector.tensor_tensor(H_t[:, g], PS[:, H_DOWN, g * D:(g + 1) * D], H_row, ALU.mult)
                    ch.link(last)
                    for g in range(G):
                        add_to_x(dve, ch, i * G + g, H_t[:, g], gates[:, 1, 3:4])

            D_pipeline(dve, ch, body)

        def H_gpsimd(pool, ch):
            def body(ch, i, s):
                if s is not None:
                    norm_gpsimd(pool, ch, s)

            D_pipeline(pool, ch, body)

        def H_scalar(act, ch):
            def body(ch, i, s):
                def silu(c):
                    act.wait_ge(H_gates.sem, H_gates.at(s, c))
                    for n in range(2):
                        last = nc.scalar.activation(H_silu[:, c % 2, n * D:(n + 1) * D], PS[:, H_GATE + c % 2, n * D:(n + 1) * D], ACT.Silu,
                                                    scale=H_gate[:, 2 * c + n:2 * c + n + 1])
                    last.then_inc(H_silus.sem, 1)

                if s is not None:
                    act.wait_ge(xnT_done.sem, xnT_done.at(s, G - 1))
                    for k in range(KC):
                        last = nc.scalar.activation(xT[:, k].rearrange("p g t -> p (g t)"), PS[:, H_X, k * D:(k + 1) * D], ACT.Copy,
                                                    scale=H_col[:, k:k + 1])
                    last.then_inc(xT_ready.sem, G)
                    act.wait_ge(H_rot.sem, H_rot.at(s))
                    nc.scalar.activation(H_rT.rearrange("p a b -> p (a b)"), PS[:, H_X, :], ACT.Copy, scale=1.0 / (16 * 64)).then_inc(H_rTs.sem, 1)
                    silu(0)
                    silu(1)
                if i is not None:
                    for c in range(CHUNKS):
                        act.wait_ge(H_turned.sem, H_turned.at(i, c))
                        nc.scalar.activation(H_yT[:, 2 * c:2 * c + 2].rearrange("p a b -> p (a b)"), PS[:, H_ROT + c % 2, :], ACT.Copy,
                                             scale=1.0 / (32 * 64)).then_inc(H_yTs.sem, 1)
                if s is not None:
                    for c in (2, 3):
                        act.wait_ge(H_chunks.sem, H_chunks.at(s, c - 2))
                        silu(c)

            D_pipeline(act, ch, body)

        def H_tensor(pe):
            def body(ch, i, s):
                def gate_and_up(c):
                    for bank_, name, done in ((H_GATE, "gate", H_gates), (H_UP, "up", H_ups)):
                        if c >= 2:
                            read = H_silus if name == "gate" else H_chunks
                            pe.wait_ge(read.sem, read.at(s, c - 2))
                        for n in range(2):
                            for k in range(KC):
                                at = (2 * c + n) * P
                                last = nc.tensor.matmul(PS[:, bank_ + c % 2, n * D:(n + 1) * D], wH[name][:, k, at:at + P], H_rT[:, k, :],
                                                        start=k == 0, stop=k == KC - 1)
                        last.then_inc(done.sem, 1)

                if s is not None:
                    for g in range(G):
                        pe.wait_ge(xn_ready.sem, xn_ready.at(s, g))
                        for k in range(KC):
                            at = (k * G + g) * P
                            last = nc.tensor.transpose(PS[:, H_X, at:at + P], xn[:, g, k * P:(k + 1) * P], ident[:])
                        last.then_inc(xnT_done.sem, 1)
                    pe.wait_ge(xT_ready.sem, xT_ready.at(s, G - 1))
                    for m in range(KC):
                        for k in range(KC):
                            last = nc.tensor.matmul(PS[:, H_X, m * D:(m + 1) * D], had256[:, k, m * P:(m + 1) * P],
                                                    xT[:, k].rearrange("p g t -> p (g t)"), start=k == 0, stop=k == KC - 1)
                    last.then_inc(H_rot.sem, 1)
                    pe.wait_ge(H_rTs.sem, H_rTs.at(s))
                    gate_and_up(0)
                    gate_and_up(1)
                if i is not None:
                    pe.wait_ge(H_hs.sem, H_hs.at(i))
                    for c in range(CHUNKS):
                        if c >= 2:
                            pe.wait_ge(H_yTs.sem, H_yTs.at(i, c - 2))
                        nc.tensor.matmul(PS[:, H_ROT + c % 2, :], had128[:], H_h2[:, 2 * c:2 * c + 2, :].rearrange("p a b -> p (a b)"),
                                         start=True, stop=True).then_inc(H_turned.sem, 1)
                if s is not None:
                    gate_and_up(2)
                    gate_and_up(3)
                if i is not None:
                    pe.wait_ge(H_yTs.sem, H_yTs.at(i, CHUNKS - 1))
                    pe.wait_ge(x_done.sem, x_done.nth(i, -1))
                    for f in range(FC):
                        for g in range(G):
                            last = nc.tensor.matmul(PS[:, H_DOWN, g * D:(g + 1) * D], H_yT[:, f, g * P:(g + 1) * P], wH["down"][:, f, :],
                                                    start=f == 0 and g == 0, stop=f == FC - 1 and g == G - 1)
                    last.then_inc(H_down.sem, 1)

            D_pipeline(pe, None, body)

        LOOPS[7] = (None, H_tensor, H_scalar, H_gpsimd, H_vector)
        SUB.append((None, None, None, None, None))
        for n in range(8):
            weights_sent[n] = 16 * len(LOADS[n])
        weights_sent[2] += 16
        weights_sent[3] += 16 * len(LOADS["3 attention"])
        block = ctx.enter_context(nc.Block())

        @block.sync
        def _(sp):
            def const(dst, src):
                sp.dma_start(dst, src).then_inc(const_in, 16)

            sp.dma_start(X[:, 0:G], t["x"][:, 0:G]).then_inc(x_in, 16)
            load_weights(sp, 0)
            ctx_base[0] = 0
            ctx_sync(sp, 0)
            const(X[:, G:], t["x"][:, G:])
            const(gates[:], t["gates"].rearrange("(o a) b -> o a b", o=1).broadcast_to([P, 2, 4]))
            const(had256[:], t["had256"])
            const(had128[:], t["had128"])
            load_weights(sp, 1)
            ctx_sync(sp, 1)
            load_weights(sp, 2)
            for n, (f, *_) in enumerate(SUB[:layers]):
                if n == 2:
                    sp.wait_ge(B_quantised, 1)
                    sp.dma_start(wC["proj"], t["C_proj"]).then_inc(weights_in[2], 16)
                if n in LOAD_AT:
                    for m, prior in LOAD_AT[n]:
                        if (3 if m == "3 attention" else m) < layers:
                            sp.wait_ge(x_done.sem, NB * (prior + 1))
                            load_weights(sp, m)
                if (n, 0) in BEFORE:
                    BEFORE[n, 0](sp)
                if f is None:
                    continue
                with sp.Fori(0 if n else 2, STEPS) as i:
                    f(sp, i)
                ctx_base[0] += STEPS
            sp.wait_ge(x_done.sem, NB * layers)
            sp.dma_start(out, X[:]).then_inc(out_stored, 16)
            sp.wait_ge(out_stored, 16)

        def run(eng, chain_sem, which):
            for f in shared:
                f.base = 0
            ctx_base[0] = 0
            ch = Chain(eng, chain_sem) if chain_sem is not None else None
            for n, fs in enumerate(SUB[:layers]):
                if weights_sent[n] and which == 1 or (n, which) in WEIGHT_USERS:
                    eng.wait_ge(weights_in[n], weights_sent[n])
                if (n, which) in BEFORE:
                    BEFORE[n, which](eng, ch)
                    if ch:
                        ch.restart()
                if (n, 0) in BEFORE:
                    ctx_base[0] += STEPS
                if n in LOOPS:
                    if ch:
                        LOOPS[n][which](eng, ch)
                        ch.restart()
                    else:
                        LOOPS[n][which](eng)
                else:
                    with eng.Fori(0, STEPS) as i:
                        if ch:
                            fs[which](eng, ch, i)
                            ch.restart()
                        else:
                            fs[which](eng, i)
                for f in shared:
                    f.base += NB
                if fs[0] is not None:
                    ctx_base[0] += STEPS

        @block.gpsimd
        def _(pool):
            nc.gpsimd.memset(ident[:], 0.0).then_inc(pool_order, 1)
            nc.gpsimd.memset(minus_half[:], -0.5).then_inc(pool_order, 1)
            nc.gpsimd.memset(eps5[:], 1e-5).then_inc(pool_order, 1)
            nc.gpsimd.memset(ones[:], 1.0).then_inc(pool_order, 1)
            pool.wait_ge(pool_order, 4)
            nc.gpsimd.affine_select(out=ident[:], in_=ident[:], compare_op=ALU.not_equal, fill=1.0, base=0,
                                    pattern=[[-1, P]], channel_multiplier=1).then_inc(pool_order, 1)
            pool.wait_ge(pool_order, 5)
            nc.gpsimd.tensor_copy(ident_b[:], ident[:]).then_inc(ident_ready, 1)
            pool.sem_clear(pool_order)
            run(pool, pool_order, 3)

        @block.scalar
        def _(act):
            run(act, act_order, 2)

        @block.tensor
        def _(pe):
            for g in range(G):
                pe.sem_inc(ctx_read[g], 1)
            pe.wait_ge(ident_ready, 1)
            run(pe, None, 1)

        @block.vector
        def _(dve):
            dve.wait_ge(x_in, 16)
            run(dve, dve_order, 4)


def rows(w):
    k, n = w.shape
    return w.reshape(k // P, P, n).transpose(1, 0, 2)


def hadamard(n):
    import numpy as np
    h = np.ones((1, 1), np.float32)
    while h.shape[0] < n:
        h = np.block([[h, h], [h, -h]])
    return h.astype(np.float32)


def lay_out(i):
    import numpy as np
    a = {k: np.asarray(v) for k, v in i.items()}
    ctxs = a["ctx_2048"]
    r = {
        "x": a["x"].transpose(1, 0, 2),
        "ctxT": ctxs.transpose(2, 0, 1).reshape(KC, P, NB, P).transpose(1, 0, 2, 3),
        "gates": np.stack([a["g_xattn"], a["g_ffn"]]),
        "had256": rows(hadamard(D)),
        "had128": hadamard(P),
    }
    kv = np.concatenate([a["L0_xattn_Wk"], a["L0_xattn_Wv"]])
    r["A_q"] = rows(a["L0_xattn_Wq"].T)
    r["A_kv"] = rows(np.concatenate([kv[0::2], kv[1::2]]).T)
    r["B_gate"] = rows(a["L0_ffn_w_gate"].T)
    r["B_up"] = rows(a["L0_ffn_w_up"].T)
    r["B_down"] = rows(a["L0_ffn_w_down"].T)
    L = "L1_xattn_"
    for n, w in (("q", "wq"), ("qx", "wqx"), ("k", "wk"), ("v", "wv"), ("proj", "wproj")):
        r["C_" + n] = rows(a[L + w].T)
    for n, w in zip(("kx", "vx"), np.split(a[L + "w_kv_x"], 2)):
        r["C_" + n] = rows(w.T)
    col = lambda v: v.reshape(-1, P).T
    r["C_col"] = np.concatenate([col(a[L + n]) for n in (
        "ln_w", "ln_b", "q_in_scale", "qx_in_scale", "k_in_scale", "v_in_scale",
        "qln_w", "qln_b", "kln_w", "kln_b", "qxln_w", "qxln_b", "kxln_w", "kxln_b", "proj_smooth")], axis=1)
    r["C_scalar"] = np.stack([a[L + n].reshape(()) for n in (
        "wq_scale", "wqx_scale", "wk_scale", "wv_scale", "proj_w_scale", "proj_in_scale")]).reshape(1, 6)
    L = "L1_ffn_"
    for n, w in (("q", "Wq"), ("k", "Wk")):
        padded = np.zeros((16, 32, D), a[L + w].dtype)
        padded[:, :16] = a[L + w].reshape(16, 16, D)
        r["D_" + n] = rows(padded.reshape(512, D).T)
    padded = np.zeros((16, 32, D), a[L + "Wo"].dtype)
    padded[:, :16] = a[L + "Wo"].T.reshape(16, 16, D)
    r["D_o"] = rows(padded.reshape(512, D))
    for n, w in (("v", "Wv"), ("in", "W_in_base"), ("up", "W_up_base"), ("down", "W_down")):
        r["D_" + n] = rows(a[L + w].T)
    r["D_a"] = rows(a[L + "A"])
    r["D_b"] = a[L + "B"]
    r["D_col"] = np.concatenate([col(a[L + "ln1_w"]), col(a[L + "ln2_w"])], axis=1)
    r["D_mask"] = np.where(np.tril(np.ones((P, P), bool)), np.float32(0), np.float32(NEG))
    L = "L2_xattn_"
    for n, w in (("q", "Wq"), ("kv", "Wkv"), ("p", "Wp")):
        r["E_" + n] = rows(a[L + w])
    r["E_bias"] = np.concatenate([a[L + "bq"], a[L + "bkv"], a[L + "bp"]]).reshape(1, -1)
    L = "L2_ffn_"
    r["F_gate"] = rows(a[L + "gate_w"])
    r["F_w1"] = rows(a[L + "w1"].transpose(1, 0, 2).reshape(D, 8 * P))
    r["F_w2"] = a[L + "w2"].transpose(1, 0, 2)
    r["F_sw1"] = rows(a[L + "shared_w1"])
    r["F_sw2"] = rows(a[L + "shared_w2"])
    r["F_b2"] = a[L + "b2"]
    r["F_sb2"] = a[L + "shared_b2"].reshape(1, D)
    r["F_col"] = np.concatenate([a[L + "b1"].T, col(a[L + "shared_b1"])], axis=1)
    r["ctx"] = ctxs.transpose(1, 0, 2)
    r["G_mask"] = a["mask_BxS2_bk0"].reshape(1, NB * P)
    L = "L3_ffn_"
    for n, w in (("up", "W_up"), ("gate", "W_gate"), ("down", "W_down")):
        r["H_" + n] = rows(a[L + w].T)
    r["H_col"] = np.concatenate([col(a[L + n]) for n in ("SU_ug", "SU_dp", "Wscale_ug")], axis=1)
    r["H_row"] = a[L + "Wscale_dp"].reshape(1, D)
    for f in LAYOUTS:
        r.update(f(a, np))
    return {k: np.ascontiguousarray(v) for k, v in r.items()}


LAYOUTS = []


def kernel(**inputs):
    import concourse.bacc as bacc
    from concourse.bass_utils import run_bass_kernel_spmd

    nc = bacc.Bacc("TRN2", target_bir_lowering=False, num_devices=1)
    arrays = lay_out(inputs)
    t = {k: nc.dram_tensor(f"in_{k}", v.shape, mybir.dt.from_np(v.dtype), kind="ExternalInput").ap() for k, v in arrays.items()}
    out = nc.dram_tensor("out", (P, NB, D), F32, kind="ExternalOutput").ap()
    program(nc, t, out)
    r = run_bass_kernel_spmd(nc, [{f"in_{k}": v for k, v in arrays.items()}], core_ids=[0])
    return r.results[0]["out"].transpose(1, 0, 2)
```
